# Optimizing a Trainium2 kernel written in Bass

```python
import numpy as np
import jax
import jax.numpy as jnp

def _softmax(x, axis=-1):
    return jax.nn.softmax(x, axis=axis)

def _gelu(x):
    return jax.nn.gelu(x, approximate=True)

def _silu(x):
    return jax.nn.silu(x)

def _sigmoid(x):
    return jax.nn.sigmoid(x)

def _layernorm(x, axis=-1, eps=1e-05):
    m = jnp.mean(x, axis=axis, keepdims=True)
    v = jnp.var(x, axis=axis, keepdims=True)
    return (x - m) / jnp.sqrt(v + eps)

def _scatter_add(tgt, idx, src, axis=0):
    return tgt.at[idx].add(src)

def _segment_sum(src, seg, n):
    return jax.ops.segment_sum(src, seg, n)
kernel_name = 'mk_seq_preln_d1_jaxref_r4_a5176c'

def setup_inputs(seed: int=0):
    np.random.seed(seed)
    _w = jnp.asarray

    def _L0_attn_setup():
        import jax, jax.numpy as jnp
        import numpy as np
        B, CTX, DIMS, HEAD = (8, 1024, 256, 16)
        HD = DIMS // HEAD
        EPS = 1e-05
        THRESH = 0.01
        FACTOR = 0.1
        MAX_IT = 3

        def _ln(x, w):
            m = jnp.mean(x, axis=-1, keepdims=True)
            v = jnp.mean((x - m) ** 2, axis=-1, keepdims=True)
            return (x - m) * jax.lax.rsqrt(v + EPS) * w
        key = jax.random.key(seed)
        ks = jax.random.split(key, 9)
        w = lambda k, shp: jax.random.normal(k, shp, jnp.float32) * 0.02
        return {'x': jax.random.normal(ks[0], (B, CTX, DIMS), jnp.float32), 'qw': w(ks[1], (DIMS, DIMS)), 'qb': jnp.zeros((DIMS,), jnp.float32), 'kw': w(ks[2], (DIMS, DIMS)), 'vw': w(ks[3], (DIMS, DIMS)), 'vb': jnp.zeros((DIMS,), jnp.float32), 'ow': w(ks[4], (DIMS, DIMS)), 'ob': jnp.zeros((DIMS,), jnp.float32), 'lna_w': jnp.ones((DIMS,), jnp.float32), 'lnb_w': jnp.ones((DIMS,), jnp.float32), 'lnc_w': jnp.ones((HD,), jnp.float32), 'lnd_w': jnp.ones((HD,), jnp.float32), 'lqw': w(ks[5], (HD, HD)), 'lqb': jnp.zeros((HD,), jnp.float32), 'lkw': w(ks[6], (HD, HD)), 'lkb': jnp.zeros((HD,), jnp.float32), 'lvw': w(ks[7], (HD, HD)), 'lvb': jnp.zeros((HD,), jnp.float32)}
    _L0_attn_in = _L0_attn_setup()

    def _L0_ffn_setup():
        import jax, jax.numpy as jnp
        import numpy as np
        from jax import lax
        B, S, H = (2, 256, 256)
        I = 128
        E = 32
        TOP_K = 4
        N_GROUP = 4
        TOPK_GROUP = 2
        SCALE = 2.5
        N_SHARED = 2
        SH_I = I * N_SHARED

        def _route(tokens, router_weight, router_bias):
            logits = tokens.astype(jnp.float32) @ router_weight.astype(jnp.float32).T
            scores = jax.nn.sigmoid(logits)
            sfc = scores + router_bias[None, :]
            T = tokens.shape[0]
            grp = sfc.reshape(T, N_GROUP, E // N_GROUP)
            group_scores = lax.top_k(grp, 2)[0].sum(-1)
            _, gidx = lax.top_k(group_scores, TOPK_GROUP)
            gmask = jax.nn.one_hot(gidx, N_GROUP, dtype=sfc.dtype).sum(1)
            smask = jnp.broadcast_to(gmask[:, :, None], (T, N_GROUP, E // N_GROUP)).reshape(T, E)
            tmp = jnp.where(smask > 0, sfc, 0.0)
            _, topk_idx = lax.top_k(tmp, TOP_K)
            topk_w = jnp.take_along_axis(scores, topk_idx, axis=1)
            topk_w = topk_w / (topk_w.sum(-1, keepdims=True) + 1e-20)
            topk_w = topk_w * SCALE
            return (topk_idx, topk_w)
        key = jax.random.key(seed)
        ks = jax.random.split(key, 10)
        std = 0.02
        return {'hidden_states': jax.random.normal(ks[0], (B, S, H), jnp.float32), 'router_weight': jax.random.normal(ks[1], (E, H), jnp.float32) * std, 'router_bias': jnp.zeros((E,), jnp.float32), 'gate_w': jax.random.normal(ks[2], (E, I, H), jnp.float32) * std, 'up_w': jax.random.normal(ks[3], (E, I, H), jnp.float32) * std, 'down_w': jax.random.normal(ks[4], (E, H, I), jnp.float32) * std, 'shared_gate_w': jax.random.normal(ks[5], (SH_I, H), jnp.float32) * std, 'shared_up_w': jax.random.normal(ks[6], (SH_I, H), jnp.float32) * std, 'shared_down_w': jax.random.normal(ks[7], (H, SH_I), jnp.float32) * std}
    _L0_ffn_in = _L0_ffn_setup()
    _d = {'L0_attn_x': _L0_attn_in['x'], 'L0_attn_qw': _L0_attn_in['qw'], 'L0_attn_qb': _L0_attn_in['qb'], 'L0_attn_kw': _L0_attn_in['kw'], 'L0_attn_vw': _L0_attn_in['vw'], 'L0_attn_vb': _L0_attn_in['vb'], 'L0_attn_ow': _L0_attn_in['ow'], 'L0_attn_ob': _L0_attn_in['ob'], 'L0_attn_lna_w': _L0_attn_in['lna_w'], 'L0_attn_lnb_w': _L0_attn_in['lnb_w'], 'L0_attn_lnc_w': _L0_attn_in['lnc_w'], 'L0_attn_lnd_w': _L0_attn_in['lnd_w'], 'L0_attn_lqw': _L0_attn_in['lqw'], 'L0_attn_lqb': _L0_attn_in['lqb'], 'L0_attn_lkw': _L0_attn_in['lkw'], 'L0_attn_lkb': _L0_attn_in['lkb'], 'L0_attn_lvw': _L0_attn_in['lvw'], 'L0_attn_lvb': _L0_attn_in['lvb'], 'L0_ffn_router_weight': _L0_ffn_in['router_weight'], 'L0_ffn_router_bias': _L0_ffn_in['router_bias'], 'L0_ffn_gate_w': _L0_ffn_in['gate_w'], 'L0_ffn_up_w': _L0_ffn_in['up_w'], 'L0_ffn_down_w': _L0_ffn_in['down_w'], 'L0_ffn_shared_gate_w': _L0_ffn_in['shared_gate_w'], 'L0_ffn_shared_up_w': _L0_ffn_in['shared_up_w'], 'L0_ffn_shared_down_w': _L0_ffn_in['shared_down_w']}
    _x0 = _d['L0_attn_x']
    _d['L0_attn_x'] = jax.random.normal(jax.random.fold_in(jax.random.key(seed), 1), (8, 512, 256), dtype=_x0.dtype)
    del _x0
    return _d

def reference(L0_attn_x, L0_attn_qw, L0_attn_qb, L0_attn_kw, L0_attn_vw, L0_attn_vb, L0_attn_ow, L0_attn_ob, L0_attn_lna_w, L0_attn_lnb_w, L0_attn_lnc_w, L0_attn_lnd_w, L0_attn_lqw, L0_attn_lqb, L0_attn_lkw, L0_attn_lkb, L0_attn_lvw, L0_attn_lvb, L0_ffn_router_weight, L0_ffn_router_bias, L0_ffn_gate_w, L0_ffn_up_w, L0_ffn_down_w, L0_ffn_shared_gate_w, L0_ffn_shared_up_w, L0_ffn_shared_down_w):

    def _L0_attn_ref(x, qw, qb, kw, vw, vb, ow, ob, lna_w, lnb_w, lnc_w, lnd_w, lqw, lqb, lkw, lkb, lvw, lvb):
        import jax, jax.numpy as jnp
        import numpy as np
        B, CTX, DIMS, HEAD = (8, 1024, 256, 16)
        HD = DIMS // HEAD
        EPS = 1e-05
        THRESH = 0.01
        FACTOR = 0.1
        MAX_IT = 3

        def _ln(x, w):
            m = jnp.mean(x, axis=-1, keepdims=True)
            v = jnp.mean((x - m) ** 2, axis=-1, keepdims=True)
            return (x - m) * jax.lax.rsqrt(v + EPS) * w
        b, ctx, dims = x.shape
        q = _ln(x, lna_w) @ qw.T + qb
        xb = _ln(x, lnb_w)
        k = xb @ kw.T
        v = xb @ vw.T + vb
        split = lambda t: t.reshape(b, ctx, HEAD, HD).transpose(0, 2, 1, 3)
        query, key_t, value = (split(q), split(k), split(v))
        eff = min(ctx, HEAD)
        kn = _ln(key_t[:, :, :eff, :] @ lkw.T + lkb, lnd_w)
        vi = value[:, :, :eff, :] @ lvw.T + lvb
        scale = 1.0 / np.sqrt(HD)

        def step(qcur):
            qn = _ln(qcur[:, :, :eff, :] @ lqw.T + lqb, lnc_w)
            logits = jnp.einsum('bhqd,bhkd->bhqk', qn, kn) * scale
            attn = jax.nn.softmax(logits, axis=-1) @ vi
            return jnp.zeros_like(qcur).at[:, :, :eff, :].set(attn)
        prev = jnp.zeros_like(query)
        attn_out = jnp.zeros_like(query)
        qcur = query
        done = jnp.asarray(False)
        for it in range(MAX_IT):
            iter_out = step(qcur)
            diff = jnp.mean(jnp.abs(iter_out - prev))
            brk = (diff < THRESH + FACTOR * diff) & jnp.asarray(it > 0) & ~done
            attn_out = jnp.where(done, attn_out, iter_out)
            prev = jnp.where(done, prev, iter_out)
            qcur = jnp.where(done | brk, qcur, qcur + iter_out)
            done = done | brk
        out = attn_out.transpose(0, 2, 1, 3).reshape(b, ctx, dims)
        return out @ ow.T + ob

    def _L0_ffn_ref(hidden_states, router_weight, router_bias, gate_w, up_w, down_w, shared_gate_w, shared_up_w, shared_down_w):
        import jax, jax.numpy as jnp
        import numpy as np
        from jax import lax
        B, S, H = (2, 256, 256)
        I = 128
        E = 32
        TOP_K = 4
        N_GROUP = 4
        TOPK_GROUP = 2
        SCALE = 2.5
        N_SHARED = 2
        SH_I = I * N_SHARED

        def _route(tokens, router_weight, router_bias):
            logits = tokens.astype(jnp.float32) @ router_weight.astype(jnp.float32).T
            scores = jax.nn.sigmoid(logits)
            sfc = scores + router_bias[None, :]
            T = tokens.shape[0]
            grp = sfc.reshape(T, N_GROUP, E // N_GROUP)
            group_scores = lax.top_k(grp, 2)[0].sum(-1)
            _, gidx = lax.top_k(group_scores, TOPK_GROUP)
            gmask = jax.nn.one_hot(gidx, N_GROUP, dtype=sfc.dtype).sum(1)
            smask = jnp.broadcast_to(gmask[:, :, None], (T, N_GROUP, E // N_GROUP)).reshape(T, E)
            tmp = jnp.where(smask > 0, sfc, 0.0)
            _, topk_idx = lax.top_k(tmp, TOP_K)
            topk_w = jnp.take_along_axis(scores, topk_idx, axis=1)
            topk_w = topk_w / (topk_w.sum(-1, keepdims=True) + 1e-20)
            topk_w = topk_w * SCALE
            return (topk_idx, topk_w)
        tokens = hidden_states.reshape(-1, H)
        topk_idx, topk_w = _route(tokens, router_weight, router_bias)
        gate_vals = jax.nn.silu(jnp.einsum('th,eih->tei', tokens, gate_w))
        up_vals = jnp.einsum('th,eih->tei', tokens, up_w)
        hidden_vals = gate_vals * up_vals
        expert_out = jnp.einsum('tei,ehi->teh', hidden_vals, down_w)
        sel = jnp.take_along_axis(expert_out, topk_idx[:, :, None], axis=1)
        mixed = (sel * topk_w[:, :, None].astype(sel.dtype)).sum(1)
        mixed = mixed.reshape(hidden_states.shape)
        sg = jax.nn.silu(jnp.einsum('bsh,ih->bsi', hidden_states, shared_gate_w))
        su = jnp.einsum('bsh,ih->bsi', hidden_states, shared_up_w)
        shared = jnp.einsum('bsi,hi->bsh', sg * su, shared_down_w)
        return mixed + shared
    x = L0_attn_x
    x = x + _L0_attn_ref(_layernorm(x, axis=-1), L0_attn_qw, L0_attn_qb, L0_attn_kw, L0_attn_vw, L0_attn_vb, L0_attn_ow, L0_attn_ob, L0_attn_lna_w, L0_attn_lnb_w, L0_attn_lnc_w, L0_attn_lnd_w, L0_attn_lqw, L0_attn_lqb, L0_attn_lkw, L0_attn_lkb, L0_attn_lvw, L0_attn_lvb)
    x = x + _L0_ffn_ref(_layernorm(x, axis=-1), L0_ffn_router_weight, L0_ffn_router_bias, L0_ffn_gate_w, L0_ffn_up_w, L0_ffn_down_w, L0_ffn_shared_gate_w, L0_ffn_shared_up_w, L0_ffn_shared_down_w)
    return x

_drawn_inputs = setup_inputs


def setup_inputs(seed=0):
    import zlib

    import numpy as np

    out = dict(_drawn_inputs(seed))
    spreads = {'L0_attn_qb': (0.0, 0.8),
     'L0_attn_vb': (0.0, 0.8),
     'L0_attn_ob': (0.0, 0.1),
     'L0_attn_lna_w': (1.0, 0.6),
     'L0_attn_lnb_w': (1.0, 0.6),
     'L0_attn_lnc_w': (1.0, 0.6),
     'L0_attn_lnd_w': (1.0, 0.6),
     'L0_attn_lqb': (0.0, 0.8),
     'L0_attn_lkb': (0.0, 0.8),
     'L0_attn_lvb': (0.0, 0.8),
     'L0_ffn_router_bias': (0.0, 0.509)}
    factors = {'L0_attn_qw': 8.0,
     'L0_attn_kw': 8.0,
     'L0_attn_vw': 8.0,
     'L0_attn_ow': 8.0,
     'L0_attn_lqw': 8.0,
     'L0_attn_lkw': 8.0,
     'L0_attn_lvw': 8.0,
     'L0_ffn_router_weight': 4.558,
     'L0_ffn_gate_w': 3.823,
     'L0_ffn_up_w': 3.774,
     'L0_ffn_down_w': 3.775,
     'L0_ffn_shared_gate_w': 3.385,
     'L0_ffn_shared_up_w': 3.339,
     'L0_ffn_shared_down_w': 3.337}
    for name, (base, spread) in spreads.items():
        noise = np.random.default_rng([zlib.crc32(name.encode()), seed]).standard_normal(out[name].shape)
        drawn = base * np.exp(spread * noise) if base else spread * noise
        out[name] = jnp.asarray(drawn.astype(out[name].dtype))
    for name, factor in factors.items():
        out[name] = (out[name] * factor).astype(out[name].dtype)
    return out
```

```python
from contextlib import ExitStack

import numpy as np

import concourse.bass as bass
from concourse import mybir

F32 = mybir.dt.float32
BF16 = mybir.dt.bfloat16
I32 = mybir.dt.int32
U16 = mybir.dt.uint16
U32 = mybir.dt.uint32
ALU = mybir.AluOpType
ACT = mybir.ActivationFunctionType
AX = mybir.AxisListType

P = 128
BATCH, CTX, D = 8, 512, 256
HEADS, HD = 16, 16
ROWS = 16
TOKENS = BATCH * CTX
TT = TOKENS // P
REST = (CTX - ROWS) // ROWS
E, I, TOPK = 32, 128, 4
GROUPS, GSIZE, TOPG = 4, 8, 2
PAIRS = TOKENS * TOPK
KC = D // P
EPS = 1e-5
MASKED = -1e30
ITERATIONS = 3
DIFF_LIMIT, DIFF_FACTOR = 0.01, 0.1
ROUTE_SCALE = 2.5
SLOT_TILES = 160
assert (PAIRS + E * (P - 1)) // P <= SLOT_TILES
GROUPS_OF_TILES = [(1, 9), (9, 17), (17, 25), (25, 32)]
CODE = 0x800
HOTS = 8
N_CONSTS = 27

STEPS = 14
EXPERTS_AT = [0, 1, 2, 3, 4, 7, 8, 9, 10, 11]
SHARED_AT = [5, 12]
FED_AT = sorted(EXPERTS_AT + SHARED_AT)
DONE_AT = sorted(EXPERTS_AT + [s + 1 for s in SHARED_AT])
NEXP, NFED = len(EXPERTS_AT), len(FED_AT)
BODIES = SLOT_TILES // NEXP
RING = 5
LAG = 2
EIDS = 12
assert BODIES * len(SHARED_AT) == TT and NEXP % RING == 0

ATT_STEPS = 4 + 6 * ITERATIONS - 1 + 3
LOGIT_STEPS = [4 + 6 * it + 2 for it in range(ITERATIONS)]
TILES_AT = [TT // ATT_STEPS + (step < (TT - 1) % ATT_STEPS) for step in range(ATT_STEPS)]
assert sum(TILES_AT) == TT - 1

ROW_PARTS = [("lna", D), ("lnb", D), ("ob", D), ("lqb", HD), ("lkb", HD), ("lvb", HD), ("lnc", HD),
             ("lnd", HD), ("bias", E)]
ROW_AT = {}
for _name, _n in ROW_PARTS:
    ROW_AT[_name] = (sum(n for _, n in ROW_PARTS[:len(ROW_AT)]), _n)
ROW_LEN = sum(n for _, n in ROW_PARTS)


def counted(table, step):
    body, s = divmod(step, STEPS)
    return body * len(table) + sum(x < s for x in table)


def wait_count(eng, sem, body, per_body, offset):
    if isinstance(body, int):
        if body * per_body + offset > 0:
            eng.wait_ge(sem, body * per_body + offset)
    else:
        assert per_body + offset > 0
        eng.wait_ge(sem, body * per_body + offset)


def build_program(nc, x, qkvo, gate_up, down, sh_gate_up, sh_down, router, rows, cols, local, out,
                  tokens_dram, pairs_dram):
    ctx = ExitStack()
    with ctx:
        def sb(name, shape, dt=F32):
            return ctx.enter_context(nc.sbuf_tensor(name, shape, dt))

        def sem(name):
            return ctx.enter_context(nc.semaphore(name))

        bank = [ctx.enter_context(nc.psum_tensor(f"bank{i}", [P, 512], F32)) for i in range(8)]
        gu_w = sb("gu_w", [P, E, KC, 2 * I])
        dn_w = sb("dn_w", [P, E, D])
        sgu_w = sb("sgu_w", [P, 2, KC, 2 * I])
        sdn_w = sb("sdn_w", [P, 2, D])
        x_sb = sb("x_sb", [P, TT, D])
        xn = sb("xn", [P, 4, D])
        row_sb = sb("row_sb", [P, ROW_LEN])
        col_sb = sb("col_sb", [P, 4])
        rt_w = sb("rt_w", [P, KC, E])
        ident = sb("ident", [P, P])
        stats = sb("stats", [P, TT, 6])
        mv = sb("mv", [P, TT, 2])
        var_e = sb("var_e", [P, TT])
        rstd = sb("rstd", [P, TT])
        half = sb("half", [P, TT])
        shift = sb("shift", [P, TT])
        xnT = sb("xnT", [P, 2, KC, P])
        wts = sb("wts", [P, TT, TOPK])
        pair_at = sb("pair_at", [P, SLOT_TILES], I32)
        tok_at = sb("tok_at", [P, SLOT_TILES + RING], I32)
        eids = sb("eids", [1, BODIES, EIDS], I32)

        def row(name):
            a, n = ROW_AT[name]
            return row_sb[:, a:a + n]

        scratch = sb("scratch", [P, 4 * TOPK * D])
        def piece(k, n=1):
            return scratch[:, k * TT * E:(k + n) * TT * E]
        sc3 = piece(0).rearrange("p (t e) -> p t e", e=E)
        sel = piece(1)
        hot_b = piece(2, 2).bitcast(BF16).rearrange("p (k t e) -> p k t e", k=TOPK, e=E)
        load4 = scratch[:, :].rearrange("p (s k d) -> p s k d", s=4, k=TOPK)
        work = sb("work", [P, 3, TT * E])
        small = sb("small", [P, 7, TT * GROUPS])
        idxf = sb("idxf", [P, TT, TOPK])
        e_row = sb("e_row", [P, 8, E])
        code_u = sb("code_u", [P, TT * TOPK], U16)
        lower = sb("lower", [P, P], BF16)
        ones_b = sb("ones_b", [P, P], BF16)
        iota_b = sb("iota_b", [P, SLOT_TILES, HOTS], BF16)
        iota_e = sb("iota_e", [P, E])
        iota_g = sb("iota_g", [P, GROUPS])
        iota_p = sb("iota_p", [P, 2])
        ecol = sb("ecol", [P, 4])

        loopb = sb("loopb", [P, 22 * D])
        def lb(k, n=1):
            return loopb[:, k * D:(k + n) * D]
        xg = lb(0, RING).rearrange("p (r d) -> p r d", d=D)
        yb = lb(5, RING).rearrange("p (r d) -> p r d", d=D)
        xs = lb(10, 2).rearrange("p (r d) -> p r d", d=D)
        xT = lb(12, 2).rearrange("p (r c t) -> p r c t", r=2, c=KC)
        silu = lb(14).rearrange("p (r i) -> p r i", r=2)
        hid = lb(15).rearrange("p (r i) -> p r i", r=2)
        hidT = lb(16).rearrange("p (r i) -> p r i", r=2)
        hotr = lb(0, 4).bitcast(BF16).rearrange("p (b r h) -> p b r h", b=2, h=HOTS)
        hotj = lb(11, 5).bitcast(BF16).rearrange("p (b j h) -> p b j h", b=2, h=HOTS)
        top8 = lb(5).rearrange("p (t j) -> p t j", j=8)
        idx8 = lb(6).bitcast(U32).rearrange("p (t j) -> p t j", j=8)
        slots = lb(7, 4)
        slot_f = slots[:, 0:TT * TOPK].rearrange("p (t k) -> p t k", k=TOPK)
        slot_i = slots[:, P:4 * P].bitcast(I32).rearrange("p (m n) -> p m n", m=3)
        slot_b = slots[:, 4 * P:5 * P].bitcast(BF16).rearrange("p (m n) -> p m n", m=2)
        stage_g = sb("stage_g", [P, NEXP], I32)
        stage_s = sb("stage_s", [P, NEXP], I32)

        w4 = scratch[:, 0:8 * D].rearrange("p (m c n) -> p m c n", m=4, c=KC)
        head_mask = sb("head_mask", [P, HEADS // 2])
        quad_mask = sb("quad_mask", [P, 4])
        batch_mask = sb("batch_mask", [P, 2, ROWS])
        spread = small[:, 0:4, :].rearrange("p g (a t) -> p g a t", a=4)
        local_sb = sb("local_sb", [P, 3, HD])
        blockw = lb(0, 3).rearrange("p (m h d) -> p m h d", m=6, d=HD)[:, 0:3]
        at_a, at_b, at_c = lb(3), lb(4), lb(5)
        at_d = lb(6)
        inT = lb(7, 2).rearrange("p (m c t) -> p m c t", m=2, c=KC)
        q_cur = lb(9).rearrange("p (c t) -> p c t", c=KC)
        at_T = lb(10).rearrange("p (c t) -> p c t", c=KC)
        att_out = lb(11, 3).rearrange("p (i n) -> p i n", i=3)
        prob = lb(14, 2)
        probT = lb(16, 2).rearrange("p (j t) -> p j t", j=4)
        keys = work[:, 0:2, :].rearrange("p c (h t) -> p c h t", t=P)
        vals = lb(18, 4).rearrange("p (g n) -> p g n", g=4)
        hst = sb("hst", [P, 6, HEADS])
        dsum = sb("dsum", [P, 4])
        stop_i = sb("stop_i", [P, 1], I32)
        ones_f = lb(0, 3)[:, 4 * P:5 * P]

        att_x_in = sem("att_x_in")
        x_in = [sem(f"x_in{g}") for g in range(len(GROUPS_OF_TILES))]
        small_in = sem("small_in")
        attw_in = sem("attw_in")
        expert_w_in = sem("expert_w_in")
        consts_made = sem("consts_made")
        var_ready = sem("var_ready")
        rstd_ready = sem("rstd_ready")
        norm_ready = sem("norm_ready")
        xn_ready = sem("xn_ready")
        xn_turned = sem("xn_turned")
        xnT_ready = sem("xnT_ready")
        logits_done = sem("logits_done")
        tok_stored = [sem(f"tok_stored{s}") for s in range(4)]
        att_dve = sem("att_dve")
        att_pe = sem("att_pe")
        att_exp = sem("att_exp")
        dve_seq = sem("dve_seq")
        pool_seq = sem("pool_seq")
        scores_done = sem("scores_done")
        hot_ready = sem("hot_ready")
        counts_done = sem("counts_done")
        pairs_hot = sem("pairs_hot")
        pairs_used = sem("pairs_used")
        rows_hot = sem("rows_hot")
        codes_done = sem("codes_done")
        ecol_ready = sem("ecol_ready")
        eid_turned = sem("eid_turned")
        tables_ready = sem("tables_ready")
        gathered = [sem(f"gathered{k}") for k in range(RING)]
        scattered = [sem(f"scattered{k}") for k in range(RING)]
        shared_in = [sem(f"shared_in{k}") for k in range(2)]
        staged = sem("staged")
        x_turned = sem("x_turned")
        xT_ready = sem("xT_ready")
        gu_done = sem("gu_done")
        silu_done = sem("silu_done")
        hid_ready = sem("hid_ready")
        hid_turned = sem("hid_turned")
        hidT_ready = sem("hidT_ready")
        y_done = sem("y_done")
        y_ready = sem("y_ready")
        pairs_in = [sem(f"pairs_in{s}") for s in range(4)]
        added = sem("added")
        tile_summed = sem("tile_summed")
        stored = sem("stored")

        turn_ps = [bank[0][:, 0:D].rearrange("p (c t) -> p c t", c=KC),
                   bank[1][:, 0:D].rearrange("p (c t) -> p c t", c=KC)]
        logit_ps = [bank[2], bank[3]]
        att_ps = bank[4:8]

        x_rest = x[:, ROWS:CTX, :].rearrange("b (q j) d -> b q (j d)", j=REST)
        out_rest = out[:, ROWS:CTX, :].rearrange("b (q j) d -> b q (j d)", j=REST)
        tok_tiles = tokens_dram.rearrange("(p t) d -> p t d", t=TT)
        pair_tiles = pairs_dram.rearrange("(p t k) d -> p t (k d)", t=TT, k=TOPK)
        tile_order = list(range(1, TT)) + [0]

        block = ctx.enter_context(nc.Block())

        @block.sync
        def _(sp):
            sp.dma_start(x_sb[:, 0, :], x[:, 0:ROWS, :]).then_inc(att_x_in, 16)
            sp.dma_start(row_sb[:, :], rows.to_broadcast([P, ROW_LEN])).then_inc(small_in, 16)
            sp.dma_start(rt_w[:, :, :], router).then_inc(small_in, 16)
            for g, (a, b) in enumerate(GROUPS_OF_TILES):
                sp.dma_start(x_sb[:, a:b, :].rearrange("p j d -> p (j d)"),
                             x_rest[:, :, (a - 1) * D:(b - 1) * D]).then_inc(x_in[g], 16)
            for n, t in enumerate(tile_order):
                if n == TT - 1:
                    for m in range(4):
                        e = slice(8 * m, 8 * m + 8)
                        sp.dma_start(gu_w[:, e], gate_up[:, e]).then_inc(expert_w_in, 16)
                        sp.dma_start(dn_w[:, e], down[:, e]).then_inc(expert_w_in, 16)
                    sp.dma_start(sgu_w[:, :, :, :], sh_gate_up).then_inc(expert_w_in, 16)
                    sp.dma_start(sdn_w[:, :, :], sh_down).then_inc(expert_w_in, 16)
                sp.wait_ge(xn_ready, n + 1)
                sp.dma_start(tok_tiles[:, t, :], xn[:, n % 4, :]).then_inc(tok_stored[n % 4], 16)
            for s in range(4):
                sp.wait_ge(tok_stored[s], 16 * (TT // 4))
            sp.wait_ge(tables_ready, 1)
            for w in range(2):
                sp.dma_start(xs[:, w, :], tok_tiles[:, w, :]).then_inc(shared_in[w], 16)
            with sp.Fori(1, BODIES) as body:
                for w in range(2):
                    sp.wait_ge(x_turned, (body - 1) * NFED + counted(FED_AT, SHARED_AT[w]) + 1)
                    sp.dma_start(xs[:, w, :], tok_tiles[:, bass.ds(body * 2 + w, 1), :].rearrange("p a d -> p (a d)")
                                 ).then_inc(shared_in[w], 16)
            for k in range(RING):
                sp.wait_ge(scattered[k], 16 * (SLOT_TILES // RING))
            for t in range(TT):
                if t >= 4:
                    sp.wait_ge(tile_summed, t - 3)
                sp.dma_start(load4[:, t % 4].rearrange("p k d -> p (k d)"), pair_tiles[:, t, :]
                             ).then_inc(pairs_in[t % 4], 16)

        @block.gpsimd
        def _(pool):
            made = [0]

            def const(ins):
                made[0] += 1
                ins.then_inc(consts_made, 1)
                pool.wait_ge(consts_made, made[0])

            const(pool.memset(half[:, :], -0.5))
            const(pool.memset(ident[:, :], 0.0))
            const(pool.affine_select(ident[:, :], ident[:, :], [[-1, P]], ALU.not_equal, 1.0, base=0,
                                     channel_multiplier=1))
            rstds = [0]

            def inverse_root(out_ap, in_ap, exponent):
                rstds[0] += 1
                pool.wait_ge(var_ready, rstds[0])
                pool.tensor_tensor(out_ap, in_ap, exponent, ALU.pow).then_inc(rstd_ready, 1)

            for _ in range(2):
                inverse_root(rstd[:, 0:1], var_e[:, 0:1], half[:, 0:1])
            const(pool.memset(ones_f[:, :], 1.0))
            const(pool.memset(ones_b[:, :], 1.0))
            for mask, n, width in ((head_mask, HEADS // 2, HD), (quad_mask, 4, 32)):
                const(pool.memset(mask[:, :], 1.0))
                const(pool.affine_select(mask[:, :], mask[:, :], [[-width, n]], ALU.is_ge, 0.0, base=0,
                                         channel_multiplier=1))
                const(pool.affine_select(mask[:, :], mask[:, :], [[width, n]], ALU.is_ge, 0.0, base=width - 1,
                                         channel_multiplier=-1))
            const(pool.memset(batch_mask[:, :, :], 0.0))
            for g in range(4):
                q = batch_mask[32 * g:32 * g + 32]
                const(pool.affine_select(q[:, 0, :], q[:, 0, :], [[0, ROWS]], ALU.is_ge, MASKED, base=ROWS - 1,
                                         channel_multiplier=-1))
                const(pool.affine_select(q[:, 1, :], q[:, 1, :], [[0, ROWS]], ALU.is_ge, MASKED, base=-ROWS,
                                         channel_multiplier=1))
            const(pool.iota(iota_b[:, :, :], [[1, SLOT_TILES], [0, HOTS]], base=0, channel_multiplier=0,
                            allow_small_or_imprecise_dtypes=True))
            const(pool.iota(iota_e[:, :], [[1, E]], base=0, channel_multiplier=0,
                            allow_small_or_imprecise_dtypes=True))
            const(pool.iota(iota_g[:, :], [[1, GROUPS]], base=0, channel_multiplier=0,
                            allow_small_or_imprecise_dtypes=True))
            const(pool.iota(iota_p[:, :], [[P, 2]], base=0, channel_multiplier=1,
                            allow_small_or_imprecise_dtypes=True))
            const(pool.iota(code_u[:, :], [[1, TT * TOPK]], base=CODE, channel_multiplier=TT * TOPK,
                            allow_small_or_imprecise_dtypes=True))
            const(pool.affine_select(lower[:, :], ones_b[:, :], [[1, P]], ALU.is_gt, 0.0, base=0,
                                     channel_multiplier=-1))
            const(pool.memset(tok_at[:, SLOT_TILES:], 0))
            assert made[0] == N_CONSTS
            for a, b in GROUPS_OF_TILES:
                inverse_root(rstd[:, a:b], var_e[:, a:b], half[:, a:b])
            for _ in range(1 + ITERATIONS):
                inverse_root(hst[:, 3, :], hst[:, 2, :], half[:, 0:HEADS])
            inverse_root(rstd[:, 0:1], var_e[:, 0:1], half[:, 0:1])

            for s in range(4):
                pool.wait_ge(tok_stored[s], 16 * (TT // 4))
            pool.wait_ge(tables_ready, 1)

            def gather(k, index):
                pool.indirect_dma_start(out=xg[:, k, :], out_offset=None, in_=tokens_dram,
                                        in_offset=bass.IndirectOffsetOnAxis(ap=index, axis=0)
                                        ).then_inc(gathered[k], 16)

            for k in range(RING):
                gather(k, tok_at[:, k:k + 1])

            def wait_before_dma(sem_, body, per_body, offset):
                wait_count(pool, sem_, body, per_body, offset)
                if not isinstance(body, int):
                    pool.sem_inc(pool_seq, 1)

            def stage(body, h):
                for k in range(RING):
                    wait_count(pool, gathered[k], body, 16 * 2, 16 * h if not isinstance(body, int) or body else 0)
                    wait_count(pool, scattered[k], body, 16 * 2, 16 * (h - 1))
                if not isinstance(body, int):
                    pool.sem_inc(pool_seq, 1)
                at, first = h * RING, body * NEXP + h * RING
                pool.tensor_copy(stage_g[:, at:at + RING], tok_at[:, bass.ds(first + RING, RING)]).then_inc(staged, 1)
                pool.tensor_copy(stage_s[:, at:at + RING], pair_at[:, bass.ds(first, RING)]).then_inc(staged, 1)

            def scatter(body, u):
                back, column = divmod(u, NEXP)
                wait_before_dma(y_ready, body, NFED, counted(DONE_AT, back * STEPS + EXPERTS_AT[column]) + 1)
                pool.indirect_dma_start(out=pairs_dram,
                                        out_offset=bass.IndirectOffsetOnAxis(ap=stage_s[:, column:column + 1], axis=0),
                                        in_=yb[:, column % RING, :], in_offset=None, bounds_check=PAIRS - 1,
                                        oob_is_err=False).then_inc(scattered[column % RING], 16)

            def body_of(body, first, last):
                for u, step in enumerate(EXPERTS_AT):
                    k = u % RING
                    if u == 2 and not (isinstance(body, int) and body == 0):
                        stage(body, 1)
                    if u == 7 and not last:
                        stage(body + 1, 0)
                    if k == 0:
                        wait_before_dma(staged, body, 4, 2 + 2 * (u // RING))
                    if not (last and u >= NEXP - RING):
                        wait_before_dma(x_turned, body, NFED, counted(FED_AT, step) + 1)
                        gather(k, stage_g[:, u:u + 1])
                    if not (first and u < LAG):
                        scatter(body, u - LAG)

            stage(0, 0)
            stage(0, 1)
            body_of(0, True, False)
            with pool.Fori(1, BODIES - 1) as body:
                body_of(body, False, False)
            body_of(BODIES - 1, False, True)
            for u in range(NEXP - LAG, NEXP):
                scatter(BODIES - 1, u)

        @block.scalar
        def _(act):
            act.dma_start(w4[:, :, :, :], qkvo).then_inc(attw_in, 16)
            act.dma_start(col_sb[:, :], cols).then_inc(attw_in, 16)
            act.dma_start(local_sb[:, :, :], local).then_inc(attw_in, 16)

            def normalise(n, t):
                if n >= 4:
                    act.wait_ge(tok_stored[n % 4], 16 * (n // 4))
                    act.wait_ge(xn_turned, n - 3)
                act.activation(xn[:, n % 4, :], x_sb[:, t, :], ACT.Identity, bias=shift[:, t:t + 1],
                               scale=rstd[:, t:t + 1]).then_inc(xn_ready, 1)

            def keep_turned(n):
                act.wait_ge(xn_turned, n + 1)
                if n >= 2:
                    act.wait_ge(logits_done, n - 1)
                act.activation(xnT[:, n % 2], turn_ps[n % 2], ACT.Copy).then_inc(xnT_ready, 1)

            n = exps = 0
            for step, tiles in enumerate(TILES_AT):
                for _ in range(tiles):
                    t = tile_order[n]
                    for g, (a, b) in enumerate(GROUPS_OF_TILES):
                        if t == a:
                            act.wait_ge(norm_ready, g + 1)
                    normalise(n, t)
                    if n:
                        keep_turned(n - 1)
                    n += 1
                if step in LOGIT_STEPS:
                    act.wait_ge(att_exp, 2 * exps + 1)
                    act.activation(prob, prob, ACT.Exp, scale=float(HD) ** -0.5).then_inc(att_exp, 1)
                    exps += 1
            keep_turned(n - 1)
            act.wait_ge(norm_ready, len(GROUPS_OF_TILES) + 1)
            normalise(n, 0)
            keep_turned(n)
            act.wait_ge(logits_done, TT)
            for h in range(2):
                act.activation(sc3[:, 16 * h:16 * h + 16, :], logit_ps[h][:, :].rearrange("p (t e) -> p t e", e=E),
                               ACT.Sigmoid).then_inc(scores_done, 1)

            def keep_x(body, step):
                f = counted(FED_AT, step)
                wait_count(act, x_turned, body, NFED, f + 1)
                prev = FED_AT[(f - 2) % NFED] + (1 if FED_AT[(f - 2) % NFED] in SHARED_AT else 0)
                wait_count(act, gu_done, body, STEPS, (f - 2) // NFED * STEPS + prev + 1)
                act.activation(xT[:, f % 2], turn_ps[f % 2], ACT.Copy).then_inc(xT_ready, 1)

            def gate(body, step):
                wait_count(act, gu_done, body, STEPS, step + 1)
                wait_count(act, hid_ready, body, STEPS, step - 1)
                act.activation(silu[:, step % 2], bank[2 + step % 2][:, 0:I], ACT.Silu).then_inc(silu_done, 1)

            def body_of(body, last):
                for step in range(STEPS):
                    gate(body, step)
                    if (step + 2) % STEPS in FED_AT and not (last and step + 2 >= STEPS):
                        keep_x(body, step + 2)

            act.wait_ge(tables_ready, 1)
            keep_x(0, 0)
            keep_x(0, 1)
            body_of(0, False)
            with act.Fori(1, BODIES - 1) as body:
                body_of(body, False)
            body_of(BODIES - 1, True)

            for g, (a, b) in enumerate([(0, 1), *GROUPS_OF_TILES]):
                act.wait_ge(tile_summed, b)
                if g == 0:
                    act.dma_start(out[:, 0:ROWS, :], x_sb[:, 0, :]).then_inc(stored, 16)
                else:
                    act.dma_start(out_rest[:, :, (a - 1) * D:(b - 1) * D],
                                  x_sb[:, a:b, :].rearrange("p j d -> p (j d)")).then_inc(stored, 16)
            act.wait_ge(stored, 16 * (1 + len(GROUPS_OF_TILES)))

        @block.tensor
        def _(pe):
            pe.wait_ge(consts_made, 3)
            pe.wait_ge(small_in, 32)

            def turn(n):
                pe.wait_ge(xn_ready, n + 1)
                if n >= 2:
                    pe.wait_ge(xnT_ready, n - 1)
                for c in range(KC):
                    ins = pe.transpose(turn_ps[n % 2][:, c, :], xn[:, n % 4, c * P:(c + 1) * P], ident[:, :])
                ins.then_inc(xn_turned, 1)

            def logits(n, t):
                pe.wait_ge(xnT_ready, n + 1)
                o = logit_ps[t // 16][:, (t % 16) * E:(t % 16 + 1) * E]
                for c in range(KC):
                    ins = pe.matmul(o, xnT[:, n % 2, c, :], rt_w[:, c, :], start=(c == 0), stop=(c == KC - 1),
                                    skip_group_check=True)
                ins.then_inc(logits_done, 1)

            step, turned = [0], [0]

            def after_dve():
                for _ in range(TILES_AT[step[0]]):
                    n = turned[0]
                    turn(n)
                    if n:
                        logits(n - 1, tile_order[n - 1])
                    turned[0] += 1
                step[0] += 1
                pe.wait_ge(att_dve, step[0])

            after_dve()
            pe.wait_ge(attw_in, 48)
            for m, src in enumerate((at_a, at_b)):
                for c in range(KC):
                    ins = pe.transpose(att_ps[0][:, (m * KC + c) * P:(m * KC + c + 1) * P],
                                       src[:, c * P:(c + 1) * P], ident[:, :])
            ins.then_inc(att_pe, 1)
            after_dve()
            for m, src in ((0, 0), (1, 1), (2, 1)):
                for c in range(KC):
                    for k in range(KC):
                        ins = pe.matmul(att_ps[1 + m][:, c * P:(c + 1) * P], w4[:, m, k, c * P:(c + 1) * P],
                                        inT[:, src, k, :], start=(k == 0), stop=(k == KC - 1))
            ins.then_inc(att_pe, 1)
            after_dve()
            for m, src in ((0, at_T), (1, at_d.rearrange("p (c t) -> p c t", c=KC))):
                for c in range(KC):
                    ins = pe.matmul(att_ps[m][:, c * P:(c + 1) * P], src[:, c, :],
                                    blockw[:, 1 + m].rearrange("p h d -> p (h d)"), start=True, stop=True)
            ins.then_inc(att_pe, 1)
            after_dve()
            for c in range(KC):
                ins = pe.transpose(att_ps[2][:, c * P:(c + 1) * P], at_a[:, c * P:(c + 1) * P], ident[:, :])
            for g in range(4):
                ins = pe.matmul(att_ps[(0, 3)[g // 2]][:, (g % 2) * D:(g % 2 + 1) * D],
                                spread[:, g].rearrange("p a t -> p (a t)"), at_b, start=True, stop=True)
            ins.then_inc(att_pe, 1)
            for it in range(ITERATIONS):
                after_dve()
                for c in range(KC):
                    ins = pe.matmul(att_ps[0][:, c * P:(c + 1) * P], q_cur[:, c, :],
                                    blockw[:, 0].rearrange("p h d -> p (h d)"), start=True, stop=True)
                ins.then_inc(att_pe, 1)
                after_dve()
                for c in range(KC):
                    ins = pe.transpose(att_ps[1][:, c * P:(c + 1) * P], at_a[:, c * P:(c + 1) * P], ident[:, :])
                ins.then_inc(att_pe, 1)
                after_dve()
                for g in range(4):
                    for c in range(KC):
                        ins = pe.matmul(att_ps[2][32 * g:32 * g + 32, c * D:(c + 1) * D],
                                        at_T[:, c, 32 * g:32 * g + 32],
                                        keys[:, c, :, 32 * g:32 * g + 32], start=True, stop=True)
                ins.then_inc(att_pe, 1)
                after_dve()
                for j in range(4):
                    ins = pe.transpose(att_ps[3][:, j * P:(j + 1) * P], prob[:, j * P:(j + 1) * P], ident[:, :])
                ins.then_inc(att_pe, 1)
                after_dve()
                for g in range(4):
                    for j in range(4):
                        ins = pe.matmul(att_ps[0][32 * g:32 * g + 32, 64 * j:64 * j + 64],
                                        probT[:, j, 32 * g:32 * g + 32], vals[:, g, 64 * j:64 * j + 64],
                                        start=True, stop=True)
                ins.then_inc(att_pe, 1)
                if it < ITERATIONS - 1:
                    after_dve()
                    for c in range(KC):
                        ins = pe.transpose(att_ps[1][:, c * P:(c + 1) * P],
                                           att_out[:, it, c * P:(c + 1) * P], ident[:, :])
                    ins.then_inc(att_pe, 1)
            after_dve()
            pe.matmul(att_ps[2][:, 0:1], ones_f[:, :], dsum[:, 0:1], start=True, stop=True).then_inc(att_pe, 1)
            after_dve()
            for c in range(KC):
                ins = pe.transpose(att_ps[1][:, c * P:(c + 1) * P], at_a[:, c * P:(c + 1) * P], ident[:, :])
            ins.then_inc(att_pe, 1)
            after_dve()
            for k in range(KC):
                ins = pe.matmul(att_ps[0][:, 0:D], at_T[:, k, :], w4[:, 3, k, :], start=(k == 0), stop=(k == KC - 1))
            ins.then_inc(att_pe, 1)
            assert step[0] == ATT_STEPS
            logits(TT - 2, tile_order[TT - 2])
            turn(TT - 1)
            logits(TT - 1, 0)

            pe.wait_ge(hot_ready, 1)
            for m, mat in enumerate((lower, ones_b)):
                for h in range(2):
                    for k in range(TOPK):
                        ins = pe.matmul(bank[4 + 2 * m + h][:, :], mat[:, :],
                                        hot_b[:, k, 16 * h:16 * h + 16, :].rearrange("p t e -> p (t e)"),
                                        start=(k == 0), stop=(k == TOPK - 1))
            ins.then_inc(counts_done, 1)
            turns = TT * TOPK // (2 * HOTS)

            def codes(i, first=False, last=False):
                for b in range(2):
                    pe.wait_ge(pairs_hot, i * 2 + b + 1)
                    for h in range(HOTS):
                        ins = pe.matmul(bank[0][:, 0:SLOT_TILES], hotr[:, b, :, h], hotj[:, b, :, h],
                                        start=(first and b == h == 0), stop=(last and b == 1 and h == HOTS - 1))
                    ins.then_inc(pairs_used, 1)

            codes(0, first=True)
            with pe.Fori(1, turns - 1) as i:
                codes(i)
            codes(turns - 1, last=True)
            pe.wait_ge(ecol_ready, 1)
            for c in range(2):
                ins = pe.matmul(bank[1][0:1, c * P:(c + 1) * P], ecol[:, c:c + 1], ident[:, :], start=True, stop=True)
            ins.then_inc(eid_turned, 1)

            pe.wait_ge(tables_ready, 1)
            pe.wait_ge(expert_w_in, 160)

            def turn_x(body, step):
                f = counted(FED_AT, step)
                s = step % STEPS
                if s in SHARED_AT:
                    w = SHARED_AT.index(s)
                    src = xs[:, w, :]
                    wait_count(pe, shared_in[w], body, 16, 16 * (step // STEPS + 1))
                else:
                    u = EXPERTS_AT.index(s) + step // STEPS * NEXP
                    src = xg[:, u % RING, :]
                    wait_count(pe, gathered[u % RING], body, 16 * NEXP // RING, 16 * (u // RING + 1))
                wait_count(pe, xT_ready, body, NFED, f - 1)
                for c in range(KC):
                    ins = pe.transpose(turn_ps[f % 2][:, c, :], src[:, c * P:(c + 1) * P], ident[:, :])
                ins.then_inc(x_turned, 1)

            def gate_up_of(body, step, eid):
                half_ = step in [s + 1 for s in SHARED_AT]
                f = counted(FED_AT, step - half_)
                if not half_:
                    wait_count(pe, xT_ready, body, NFED, f + 1)
                wait_count(pe, hid_ready, body, STEPS, step - 1)
                for c in range(KC):
                    if eid is None:
                        w = sgu_w[:, int(half_), c, :]
                    else:
                        w = gu_w[:, bass.ds(eid, 1), c, :].rearrange("p a i -> p (a i)")
                    ins = pe.matmul(bank[2 + step % 2][:, 0:2 * I], xT[:, f % 2, c, :], w, start=(c == 0),
                                    stop=(c == KC - 1))
                ins.then_inc(gu_done, 1)

            def turn_hid(body, step):
                wait_count(pe, hid_ready, body, STEPS, step + 1)
                wait_count(pe, hidT_ready, body, STEPS, step - 1)
                pe.transpose(bank[4 + step % 2][:, 0:P], hid[:, step % 2], ident[:, :]).then_inc(hid_turned, 1)

            def down_of(body, step, eid):
                s = step % STEPS
                first, second = s in SHARED_AT, s - 1 in SHARED_AT
                m = counted(DONE_AT, step)
                wait_count(pe, hidT_ready, body, STEPS, step + 1)
                if not second:
                    wait_count(pe, y_ready, body, NFED, m - 1)
                if eid is None:
                    w = sdn_w[:, int(second), :]
                else:
                    w = dn_w[:, bass.ds(eid, 1), :].rearrange("p a d -> p (a d)")
                ins = pe.matmul(bank[6 + m % 2][:, 0:D], hidT[:, step % 2], w, start=not second, stop=not first)
                ins.then_inc(y_done, 1)

            def body_of(body, first, last):
                src = (eids[0:1, body, 0:NEXP] if isinstance(body, int)
                       else eids[0:1, bass.ds(body, 1), 0:NEXP].rearrange("p a n -> p (a n)"))
                _, ids = nc.values_load_multi_w_load_instructions(
                    src, engines=(mybir.EngineType.PE,), min_val=0, max_val=E - 1,
                    skip_runtime_bounds_check_because="clamped to E - 1 where the table is made")
                eid_of = {s: ids[u] for u, s in enumerate(EXPERTS_AT)}
                for step in range(STEPS):
                    gate_up_of(body, step, eid_of.get(step))
                    if (step + 2) % STEPS in FED_AT and not (last and step + 2 >= STEPS):
                        turn_x(body, step + 2)
                    if not (first and step < 1):
                        turn_hid(body, step - 1)
                    if not (first and step < 2):
                        down_of(body, step - 2, eid_of.get(step - 2))

            turn_x(0, 0)
            turn_x(0, 1)
            body_of(0, True, False)
            with pe.Fori(1, BODIES - 1) as body:
                body_of(body, False, False)
            body_of(BODIES - 1, False, True)
            turn_hid(BODIES - 1, STEPS - 1)
            down_of(BODIES - 1, STEPS - 2, None)
            down_of(BODIES - 1, STEPS - 1, None)

        @block.vector
        def _(dve):
            done = [0]

            def seq(ins):
                done[0] += 1
                ins.then_inc(dve_seq, 1)
                dve.wait_ge(dve_seq, done[0])

            roots = [0]

            def root():
                roots[0] += 1
                dve.wait_ge(rstd_ready, roots[0])

            def finish_stats(a, b):
                dve.tensor_scalar(var_e[:, a:b], mv[:, a:b, 1:2].rearrange("p t a -> p (t a)"), EPS, None, ALU.add
                                  ).then_inc(var_ready, 1)
                root()
                dve.scalar_tensor_tensor(shift[:, a:b], mv[:, a:b, 0:1].rearrange("p t a -> p (t a)"), -1.0,
                                         rstd[:, a:b], ALU.mult, ALU.mult).then_inc(norm_ready, 1)

            pes, exps = [0], [0]

            def to_pe(ins):
                ins.then_inc(att_dve, 1)

            def from_pe():
                pes[0] += 1
                dve.wait_ge(att_pe, pes[0])

            dve.wait_ge(att_x_in, 16)
            dve.wait_ge(small_in, 32)
            x0 = x_sb[:, 0, :]

            def centred(dst, src):
                seq(dve.bn_stats(stats[:, 0, :], src))
                seq(dve.bn_aggr(mv[:, 0, :], stats[:, 0, :]))
                dve.tensor_scalar(var_e[:, 0:1], mv[:, 0, 1:2], EPS, None, ALU.add).then_inc(var_ready, 1)
                root()
                seq(dve.tensor_scalar(dst, src, mv[:, 0, 0:1], rstd[:, 0:1], ALU.subtract, ALU.mult))

            centred(at_c, x0)
            centred(at_d, at_c)
            for g, (a, b) in enumerate(GROUPS_OF_TILES):
                dve.wait_ge(x_in[g], 16)
                seq(dve.tensor_tensor(x_sb[:, a:b, :], x_sb[:, a:b, :],
                                      row("ob").unsqueeze(1).to_broadcast([P, b - a, D]), ALU.add))
                for t in range(a, b):
                    ins = dve.bn_stats(stats[:, t, :], x_sb[:, t, :])
                seq(ins)
                for t in range(a, b):
                    ins = dve.bn_aggr(mv[:, t, :], stats[:, t, :])
                seq(ins)
                finish_stats(a, b)
            dve.wait_ge(consts_made, N_CONSTS)
            dve.wait_ge(attw_in, 48)
            for m in range(3):
                dve.tensor_tensor(blockw[:, m], local_sb[:, m, :].unsqueeze(1).to_broadcast([P, HEADS // 2, HD]),
                                  head_mask[:, :].unsqueeze(2).to_broadcast([P, HEADS // 2, HD]), ALU.mult)
            for g in range(4):
                dve.tensor_copy(spread[:, g], ident[:, 32 * g:32 * g + 32].unsqueeze(1).to_broadcast([P, 4, 32]))
            dve.tensor_tensor(at_a, at_d, row("lna"), ALU.mult)
            to_pe(dve.tensor_tensor(at_b, at_d, row("lnb"), ALU.mult))
            from_pe()
            to_pe(dve.tensor_copy(inT[:, :, :, :].rearrange("p m c t -> p (m c t)"), att_ps[0][:, :]))
            from_pe()
            for c in range(KC):
                dve.tensor_scalar(q_cur[:, c, :], att_ps[1][:, c * P:(c + 1) * P], col_sb[:, c:c + 1], None, ALU.add)
                dve.tensor_copy(at_T[:, c, :], att_ps[2][:, c * P:(c + 1) * P])
                ins = dve.tensor_scalar(at_d[:, c * P:(c + 1) * P], att_ps[3][:, c * P:(c + 1) * P],
                                        col_sb[:, 2 + c:3 + c], None, ALU.add)
            to_pe(ins)
            from_pe()

            def heads(ap):
                return ap.rearrange("p (h d) -> p h d", d=HD)

            def per_head(ap):
                return ap.unsqueeze(2).to_broadcast([P, HEADS, HD])

            def per_dim(ap):
                return ap.unsqueeze(1).to_broadcast([P, HEADS, HD])

            def head_norm(dst, ps, bias, weight):
                seq(dve.tensor_tensor(heads(at_c), heads(ps), per_dim(row(bias)), ALU.add))
                seq(dve.tensor_reduce(hst[:, 0, :], heads(at_c), AX.X, ALU.add))
                seq(dve.tensor_scalar(hst[:, 1, :], hst[:, 0, :], 1.0 / HD, None, ALU.mult))
                seq(dve.tensor_tensor(heads(at_c), heads(at_c), per_head(hst[:, 1, :]), ALU.subtract))
                seq(dve.tensor_tensor(at_d, at_c, at_c, ALU.mult))
                seq(dve.tensor_reduce(hst[:, 0, :], heads(at_d), AX.X, ALU.add))
                dve.tensor_scalar(hst[:, 2, :], hst[:, 0, :], 1.0 / HD, EPS, ALU.mult, ALU.add).then_inc(var_ready, 1)
                root()
                seq(dve.tensor_tensor(heads(at_c), heads(at_c), per_head(hst[:, 3, :]), ALU.mult))
                return dve.tensor_tensor(heads(dst), heads(at_c), per_dim(row(weight)), ALU.mult)

            seq(dve.tensor_tensor(heads(at_b), heads(att_ps[1][:, 0:D]), per_dim(row("lvb")), ALU.add))
            to_pe(head_norm(at_a, att_ps[0][:, 0:D], "lkb", "lnd"))
            from_pe()
            for c in range(KC):
                dve.tensor_tensor(keys[:, c], att_ps[2][:, c * P:(c + 1) * P].unsqueeze(1).to_broadcast([P, HEADS // 2, P]),
                                  head_mask[:, :].unsqueeze(2).to_broadcast([P, HEADS // 2, P]), ALU.mult)
            for g in range(4):
                ps = att_ps[(0, 3)[g // 2]][:, (g % 2) * D:(g % 2 + 1) * D]
                for j in range(4):
                    ins = dve.tensor_tensor(heads(vals[:, g, 64 * j:64 * j + 64]), heads(ps[:, 64 * j:64 * j + 64]),
                                            quad_mask[:, :].unsqueeze(2).to_broadcast([P, 4, HD]), ALU.mult)
            to_pe(ins)
            prob3 = prob.rearrange("p (h k) -> p h k", k=32)

            def per_row(ap):
                return ap.unsqueeze(2).to_broadcast([P, HEADS, 32])

            for it in range(ITERATIONS):
                from_pe()
                to_pe(head_norm(at_a, att_ps[0][:, 0:D], "lqb", "lnc"))
                from_pe()
                to_pe(dve.tensor_copy(at_T[:, :, :].rearrange("p c t -> p (c t)"), att_ps[1][:, 0:D]))
                from_pe()
                seq(dve.tensor_tensor(prob3, att_ps[2][:, :].rearrange("p (h k) -> p h k", k=32),
                                      batch_mask[:, :, :].rearrange("p a k -> p (a k)").unsqueeze(1).to_broadcast([P, HEADS, 32]),
                                      ALU.add))
                seq(dve.tensor_reduce(hst[:, 0, :], prob3, AX.X, ALU.max))
                exps[0] += 2
                dve.tensor_tensor(prob3, prob3, per_row(hst[:, 0, :]), ALU.subtract).then_inc(att_exp, 1)
                dve.wait_ge(att_exp, exps[0])
                to_pe(dve.tensor_reduce(hst[:, 1, :], prob3, AX.X, ALU.add))
                from_pe()
                to_pe(dve.tensor_copy(probT[:, :, :].rearrange("p j t -> p (j t)"), att_ps[3][:, :]))
                seq(dve.reciprocal(hst[:, 4, :], hst[:, 1, :]))
                from_pe()
                o = att_out[:, it, :]
                ins = dve.tensor_tensor(heads(o), heads(att_ps[0][:, 0:D]), per_head(hst[:, 4, :]), ALU.mult)
                if it < ITERATIONS - 1:
                    to_pe(ins)
                    from_pe()
                    to_pe(dve.tensor_tensor(q_cur[:, :, :].rearrange("p c t -> p (c t)"),
                                            q_cur[:, :, :].rearrange("p c t -> p (c t)"), att_ps[1][:, 0:D], ALU.add))
                else:
                    seq(ins)
            seq(dve.tensor_tensor(at_b, att_out[:, 1, :], att_out[:, 0, :], ALU.subtract))
            to_pe(dve.tensor_reduce(dsum[:, 0:1], at_b, AX.X, ALU.add, apply_absolute_value=True))
            from_pe()
            seq(dve.tensor_scalar(dsum[:, 1:2], att_ps[2][:, 0:1], 1.0 / (TOKENS * D), None, ALU.mult))
            seq(dve.tensor_scalar(dsum[:, 2:3], dsum[:, 1:2], DIFF_FACTOR, DIFF_LIMIT, ALU.mult, ALU.add))
            seq(dve.tensor_tensor(dsum[:, 3:4], dsum[:, 1:2], dsum[:, 2:3], ALU.is_lt))
            seq(dve.tensor_copy(stop_i[:, :], dsum[:, 3:4]))
            seq(dve.tensor_copy(at_a, att_out[:, 2, :]))
            to_pe(dve.copy_predicated(at_a, stop_i[:, 0:1].to_broadcast([P, D]), att_out[:, 1, :]))
            from_pe()
            to_pe(dve.tensor_copy(at_T[:, :, :].rearrange("p c t -> p (c t)"), att_ps[1][:, 0:D]))
            from_pe()
            seq(dve.tensor_tensor(at_a, x0, row("ob"), ALU.add))
            seq(dve.tensor_tensor(x0, att_ps[0][:, 0:D], at_a, ALU.add))
            seq(dve.bn_stats(stats[:, 0, :], x0))
            seq(dve.bn_aggr(mv[:, 0, :], stats[:, 0, :]))
            finish_stats(0, 1)

            dve.wait_ge(scores_done, 2)
            sel3 = sel.rearrange("p (t e) -> p t e", e=E)
            seq(dve.tensor_tensor(sel3, sc3, row("bias").unsqueeze(1).to_broadcast([P, TT, E]), ALU.add))
            TG = TT * GROUPS
            s8 = sel.rearrange("p (n j) -> p n j", j=GSIZE)
            hi = work[:, 0, 0:TG * 4].rearrange("p (n j) -> p n j", j=4)
            lo = work[:, 0, TG * 4:TG * 8].rearrange("p (n j) -> p n j", j=4)
            dve.tensor_tensor(hi, s8[:, :, 0:4], s8[:, :, 4:8], ALU.max)
            seq(dve.tensor_tensor(lo, s8[:, :, 0:4], s8[:, :, 4:8], ALU.min))
            width, at = 2, 0
            tmp = work[:, 1, :]
            for width in (2, 1):
                new = [tmp[:, (at + k) * TG:(at + k + width) * TG].rearrange("p (n j) -> p n j", j=width)
                       for k in range(0, 4 * width, width)]
                h_new, h_min, l_max, l_new = new
                at += 0 if width == 1 else 8
                a, b = hi[:, :, 0:width], hi[:, :, width:2 * width]
                dve.tensor_tensor(h_new, a, b, ALU.max)
                dve.tensor_tensor(h_min, a, b, ALU.min)
                seq(dve.tensor_tensor(l_max, lo[:, :, 0:width], lo[:, :, width:2 * width], ALU.max))
                seq(dve.tensor_tensor(l_new, h_min, l_max, ALU.max))
                hi, lo = h_new, l_new
                tmp = work[:, 2, :]
                at = 0
            gs = small[:, 0, :].rearrange("p (t g) -> p t g", g=GROUPS)
            beats = small[:, 1, :].rearrange("p (t g) -> p t g", g=GROUPS)
            seq(dve.tensor_tensor(small[:, 0, :], hi.rearrange("p n a -> p (n a)"), lo.rearrange("p n a -> p (n a)"), ALU.add))
            seq(dve.tensor_copy(beats, iota_g[:, :].unsqueeze(1).to_broadcast([P, TT, GROUPS])))
            wins = []
            for d in range(1, GROUPS):
                c = small[:, 1 + d, :].rearrange("p (t g) -> p t g", g=GROUPS)[:, :, 0:GROUPS - d]
                ins = dve.tensor_tensor(c, gs[:, :, 0:GROUPS - d], gs[:, :, d:GROUPS], ALU.is_ge)
                wins.append(c)
            seq(ins)
            for d, c in enumerate(wins, 1):
                seq(dve.tensor_tensor(beats[:, :, 0:GROUPS - d], beats[:, :, 0:GROUPS - d], c, ALU.add))
                seq(dve.tensor_tensor(beats[:, :, d:GROUPS], beats[:, :, d:GROUPS], c, ALU.subtract))
            seq(dve.tensor_scalar(small[:, 5, :], small[:, 1, :], float(GROUPS - TOPG), None, ALU.is_ge))
            seq(dve.tensor_tensor(s8, s8, small[:, 5, :].unsqueeze(2).to_broadcast([P, TG, GSIZE]), ALU.mult))
            for t in range(TT):
                ins = dve.max(top8[:, t, :], sel3[:, t, :])
            seq(ins)
            for t in range(TT):
                ins = dve.max_index(idx8[:, t, :], top8[:, t, :], sel3[:, t, :])
            seq(ins)
            seq(dve.tensor_copy(idxf[:, :, :], idx8[:, :, 0:TOPK]))
            for k in range(TOPK):
                ins = dve.tensor_tensor(hot_b[:, k], iota_e[:, :].unsqueeze(1).to_broadcast([P, TT, E]),
                                        idxf[:, :, k:k + 1].to_broadcast([P, TT, E]), ALU.is_equal)
            ins.then_inc(hot_ready, 1)
            dve.wait_ge(counts_done, 1)
            cnt, incl, pos = work[:, 0, :], work[:, 1, :], work[:, 2, :]
            cnt_et = cnt.rearrange("p (e t) -> p e t", t=TT)
            incl_et = incl.rearrange("p (e t) -> p e t", t=TT)
            for h in range(2):
                seq(dve.tensor_copy(cnt_et[:, :, 16 * h:16 * h + 16].rearrange("p e t -> p t e"),
                                    bank[6 + h][:, :].rearrange("p (t e) -> p t e", e=E)))
            seq(dve.memset(pos, 1.0))
            seq(dve.tensor_tensor_scan(incl, pos, cnt, 0.0, ALU.mult, ALU.add))
            ends = incl_et[:, :, TT - 1:TT].rearrange("p e a -> p (e a)")
            begins, number, tiles, tiles_incl, tiles_i, adj = (e_row[:, k, :] for k in range(6))
            seq(dve.memset(e_row[:, :, :], 0.0))
            seq(dve.tensor_copy(begins[:, 1:E], ends[:, 0:E - 1]))
            seq(dve.tensor_tensor(number, ends, begins, ALU.subtract))
            tiles_i = tiles_i.bitcast(I32)
            seq(dve.tensor_scalar(tiles_i, number, float(P - 1), None, ALU.add))
            seq(dve.tensor_scalar(tiles_i, tiles_i, 7, None, ALU.arith_shift_right))
            seq(dve.tensor_copy(tiles, tiles_i))
            seq(dve.tensor_tensor_scan(tiles_incl, e_row[:, 6, :], tiles, 0.0, ALU.add, ALU.add))
            seq(dve.tensor_tensor(adj, tiles_incl, tiles, ALU.subtract))
            seq(dve.scalar_tensor_tensor(adj, adj, float(P), begins, ALU.mult, ALU.subtract))
            for c in range(2):
                seq(dve.tensor_tensor(e_row[:, 7, :], tiles_incl, iota_p[:, c:c + 1].to_broadcast([P, E]), ALU.is_le))
                seq(dve.tensor_reduce(ecol[:, 2 + c:3 + c], e_row[:, 7, :], AX.X, ALU.add))
            dve.tensor_scalar(ecol[:, 0:2], ecol[:, 2:4], float(E - 1), None, ALU.min).then_inc(ecol_ready, 1)
            seq(dve.tensor_tensor(incl, incl, cnt, ALU.subtract))
            seq(dve.tensor_tensor(incl_et, incl_et, adj.unsqueeze(2).to_broadcast([P, E, TT]), ALU.add))
            pos3 = pos.rearrange("p (t e) -> p t e", e=E)
            for h in range(2):
                seq(dve.tensor_tensor(pos3[:, 16 * h:16 * h + 16, :],
                                      bank[4 + h][:, :].rearrange("p (t e) -> p t e", e=E),
                                      incl_et[:, :, 16 * h:16 * h + 16].rearrange("p e t -> p t e"), ALU.add))
            for k in range(TOPK):
                seq(dve.tensor_tensor(cnt.rearrange("p (t e) -> p t e", e=E), hot_b[:, k], pos3, ALU.mult))
                seq(dve.tensor_reduce(slot_f[:, :, k:k + 1], cnt.rearrange("p (t e) -> p t e", e=E), AX.X, ALU.add))
            seq(dve.tensor_copy(slot_i[:, 0, :], slot_f[:, :, :].rearrange("p t k -> p (t k)")))
            seq(dve.tensor_scalar(slot_i[:, 1, :], slot_i[:, 0, :], P - 1, None, ALU.bitwise_and))
            seq(dve.tensor_scalar(slot_i[:, 2, :], slot_i[:, 0, :], 7, None, ALU.arith_shift_right))
            seq(dve.tensor_copy(slot_b[:, :, :], slot_i[:, 1:3, :]))
            codes_b = code_u[:, :].bitcast(BF16)

            def hot_pairs(i, first=False):
                for b in range(2):
                    if not first:
                        dve.wait_ge(pairs_used, i * 2 + b - 1)
                    g = (slice(b * HOTS, b * HOTS + HOTS) if first else bass.ds(i * (2 * HOTS) + b * HOTS, HOTS))

                    def by(column, n):
                        return column.unsqueeze(1).to_broadcast([P, n, HOTS])

                    dve.tensor_tensor(hotr[:, b], iota_b[:, 0:P, :], by(slot_b[:, 0, g], P), ALU.is_equal
                                      ).then_inc(rows_hot, 1)
                    dve.tensor_tensor(hotj[:, b], iota_b[:, :, :], by(slot_b[:, 1, g], SLOT_TILES), ALU.is_equal)
                    dve.wait_ge(rows_hot, i * 2 + b + 1)
                    dve.tensor_tensor(hotr[:, b], hotr[:, b], by(codes_b[:, g], P), ALU.mult).then_inc(pairs_hot, 1)

            hot_pairs(0, first=True)
            with dve.Fori(1, TT * TOPK // (2 * HOTS)) as i:
                hot_pairs(i)
            dve.wait_ge(pairs_used, TT * TOPK // HOTS)
            code_i = work[:, 0, 0:SLOT_TILES].bitcast(I32)
            pair_0 = work[:, 1, 0:SLOT_TILES].bitcast(I32)
            seq(dve.tensor_scalar(code_i, bank[0][:, 0:SLOT_TILES].bitcast(I32), 16, None, ALU.arith_shift_right))
            seq(dve.tensor_scalar(pair_at[:, :], code_i, float(-CODE), None, ALU.add))
            seq(dve.tensor_scalar(pair_0, pair_at[:, :], 0.0, None, ALU.max))
            seq(dve.tensor_scalar(tok_at[:, 0:SLOT_TILES], pair_0, 2, None, ALU.arith_shift_right))
            dve.wait_ge(eid_turned, 1)
            dve.tensor_copy(eids[0:1, :, 0:NEXP], bank[1][0:1, 0:SLOT_TILES].rearrange("p (b n) -> p b n", n=NEXP)
                            ).then_inc(tables_ready, 1)
            sum4 = small[:, 6, 0:TT]
            hot_score = cnt.rearrange("p (t e) -> p t e", e=E)
            weight_steps = []
            for k in range(TOPK):
                weight_steps += [lambda k=k: dve.tensor_tensor(hot_score, hot_b[:, k], sc3, ALU.mult),
                                 lambda k=k: dve.tensor_reduce(wts[:, :, k:k + 1], hot_score, AX.X, ALU.add)]
            weight_steps += [
                lambda: dve.tensor_reduce(sum4, wts[:, :, :], AX.X, ALU.add),
                lambda: dve.tensor_scalar(sum4, sum4, 1e-20, None, ALU.add),
                lambda: dve.reciprocal(sum4, sum4),
                lambda: dve.tensor_scalar(sum4, sum4, ROUTE_SCALE, None, ALU.mult),
                lambda: dve.tensor_tensor(wts[:, :, :], wts[:, :, :],
                                          sum4.unsqueeze(2).to_broadcast([P, TT, TOPK]), ALU.mult)]

            def hidden(body, step):
                wait_count(dve, silu_done, body, STEPS, step + 1)
                wait_count(dve, hid_turned, body, STEPS, step - 1)
                dve.tensor_tensor(hid[:, step % 2], silu[:, step % 2], bank[2 + step % 2][:, I:2 * I], ALU.mult
                                  ).then_inc(hid_ready, 1)

            def keep_hid(body, step):
                wait_count(dve, hid_turned, body, STEPS, step + 1)
                wait_count(dve, y_done, body, STEPS, step - 1)
                dve.tensor_copy(hidT[:, step % 2], bank[4 + step % 2][:, 0:P]).then_inc(hidT_ready, 1)

            def keep_y(body, step):
                s = step % STEPS
                if s in SHARED_AT:
                    return
                m = counted(DONE_AT, step)
                wait_count(dve, y_done, body, STEPS, step + 1)
                ps = bank[6 + m % 2][:, 0:D]
                if s - 1 in SHARED_AT:
                    w = SHARED_AT.index(s - 1) + 2 * (step // STEPS)
                    if isinstance(body, int):
                        xt = x_sb[:, 2 * body + w, :]
                    else:
                        xt = x_sb[:, bass.ds(body * 2 + w, 1), :].rearrange("p a d -> p (a d)")
                    dve.tensor_tensor(xt, ps, xt, ALU.add).then_inc(y_ready, 1)
                else:
                    u = EXPERTS_AT.index(s) + NEXP * (step // STEPS)
                    wait_count(dve, scattered[u % RING], body, 16 * NEXP // RING, 16 * (u // RING))
                    dve.tensor_copy(yb[:, u % RING, :], ps).then_inc(y_ready, 1)

            def body_of(body, first):
                for step in range(STEPS):
                    hidden(body, step)
                    if not (first and step < 1):
                        keep_hid(body, step - 1)
                    if not (first and step < 2):
                        keep_y(body, step - 2)
                    if first:
                        seq(weight_steps[step - 1]()) if 0 < step <= len(weight_steps) else None

            assert len(weight_steps) < STEPS
            body_of(0, True)
            with dve.Fori(1, BODIES) as body:
                body_of(body, False)
            keep_hid(BODIES - 1, STEPS - 1)
            keep_y(BODIES - 1, STEPS - 2)
            keep_y(BODIES - 1, STEPS - 1)

            for t in range(0, TT, 2):
                for k in range(TOPK):
                    for tile in (t, t + 1):
                        if k == 0:
                            dve.wait_ge(pairs_in[tile % 4], 16 * (tile // 4 + 1))
                        else:
                            dve.wait_ge(added, t * (TOPK - 1) + (k - 1) * 2 + tile - t + 1)
                        ins = dve.scalar_tensor_tensor(x_sb[:, tile, :], load4[:, tile % 4, k, :],
                                                       wts[:, tile, k:k + 1], x_sb[:, tile, :], ALU.mult, ALU.add)
                        ins.then_inc(added if k < TOPK - 1 else tile_summed, 1)


def kernel(**inputs):
    import concourse.bacc as bacc
    from concourse.bass_utils import run_bass_kernel_spmd

    a = {n.replace("L0_attn_", "").replace("L0_ffn_", ""): np.asarray(v) for n, v in inputs.items()}

    def chunked(w):
        w = w.reshape(*w.shape[:-2], -1, P, w.shape[-1])
        return np.ascontiguousarray(np.moveaxis(w, -2, 0))

    gate_up = np.concatenate([a["gate_w"], a["up_w"]], axis=1).transpose(0, 2, 1)
    shared = np.concatenate([a["shared_gate_w"].reshape(2, I, D), a["shared_up_w"].reshape(2, I, D)],
                            axis=1).transpose(0, 2, 1)
    wide = {"lna": "lna_w", "lnb": "lnb_w", "lnc": "lnc_w", "lnd": "lnd_w", "bias": "router_bias"}
    arrays = {
        "in_x": np.ascontiguousarray(a["x"]),
        "in_qkvo": chunked(np.stack([a[n].T for n in ("qw", "kw", "vw", "ow")])),
        "in_gate_up": chunked(gate_up),
        "in_down": np.ascontiguousarray(a["down_w"].transpose(2, 0, 1)),
        "in_sh_gate_up": chunked(shared),
        "in_sh_down": chunked(a["shared_down_w"].T),
        "in_router": chunked(a["router_weight"].T),
        "in_rows": np.concatenate([a[wide.get(n, n)] for n, _ in ROW_PARTS])[None],
        "in_cols": np.ascontiguousarray(np.concatenate([a["qb"].reshape(KC, P), a["vb"].reshape(KC, P)]).T),
        "in_local": np.ascontiguousarray(
            np.stack([np.tile(a[n].T, (P // HD, 1)) for n in ("lqw", "lkw", "lvw")], axis=1)),
    }
    nc = bacc.Bacc("TRN2", target_bir_lowering=False, num_devices=1)
    args = [nc.dram_tensor(n, v.shape, mybir.dt.from_np(v.dtype), kind="ExternalInput").ap()
            for n, v in arrays.items()]
    out = nc.dram_tensor("out", (BATCH, CTX, D), F32, kind="ExternalOutput").ap()
    tokens_dram = nc.dram_tensor("tokens_dram", (TOKENS, D), F32).ap()
    pairs_dram = nc.dram_tensor("pairs_dram", (PAIRS, D), F32).ap()
    build_program(nc, *args, out, tokens_dram, pairs_dram)
    r = run_bass_kernel_spmd(nc, [arrays], core_ids=[0])
    return r.results[0]["out"]
```

```python
from contextlib import ExitStack

import numpy as np

import concourse.bass as bass
from concourse import mybir

F32 = mybir.dt.float32
BF16 = mybir.dt.bfloat16
I32 = mybir.dt.int32
U16 = mybir.dt.uint16
U32 = mybir.dt.uint32
ALU = mybir.AluOpType
ACT = mybir.ActivationFunctionType
AX = mybir.AxisListType

P = 128
BATCH, CTX, D = 8, 512, 256
HEADS, HD = 16, 16
ROWS = 16
TOKENS = BATCH * CTX
TT = TOKENS // P
REST = (CTX - ROWS) // ROWS
E, I, TOPK = 32, 128, 4
GROUPS, GSIZE, TOPG = 4, 8, 2
PAIRS = TOKENS * TOPK
KC = D // P
EPS = 1e-5
MASKED = -1e30
ITERATIONS = 3
DIFF_LIMIT, DIFF_FACTOR = 0.01, 0.1
ROUTE_SCALE = 2.5
SLOT_TILES = 160
assert (PAIRS + E * (P - 1)) // P <= SLOT_TILES
GROUPS_OF_TILES = [(1, 9), (9, 17), (17, 25), (25, 32)]
POOL_GROUPS = [2, 3]
OUT_GROUPS = [(0, 1), (1, 9), (9, 17), (17, 25), (25, 28), (28, 30), (30, 32)]
LOADS = 8
CODE = 0x800
HOTS = 8
HOTBUFS = 4
CODED = 5
N_MASKS = 20
N_CONSTS = 27

STEPS = 12
WEIGHT_PARTS = 2 * TOPK + 2
SHARED_AT = [10, 11]
EXPERTS_AT = [s for s in range(STEPS) if s not in SHARED_AT]
NEXP = len(EXPERTS_AT)
BODIES = SLOT_TILES // NEXP
LATE = TT - BODIES
RING = 5
LAG = 3
EIDS = 12
assert LATE % 2 == 0 and NEXP == 2 * RING

ATT_STEPS = 4 + 6 * ITERATIONS - 1 + 3
LOGIT_STEPS = [4 + 6 * it + 2 for it in range(ITERATIONS)]
TILES_AT = [0, 0, 8, 8, 8, 7] + [0] * (ATT_STEPS - 6)
ROUTED_AT = 5
assert sum(TILES_AT) == TT - 1 and TILES_AT[ROUTED_AT]
ROOTS = [1, 1, GROUPS_OF_TILES[0], GROUPS_OF_TILES[1], HEADS, GROUPS_OF_TILES[2], GROUPS_OF_TILES[3],
         *[HEADS] * ITERATIONS, 1]

ROW_PARTS = [("lna", D), ("lnb", D), ("ob", D), ("lqb", HD), ("lkb", HD), ("lvb", HD), ("lnc", HD),
             ("lnd", HD), ("bias", E)]
ROW_AT = {}
for _name, _n in ROW_PARTS:
    ROW_AT[_name] = (sum(n for _, n in ROW_PARTS[:len(ROW_AT)]), _n)
ROW_LEN = sum(n for _, n in ROW_PARTS)


def wait_count(eng, sem, body, per_body, offset, loop_from=1):
    if isinstance(body, int):
        if body * per_body + offset > 0:
            eng.wait_ge(sem, body * per_body + offset)
    else:
        assert loop_from * per_body + offset > 0
        eng.wait_ge(sem, body * per_body + offset)


def late_loop(eng, parts, first):
    def turn_of(turn):
        for i in range(2):
            for part, offset in parts:
                if not isinstance(turn, int) or 0 <= 2 * turn + i + offset < LATE:
                    part(turn, i + offset)

    first()
    turn_of(0)
    turn_of(1)
    with eng.Fori(2, LATE // 2 - 1) as turn:
        turn_of(turn)
    for turn in range(LATE // 2 - 1, LATE // 2 + 2):
        turn_of(turn)


def build_program(nc, x, qkvo, gate_up, down, sh_gate_up, sh_down, router, rows, cols, local, out,
                  tokens_dram, pairs_dram):
    ctx = ExitStack()
    with ctx:
        def sb(name, shape, dt=F32):
            return ctx.enter_context(nc.sbuf_tensor(name, shape, dt))

        def sem(name):
            return ctx.enter_context(nc.semaphore(name))

        bank = [ctx.enter_context(nc.psum_tensor(f"bank{i}", [P, 512], F32)) for i in range(8)]
        gu_w = sb("gu_w", [P, E, KC, 2 * I])
        dn_w = sb("dn_w", [P, E, D])
        sgu_w = sb("sgu_w", [P, 2, KC, 2 * I])
        sdn_w = sb("sdn_w", [P, 2, D])
        x_sb = sb("x_sb", [P, TT, D])
        xn = sb("xn", [P, 4, D])
        row_sb = sb("row_sb", [P, ROW_LEN])
        col_sb = sb("col_sb", [P, 4])
        rt_w = sb("rt_w", [P, KC, E])
        ident = sb("ident", [P, P])
        stats = sb("stats", [P, TT, 6])
        mv = sb("mv", [P, TT, 2])
        var_e = sb("var_e", [P, TT])
        rstd = sb("rstd", [P, TT])
        half = sb("half", [P, TT])
        shift = sb("shift", [P, TT])
        xnT = sb("xnT", [P, 2, KC, P])
        wts = sb("wts", [P, TT, TOPK])
        pair_at = sb("pair_at", [P, SLOT_TILES], I32)
        tok_at = sb("tok_at", [P, SLOT_TILES + RING], I32)
        eids = sb("eids", [1, BODIES, EIDS], I32)

        def row(name):
            a, n = ROW_AT[name]
            return row_sb[:, a:a + n]

        scratch = sb("scratch", [P, 4 * TOPK * D])
        def piece(k, n=1):
            return scratch[:, k * TT * E:(k + n) * TT * E]
        sc3 = piece(0).rearrange("p (t e) -> p t e", e=E)
        sel = piece(1)
        hot_b = piece(2, 2).bitcast(BF16).rearrange("p (k t e) -> p k t e", k=TOPK, e=E)
        load4 = gu_w[:, 0:2 * LOADS].rearrange("p (s e) c i -> p s (e c i)", s=LOADS
                                               ).rearrange("p s (k d) -> p s k d", k=TOPK)
        work = sb("work", [P, 3, TT * E])
        small = sb("small", [P, 7, TT * GROUPS])
        idxf = sb("idxf", [P, TT, TOPK])
        e_row = sb("e_row", [P, 8, E])
        code_u = sb("code_u", [P, TT * TOPK], U16)
        lower = sb("lower", [P, P], BF16)
        ones_b = sb("ones_b", [P, P], BF16)
        iota_b = sb("iota_b", [P, SLOT_TILES, HOTS], BF16)
        iota_e = sb("iota_e", [P, E])
        iota_g = sb("iota_g", [P, GROUPS])
        iota_p = sb("iota_p", [P, 2])
        ecol = sb("ecol", [P, 4])

        loopb = sb("loopb", [P, 22 * D])
        def lb(k, n=1):
            return loopb[:, k * D:(k + n) * D]
        xg = lb(0, RING).rearrange("p (r d) -> p r d", d=D)
        more = work[:, 1:3, :].rearrange("p a n -> p (a n)")
        yb = [lb(5 + k) for k in range(RING)] + [more[:, k * D:(k + 1) * D] for k in range(NEXP - RING)]
        xs = lb(10, 2).rearrange("p (r d) -> p r d", d=D)
        xT = lb(12, 2).rearrange("p (r c t) -> p r c t", r=2, c=KC)
        silu = lb(14).rearrange("p (r i) -> p r i", r=2)
        hid = lb(15).rearrange("p (r i) -> p r i", r=2)
        hidT = lb(16).rearrange("p (r i) -> p r i", r=2)
        late_x = scratch[:, 0:LATE * D].rearrange("p (t d) -> p t d", t=LATE)
        late_silu = lb(0, 2).rearrange("p (r n) -> p r n", r=2)
        late_up = lb(2, 2).rearrange("p (r n) -> p r n", r=2)
        late_h = lb(17, 2).rearrange("p (r n) -> p r n", r=2)
        late_hidT = lb(19, 2).rearrange("p (r m t) -> p r m t", r=2, m=2)
        late_out = [lb(4), lb(21)]
        hotr = [area[:, k * D * 2:(k + 1) * D * 2].bitcast(BF16).rearrange("p (r h) -> p r h", h=HOTS)
                for area in (lb(0, 4), lb(17, 4)) for k in range(2)]
        hotj = [area[:, k * SLOT_TILES * 4:(k + 1) * SLOT_TILES * 4].bitcast(BF16)
                .rearrange("p (j h) -> p j h", h=HOTS)
                for area in (lb(11, 5), work[:, 0:2, :].rearrange("p a n -> p (a n)")) for k in range(2)]
        code_f = lb(16)[:, 0:TT * TOPK]
        top8 = dn_w[:, 18, :].rearrange("p (t j) -> p t j", j=8)
        idx8 = dn_w[:, 19, :].bitcast(U32).rearrange("p (t j) -> p t j", j=8)
        slots = lb(7, 4)
        slot_f = slots[:, 0:TT * TOPK].rearrange("p (t k) -> p t k", k=TOPK)
        slot_i = slots[:, P:4 * P].bitcast(I32).rearrange("p (m n) -> p m n", m=3)
        slot_b = slots[:, 4 * P:5 * P].bitcast(BF16).rearrange("p (m n) -> p m n", m=2)
        table_out = sb("table_out", [P, 1])
        stage_g = sb("stage_g", [P, NEXP], I32)
        stage_s = sb("stage_s", [P, NEXP], I32)

        att_mem = dn_w[:, 0:16, :].rearrange("p e d -> p (e d)")
        att_mem_b = dn_w[:, 16:18, :].rearrange("p e d -> p (e d)")
        w4 = att_mem[:, 0:8 * D].rearrange("p (m c n) -> p m c n", m=4, c=KC)
        head_mask = sb("head_mask", [P, HEADS // 2])
        quad_mask = sb("quad_mask", [P, 4])
        batch_mask = sb("batch_mask", [P, 2, ROWS])
        spread = att_mem_b[:, 0:4 * P].rearrange("p (g a t) -> p g a t", g=4, a=4)
        local_sb = sb("local_sb", [P, 3, HD])
        blockw = lb(0, 3).rearrange("p (m h d) -> p m h d", m=6, d=HD)[:, 0:3]
        at_a, at_b, at_c = lb(3), lb(4), lb(5)
        at_d = lb(6)
        inT = lb(7, 2).rearrange("p (m c t) -> p m c t", m=2, c=KC)
        q_cur = lb(9).rearrange("p (c t) -> p c t", c=KC)
        at_T = lb(10).rearrange("p (c t) -> p c t", c=KC)
        att_out = lb(11, 3).rearrange("p (i n) -> p i n", i=3)
        prob = lb(14, 2)
        probT = lb(16, 2).rearrange("p (j t) -> p j t", j=4)
        keys = att_mem[:, 8 * D:16 * D].rearrange("p (c h t) -> p c h t", c=KC, t=P)
        vals = lb(18, 4).rearrange("p (g n) -> p g n", g=4)
        hst = sb("hst", [P, 6, HEADS])
        dsum = sb("dsum", [P, 4])
        stop_i = sb("stop_i", [P, 1], I32)
        ones_f = lb(0, 3)[:, 4 * P:5 * P]

        att_x_in = sem("att_x_in")
        x_in = [sem(f"x_in{g}") for g in range(len(GROUPS_OF_TILES))]
        small_in = sem("small_in")
        attw_in = sem("attw_in")
        expert_w_in = sem("expert_w_in")
        consts_made = sem("consts_made")
        bias_added = sem("bias_added")
        var_ready = sem("var_ready")
        rstd_ready = sem("rstd_ready")
        norm_ready = sem("norm_ready")
        xn_ready = sem("xn_ready")
        xn_turned = sem("xn_turned")
        xnT_ready = sem("xnT_ready")
        logits_done = sem("logits_done")
        tok_stored = [sem(f"tok_stored{s}") for s in range(4)]
        att_ready = sem("att_ready")
        att_pe = sem("att_pe")
        att_exp = sem("att_exp")
        dve_seq = sem("dve_seq")
        pool_seq = sem("pool_seq")
        scores_done = sem("scores_done")
        hot_ready = sem("hot_ready")
        counts_done = sem("counts_done")
        places_ready = sem("places_ready")
        places_hot = sem("places_hot")
        pairs_hot = sem("pairs_hot")
        pairs_used = sem("pairs_used")
        rows_hot = sem("rows_hot")
        pairs_coded = sem("pairs_coded")
        codes_kept = sem("codes_kept")
        ecol_ready = sem("ecol_ready")
        eid_turned = sem("eid_turned")
        tables_ready = sem("tables_ready")
        gathered = [sem(f"gathered{k}") for k in range(RING)]
        scattered = [sem(f"scattered{k}") for k in range(NEXP)]
        shared_in = sem("shared_in")
        tokens_staged = sem("tokens_staged")
        pairs_staged = sem("pairs_staged")
        x_turned = sem("x_turned")
        xT_ready = sem("xT_ready")
        gu_done = sem("gu_done")
        silu_done = sem("silu_done")
        hid_ready = sem("hid_ready")
        hid_turned = sem("hid_turned")
        hidT_ready = sem("hidT_ready")
        y_done = sem("y_done")
        y_ready = sem("y_ready")
        weights_made = sem("weights_made")
        late_in = sem("late_in")
        late_ready = sem("late_ready")
        late_turned = sem("late_turned")
        late_xT = sem("late_xT")
        late_gu = sem("late_gu")
        late_gated = sem("late_gated")
        late_hid = sem("late_hid")
        late_hturned = sem("late_hturned")
        late_hT = sem("late_hT")
        late_down = sem("late_down")
        late_y = sem("late_y")
        late_added = sem("late_added")
        pairs_in = [sem(f"pairs_in{s}") for s in range(LOADS)]
        added = sem("added")
        tile_summed = sem("tile_summed")
        stored = sem("stored")

        turn_ps = [bank[0][:, 0:D].rearrange("p (c t) -> p c t", c=KC),
                   bank[1][:, 0:D].rearrange("p (c t) -> p c t", c=KC)]
        logit_ps = [bank[2], bank[3]]
        att_ps = bank[4:8]

        x_rest = x[:, ROWS:CTX, :].rearrange("b (q j) d -> b q (j d)", j=REST)
        out_rest = out[:, ROWS:CTX, :].rearrange("b (q j) d -> b q (j d)", j=REST)
        tok_tiles = tokens_dram.rearrange("(p t) d -> p t d", t=TT)
        pair_tiles = pairs_dram.rearrange("(p t k) d -> p t (k d)", t=TT, k=TOPK)
        tile_order = list(range(1, TT)) + [0]

        block = ctx.enter_context(nc.Block())

        @block.sync
        def _(sp):
            sp.dma_start(x_sb[:, 0, :], x[:, 0:ROWS, :]).then_inc(att_x_in, 16)
            sp.dma_start(row_sb[:, :], rows.to_broadcast([P, ROW_LEN])).then_inc(small_in, 16)
            sp.dma_start(rt_w[:, :, :], router).then_inc(small_in, 16)
            for g, (a, b) in enumerate(GROUPS_OF_TILES):
                sp.dma_start(x_sb[:, a:b, :].rearrange("p j d -> p (j d)"),
                             x_rest[:, :, (a - 1) * D:(b - 1) * D]).then_inc(x_in[g], 16)
            for n, t in enumerate(tile_order):
                if n == TT - 1:
                    for m in range(4):
                        e = slice(8 * m, 8 * m + 8)
                        sp.dma_start(gu_w[:, e], gate_up[:, e]).then_inc(expert_w_in, 16)
                    sp.dma_start(sgu_w[:, :, :, :], sh_gate_up).then_inc(expert_w_in, 16)
                    sp.dma_start(sdn_w[:, :, :], sh_down).then_inc(expert_w_in, 16)
                sp.wait_ge(xn_ready, n + 1)
                sp.dma_start(tok_tiles[:, t, :], xn[:, n % 4, :]).then_inc(tok_stored[n % 4], 16)
            sp.wait_ge(hot_ready, 2)
            for m in range(4):
                e = slice(8 * m, 8 * m + 8)
                sp.dma_start(dn_w[:, e], down[:, e]).then_inc(expert_w_in, 16)
            for s in range(4):
                sp.wait_ge(tok_stored[s], 16 * (TT // 4))
            sp.wait_ge(tables_ready, 1)
            sp.dma_start(xs[:, 0, :], tok_tiles[:, 0, :]).then_inc(shared_in, 16)
            sp.wait_ge(weights_made, 1)
            sp.dma_start(late_x[:, :, :].rearrange("p t d -> p (t d)"),
                         tok_tiles[:, TT - LATE:TT, :].rearrange("p t d -> p (t d)")).then_inc(late_in, 16)
            with sp.Fori(1, BODIES) as body:
                sp.wait_ge(x_turned, body * STEPS)
                sp.dma_start(xs[:, 0, :], tok_tiles[:, bass.ds(body, 1), :].rearrange("p a d -> p (a d)")
                             ).then_inc(shared_in, 16)
            for k in range(NEXP):
                sp.wait_ge(scattered[k], 16 * BODIES)

            def store(a, b):
                if b == 1:
                    sp.dma_start(out[:, 0:ROWS, :], x_sb[:, 0, :]).then_inc(stored, 16)
                else:
                    sp.dma_start(out_rest[:, :, (a - 1) * D:(b - 1) * D],
                                 x_sb[:, a:b, :].rearrange("p j d -> p (j d)")).then_inc(stored, 16)

            for t in range(TT):
                if t >= LOADS:
                    sp.wait_ge(tile_summed, t - LOADS + 1)
                sp.dma_start(load4[:, t % LOADS].rearrange("p k d -> p (k d)"), pair_tiles[:, t, :]
                             ).then_inc(pairs_in[t % LOADS], 16)
                for a, b in OUT_GROUPS:
                    if b == t - LOADS + 1:
                        store(a, b)
            for a, b in OUT_GROUPS:
                if b > TT - LOADS:
                    sp.wait_ge(tile_summed, b)
                    store(a, b)
            sp.wait_ge(stored, 16 * len(OUT_GROUPS))

        @block.gpsimd
        def _(pool):
            made = [0]

            def const(ins):
                made[0] += 1
                ins.then_inc(consts_made, 1)
                pool.wait_ge(consts_made, made[0])

            const(pool.memset(half[:, :], -0.5))
            const(pool.memset(ident[:, :], 0.0))
            const(pool.affine_select(ident[:, :], ident[:, :], [[-1, P]], ALU.not_equal, 1.0, base=0,
                                     channel_multiplier=1))
            rstds = [0]

            def inverse_root(what):
                rstds[0] += 1
                pool.wait_ge(var_ready, rstds[0])
                if what == HEADS:
                    pool.tensor_tensor(hst[:, 3, :], hst[:, 2, :], half[:, 0:HEADS], ALU.pow).then_inc(rstd_ready, 1)
                else:
                    a, b = (0, 1) if what == 1 else what
                    pool.tensor_tensor(rstd[:, a:b], var_e[:, a:b], half[:, a:b], ALU.pow).then_inc(rstd_ready, 1)

            const(pool.memset(ones_f[:, :], 1.0))
            const(pool.memset(ones_b[:, :], 1.0))
            for mask, n, width in ((head_mask, HEADS // 2, HD), (quad_mask, 4, 32)):
                const(pool.memset(mask[:, :], 1.0))
                const(pool.affine_select(mask[:, :], mask[:, :], [[-width, n]], ALU.is_ge, 0.0, base=0,
                                         channel_multiplier=1))
                const(pool.affine_select(mask[:, :], mask[:, :], [[width, n]], ALU.is_ge, 0.0, base=width - 1,
                                         channel_multiplier=-1))
            inverse_root(ROOTS[0])
            const(pool.memset(batch_mask[:, :, :], 0.0))
            for g in range(4):
                q = batch_mask[32 * g:32 * g + 32]
                const(pool.affine_select(q[:, 0, :], q[:, 0, :], [[0, ROWS]], ALU.is_ge, MASKED, base=ROWS - 1,
                                         channel_multiplier=-1))
                const(pool.affine_select(q[:, 1, :], q[:, 1, :], [[0, ROWS]], ALU.is_ge, MASKED, base=-ROWS,
                                         channel_multiplier=1))
            assert made[0] == N_MASKS
            inverse_root(ROOTS[1])
            const(pool.iota(iota_b[:, :, :], [[1, SLOT_TILES], [0, HOTS]], base=0, channel_multiplier=0,
                            allow_small_or_imprecise_dtypes=True))
            const(pool.iota(iota_e[:, :], [[1, E]], base=0, channel_multiplier=0,
                            allow_small_or_imprecise_dtypes=True))
            const(pool.iota(iota_g[:, :], [[1, GROUPS]], base=0, channel_multiplier=0,
                            allow_small_or_imprecise_dtypes=True))
            const(pool.iota(iota_p[:, :], [[P, 2]], base=0, channel_multiplier=1,
                            allow_small_or_imprecise_dtypes=True))
            const(pool.iota(code_u[:, :], [[1, TT * TOPK]], base=CODE, channel_multiplier=TT * TOPK,
                            allow_small_or_imprecise_dtypes=True))
            const(pool.affine_select(lower[:, :], ones_b[:, :], [[1, P]], ALU.is_gt, 0.0, base=0,
                                     channel_multiplier=-1))
            const(pool.memset(tok_at[:, SLOT_TILES:], 0))
            assert made[0] == N_CONSTS
            for what in ROOTS[2:]:
                inverse_root(what)
                if what in GROUPS_OF_TILES[0:2]:
                    g = POOL_GROUPS[GROUPS_OF_TILES.index(what)]
                    a, b = GROUPS_OF_TILES[g]
                    pool.wait_ge(small_in, 32)
                    pool.wait_ge(x_in[g], 16)
                    pool.tensor_tensor(x_sb[:, a:b, :], x_sb[:, a:b, :],
                                       row("ob").unsqueeze(1).to_broadcast([P, b - a, D]),
                                       ALU.add).then_inc(bias_added, 1)

            pool.wait_ge(places_ready, 1)
            for k in range(TOPK // 2, TOPK):
                pool.tensor_tensor(work[:, k - 1, :], hot_b[:, k].rearrange("p t e -> p (t e)"), sel, ALU.mult
                                   ).then_inc(places_hot, 1)

            for s in range(4):
                pool.wait_ge(tok_stored[s], 16 * (TT // 4))
            pool.wait_ge(tables_ready, 1)

            def gather(k, index):
                pool.indirect_dma_start(out=xg[:, k, :], out_offset=None, in_=tokens_dram,
                                        in_offset=bass.IndirectOffsetOnAxis(ap=index, axis=0)
                                        ).then_inc(gathered[k], 16)

            for k in range(RING):
                gather(k, tok_at[:, k:k + 1])

            def wait_before_dma(sem_, body, per_body, offset):
                wait_count(pool, sem_, body, per_body, offset)
                if not isinstance(body, int):
                    pool.sem_inc(pool_seq, 1)

            def scatter(body, u):
                back, column = divmod(u, NEXP)
                if column % RING == 0:
                    wait_before_dma(pairs_staged, body, 2, 2 * back + column // RING + 1)
                wait_before_dma(y_ready, body, STEPS, back * STEPS + EXPERTS_AT[column] + 1)
                pool.indirect_dma_start(out=pairs_dram,
                                        out_offset=bass.IndirectOffsetOnAxis(ap=stage_s[:, column:column + 1], axis=0),
                                        in_=yb[column], in_offset=None, bounds_check=PAIRS - 1,
                                        oob_is_err=False).then_inc(scattered[column], 16)

            def body_of(body, first, last):
                for u, step in enumerate(EXPERTS_AT):
                    k = u % RING
                    if k == 0:
                        wait_before_dma(tokens_staged, body, 2, 1 + u // RING)
                    if not (last and u >= NEXP - RING):
                        wait_before_dma(x_turned, body, STEPS, step + 1)
                        gather(k, stage_g[:, u:u + 1])
                    if not (first and u < LAG):
                        scatter(body, u - LAG)

            body_of(0, True, False)
            with pool.Fori(1, BODIES - 1) as body:
                body_of(body, False, False)
            body_of(BODIES - 1, False, True)
            for u in range(NEXP - LAG, NEXP):
                scatter(BODIES - 1, u)

            def late_input(turn, i):
                wait_count(pool, late_turned, turn, 2, i - 1, 2)
                src = late_x[:, 2 * turn + i, :] if isinstance(turn, int) else (
                    late_x[:, bass.ds(turn * 2 + i, 1), :].rearrange("p a d -> p (a d)"))
                pool.tensor_copy(xs[:, i % 2, :], src).then_inc(late_ready, 1)

            def late_gating(turn, i):
                wait_count(pool, late_gated, turn, 2, i + 1, 2)
                wait_count(pool, late_hturned, turn, 2, i - 1, 2)
                pool.tensor_tensor(late_h[:, i % 2], late_silu[:, i % 2], late_up[:, i % 2], ALU.mult
                                   ).then_inc(late_hid, 1)

            def late_add(turn, i):
                wait_count(pool, late_y, turn, 2, i + 1, 2)
                if isinstance(turn, int):
                    xt = x_sb[:, TT - LATE + 2 * turn + i, :]
                else:
                    xt = x_sb[:, bass.ds(turn * 2 + (TT - LATE + i), 1), :].rearrange("p a d -> p (a d)")
                pool.tensor_tensor(xt, xt, late_out[i % 2], ALU.add).then_inc(late_added, 1)

            pool.wait_ge(late_in, 16)
            pool.wait_ge(x_turned, BODIES * STEPS)
            late_loop(pool, [(late_input, 2), (late_gating, 0), (late_add, -3)], first=lambda: (
                late_input(0, 0), late_input(0, 1)))

        @block.scalar
        def _(act):
            act.dma_start(w4[:, :, :, :], qkvo).then_inc(attw_in, 16)
            act.dma_start(col_sb[:, :], cols).then_inc(attw_in, 16)
            act.dma_start(local_sb[:, :, :], local).then_inc(attw_in, 16)

            def normalise(n, t):
                if n >= 4:
                    act.wait_ge(tok_stored[n % 4], 16 * (n // 4))
                    act.wait_ge(xn_turned, n - 3)
                act.activation(xn[:, n % 4, :], x_sb[:, t, :], ACT.Identity, bias=shift[:, t:t + 1],
                               scale=rstd[:, t:t + 1]).then_inc(xn_ready, 1)

            def keep_turned(n):
                act.wait_ge(xn_turned, n + 1)
                if n >= 2:
                    act.wait_ge(logits_done, n - 1)
                act.activation(xnT[:, n % 2], turn_ps[n % 2], ACT.Copy).then_inc(xnT_ready, 1)

            def scores(a, b):
                for h in range(2):
                    lo, hi = max(a, 16 * h), min(b, 16 * h + 16)
                    if lo < hi:
                        act.activation(sc3[:, lo:hi, :], logit_ps[h][:, (lo - 16 * h) * E:(hi - 16 * h) * E]
                                       .rearrange("p (t e) -> p t e", e=E), ACT.Sigmoid).then_inc(scores_done, 1)

            def load_table(function):
                act.activation(table_out[:, :], half[:, 0:1], function)

            act.wait_ge(consts_made, 1)
            n = exps = 0
            for step, tiles in enumerate(TILES_AT):
                for _ in range(tiles):
                    t = tile_order[n]
                    for g, (a, b) in enumerate(GROUPS_OF_TILES):
                        if t == a:
                            act.wait_ge(norm_ready, g + 1)
                    normalise(n, t)
                    if n:
                        keep_turned(n - 1)
                    n += 1
                if step == ROUTED_AT:
                    keep_turned(n - 1)
                    act.wait_ge(logits_done, TT - 1)
                    scores(1, TT)
                    load_table(ACT.Exp)
                if step in LOGIT_STEPS:
                    act.wait_ge(att_exp, 2 * exps + 1)
                    act.activation(prob, prob, ACT.Exp, scale=float(HD) ** -0.5).then_inc(att_exp, 1)
                    exps += 1
                if step + 1 in LOGIT_STEPS:
                    act.wait_ge(att_pe, step + 1)
                    act.activation(at_T[:, :, :].rearrange("p c t -> p (c t)"), att_ps[1][:, 0:D], ACT.Copy
                                   ).then_inc(att_ready, 1)
                if step - 1 in LOGIT_STEPS:
                    act.wait_ge(att_pe, step + 1)
                    act.activation(probT[:, :, :].rearrange("p j t -> p (j t)"), att_ps[3][:, :], ACT.Copy
                                   ).then_inc(att_ready, 1)
            load_table(ACT.Sigmoid)
            act.wait_ge(norm_ready, len(GROUPS_OF_TILES) + 1)
            normalise(n, 0)
            keep_turned(n)
            act.wait_ge(logits_done, TT)
            scores(0, 1)
            load_table(ACT.Silu)
            act.activation(code_f[:, :], code_u[:, :].bitcast(BF16), ACT.Copy).then_inc(codes_kept, 1)
            act.wait_ge(codes_kept, 1)

            def code_pairs(i):
                for b in range(HOTBUFS):
                    act.wait_ge(rows_hot, i * HOTBUFS + b + 1)
                    for h in range(CODED):
                        if isinstance(i, int):
                            scale = code_f[:, b * HOTS + h:b * HOTS + h + 1]
                        else:
                            scale = code_f[:, bass.ds(i * (HOTBUFS * HOTS) + (b * HOTS + h), 1)]
                        ins = act.activation(hotr[b][:, :, h], hotr[b][:, :, h], ACT.Copy, scale=scale)
                    ins.then_inc(pairs_coded, 1)

            code_pairs(0)
            with act.Fori(1, TT * TOPK // (HOTBUFS * HOTS)) as i:
                code_pairs(i)

            def keep_x(body, step):
                wait_count(act, x_turned, body, STEPS, step + 1)
                wait_count(act, gu_done, body, STEPS, step - 1)
                act.activation(xT[:, step % 2], turn_ps[step % 2], ACT.Copy).then_inc(xT_ready, 1)

            def gate(body, step):
                wait_count(act, gu_done, body, STEPS, step + 1)
                wait_count(act, hid_ready, body, STEPS, step - 1)
                act.activation(silu[:, step % 2], bank[2 + step % 2][:, 0:I], ACT.Silu).then_inc(silu_done, 1)

            def stage_tokens(body, h):
                for k in range(RING):
                    wait_count(act, gathered[k], body, 16 * 2, 16 * h if not isinstance(body, int) or body else 0)
                at, first = h * RING, body * NEXP + h * RING
                act.activation(stage_g[:, at:at + RING], tok_at[:, bass.ds(first + RING, RING)], ACT.Copy
                               ).then_inc(tokens_staged, 1)

            def stage_pairs(body, h):
                for k in range(RING):
                    wait_count(act, scattered[h * RING + k], body, 16, 0)
                at, first = h * RING, body * NEXP + h * RING
                act.activation(stage_s[:, at:at + RING], pair_at[:, bass.ds(first, RING)], ACT.Copy
                               ).then_inc(pairs_staged, 1)

            def body_of(body, last):
                for step in range(STEPS):
                    gate(body, step)
                    if not (last and step + 2 >= STEPS):
                        keep_x(body, step + 2)
                    if step in (0, RING):
                        stage_pairs(body, step // RING)
                    if step == RING - 3 and not (isinstance(body, int) and body == 0):
                        stage_tokens(body, 1)
                    if step == NEXP - 3 and not last:
                        stage_tokens(body + 1, 0)

            act.wait_ge(tables_ready, 1)
            stage_tokens(0, 0)
            stage_tokens(0, 1)
            keep_x(0, 0)
            keep_x(0, 1)
            body_of(0, False)
            with act.Fori(1, BODIES - 1) as body:
                body_of(body, False)
            body_of(BODIES - 1, True)

            def late_keep_x(turn, i):
                wait_count(act, late_turned, turn, 2, i + 1, 2)
                wait_count(act, late_gu, turn, 2, i - 1, 2)
                act.activation(xT[:, i % 2], turn_ps[i % 2], ACT.Copy).then_inc(late_xT, 1)

            def late_gate(turn, i):
                wait_count(act, late_gu, turn, 2, i + 1, 2)
                wait_count(act, late_hid, turn, 2, i - 1, 2)
                gu = bank[2 + i % 2][:, :].rearrange("p (m k i) -> p m k i", m=2, k=2)
                act.activation(late_silu[:, i % 2].rearrange("p (m i) -> p m i", m=2), gu[:, :, 0, :], ACT.Silu)
                act.activation(late_up[:, i % 2].rearrange("p (m i) -> p m i", m=2), gu[:, :, 1, :], ACT.Copy
                               ).then_inc(late_gated, 1)

            def late_keep_hid(turn, i):
                wait_count(act, late_hturned, turn, 2, i + 1, 2)
                wait_count(act, late_down, turn, 2, i - 1, 2)
                act.activation(late_hidT[:, i % 2].rearrange("p m t -> p (m t)"), bank[4 + i % 2][:, 0:2 * P], ACT.Copy
                               ).then_inc(late_hT, 1)

            def late_keep_y(turn, i):
                wait_count(act, late_down, turn, 2, i + 1, 2)
                wait_count(act, late_added, turn, 2, i - 1, 2)
                act.activation(late_out[i % 2], bank[6 + i % 2][:, 0:D], ACT.Copy).then_inc(late_y, 1)

            act.wait_ge(gu_done, BODIES * STEPS)
            late_loop(act, [(late_gate, 0), (late_keep_x, 1), (late_keep_hid, -1), (late_keep_y, -2)],
                      first=lambda: late_keep_x(0, 0))

        @block.tensor
        def _(pe):
            pe.wait_ge(consts_made, 3)
            pe.wait_ge(small_in, 32)

            def turn(n):
                pe.wait_ge(xn_ready, n + 1)
                if n >= 2:
                    pe.wait_ge(xnT_ready, n - 1)
                for c in range(KC):
                    ins = pe.transpose(turn_ps[n % 2][:, c, :], xn[:, n % 4, c * P:(c + 1) * P], ident[:, :])
                ins.then_inc(xn_turned, 1)

            def logits(n, t):
                pe.wait_ge(xnT_ready, n + 1)
                o = logit_ps[t // 16][:, (t % 16) * E:(t % 16 + 1) * E]
                for c in range(KC):
                    ins = pe.matmul(o, xnT[:, n % 2, c, :], rt_w[:, c, :], start=(c == 0), stop=(c == KC - 1),
                                    skip_group_check=True)
                ins.then_inc(logits_done, 1)

            step, turned = [0], [0]

            def after_dve():
                for _ in range(TILES_AT[step[0]]):
                    n = turned[0]
                    turn(n)
                    if n:
                        logits(n - 1, tile_order[n - 1])
                    turned[0] += 1
                if step[0] == ROUTED_AT:
                    logits(TT - 2, tile_order[TT - 2])
                step[0] += 1
                pe.wait_ge(att_ready, step[0])

            after_dve()
            pe.wait_ge(attw_in, 48)
            for m, src in enumerate((at_a, at_b)):
                for c in range(KC):
                    ins = pe.transpose(att_ps[0][:, (m * KC + c) * P:(m * KC + c + 1) * P],
                                       src[:, c * P:(c + 1) * P], ident[:, :])
            ins.then_inc(att_pe, 1)
            after_dve()
            for m, src in ((0, 0), (1, 1), (2, 1)):
                for c in range(KC):
                    for k in range(KC):
                        ins = pe.matmul(att_ps[1 + m][:, c * P:(c + 1) * P], w4[:, m, k, c * P:(c + 1) * P],
                                        inT[:, src, k, :], start=(k == 0), stop=(k == KC - 1))
            ins.then_inc(att_pe, 1)
            after_dve()
            for m, src in ((0, at_T), (1, at_d.rearrange("p (c t) -> p c t", c=KC))):
                for c in range(KC):
                    ins = pe.matmul(att_ps[m][:, c * P:(c + 1) * P], src[:, c, :],
                                    blockw[:, 1 + m].rearrange("p h d -> p (h d)"), start=True, stop=True)
            ins.then_inc(att_pe, 1)
            after_dve()
            for c in range(KC):
                ins = pe.transpose(att_ps[2][:, c * P:(c + 1) * P], at_a[:, c * P:(c + 1) * P], ident[:, :])
            for g in range(4):
                ins = pe.matmul(att_ps[(0, 3)[g // 2]][:, (g % 2) * D:(g % 2 + 1) * D],
                                spread[:, g].rearrange("p a t -> p (a t)"), at_b, start=True, stop=True)
            ins.then_inc(att_pe, 1)
            for it in range(ITERATIONS):
                after_dve()
                for c in range(KC):
                    ins = pe.matmul(att_ps[0][:, c * P:(c + 1) * P], q_cur[:, c, :],
                                    blockw[:, 0].rearrange("p h d -> p (h d)"), start=True, stop=True)
                ins.then_inc(att_pe, 1)
                after_dve()
                for c in range(KC):
                    ins = pe.transpose(att_ps[1][:, c * P:(c + 1) * P], at_a[:, c * P:(c + 1) * P], ident[:, :])
                ins.then_inc(att_pe, 1)
                after_dve()
                for g in range(4):
                    for c in range(KC):
                        ins = pe.matmul(att_ps[2][32 * g:32 * g + 32, c * D:(c + 1) * D],
                                        at_T[:, c, 32 * g:32 * g + 32],
                                        keys[:, c, :, 32 * g:32 * g + 32], start=True, stop=True)
                ins.then_inc(att_pe, 1)
                after_dve()
                for j in range(4):
                    ins = pe.transpose(att_ps[3][:, j * P:(j + 1) * P], prob[:, j * P:(j + 1) * P], ident[:, :])
                ins.then_inc(att_pe, 1)
                after_dve()
                for g in range(4):
                    for j in range(4):
                        ins = pe.matmul(att_ps[0][32 * g:32 * g + 32, 64 * j:64 * j + 64],
                                        probT[:, j, 32 * g:32 * g + 32], vals[:, g, 64 * j:64 * j + 64],
                                        start=True, stop=True)
                ins.then_inc(att_pe, 1)
                if it < ITERATIONS - 1:
                    after_dve()
                    for c in range(KC):
                        ins = pe.transpose(att_ps[1][:, c * P:(c + 1) * P],
                                           att_out[:, it, c * P:(c + 1) * P], ident[:, :])
                    ins.then_inc(att_pe, 1)
            after_dve()
            pe.matmul(att_ps[2][:, 0:1], ones_f[:, :], dsum[:, 0:1], start=True, stop=True).then_inc(att_pe, 1)
            after_dve()
            for c in range(KC):
                ins = pe.transpose(att_ps[1][:, c * P:(c + 1) * P], at_a[:, c * P:(c + 1) * P], ident[:, :])
            ins.then_inc(att_pe, 1)
            after_dve()
            for k in range(KC):
                ins = pe.matmul(att_ps[0][:, 0:D], at_T[:, k, :], w4[:, 3, k, :], start=(k == 0), stop=(k == KC - 1))
            ins.then_inc(att_pe, 1)
            assert step[0] == ATT_STEPS
            turn(TT - 1)
            logits(TT - 1, 0)

            for ready, parts in ((1, [(1, 16), (16, TT)]), (2, [(0, 1)])):
                pe.wait_ge(hot_ready, ready)
                for m, mat in enumerate((lower, ones_b)):
                    for a, b in parts:
                        for k in range(TOPK):
                            ins = pe.matmul(bank[4 + 2 * m + a // 16][:, (a % 16) * E:((b - 1) % 16 + 1) * E], mat[:, :],
                                            hot_b[:, k, a:b, :].rearrange("p t e -> p (t e)"),
                                            start=(k == 0), stop=(k == TOPK - 1), skip_group_check=True)
            ins.then_inc(counts_done, 1)
            turns = TT * TOPK // (HOTBUFS * HOTS)

            def codes(i, first=False, last=False):
                for b in range(HOTBUFS):
                    pe.wait_ge(pairs_hot, i * HOTBUFS + b + 1)
                    pe.wait_ge(pairs_coded, i * HOTBUFS + b + 1)
                    for h in range(HOTS):
                        ins = pe.matmul(bank[0][:, 0:SLOT_TILES], hotr[b][:, :, h], hotj[b][:, :, h],
                                        start=(first and b == h == 0),
                                        stop=(last and b == HOTBUFS - 1 and h == HOTS - 1))
                    ins.then_inc(pairs_used, 1)

            codes(0, first=True)
            with pe.Fori(1, turns - 1) as i:
                codes(i)
            codes(turns - 1, last=True)
            pe.wait_ge(ecol_ready, 1)
            for c in range(2):
                ins = pe.matmul(bank[1][0:1, c * P:(c + 1) * P], ecol[:, c:c + 1], ident[:, :], start=True, stop=True)
            ins.then_inc(eid_turned, 1)

            pe.wait_ge(tables_ready, 1)
            pe.wait_ge(expert_w_in, 160)

            def turn_x(body, step):
                s = step % STEPS
                if s in SHARED_AT:
                    src = xs[:, 0, :]
                    wait_count(pe, shared_in, body, 16, 16 * (step // STEPS + 1))
                else:
                    u = EXPERTS_AT.index(s) + step // STEPS * NEXP
                    src = xg[:, u % RING, :]
                    wait_count(pe, gathered[u % RING], body, 16 * NEXP // RING, 16 * (u // RING + 1))
                wait_count(pe, xT_ready, body, STEPS, step - 1)
                for c in range(KC):
                    ins = pe.transpose(turn_ps[step % 2][:, c, :], src[:, c * P:(c + 1) * P], ident[:, :])
                ins.then_inc(x_turned, 1)

            def gate_up_of(body, step, eid):
                wait_count(pe, xT_ready, body, STEPS, step + 1)
                wait_count(pe, hid_ready, body, STEPS, step - 1)
                for c in range(KC):
                    if eid is None:
                        w = sgu_w[:, SHARED_AT.index(step), c, :]
                    else:
                        w = gu_w[:, bass.ds(eid, 1), c, :].rearrange("p a i -> p (a i)")
                    ins = pe.matmul(bank[2 + step % 2][:, 0:2 * I], xT[:, step % 2, c, :], w, start=(c == 0),
                                    stop=(c == KC - 1))
                ins.then_inc(gu_done, 1)

            def turn_hid(body, step):
                wait_count(pe, hid_ready, body, STEPS, step + 1)
                wait_count(pe, hidT_ready, body, STEPS, step - 1)
                pe.transpose(bank[4 + step % 2][:, 0:P], hid[:, step % 2], ident[:, :]).then_inc(hid_turned, 1)

            def down_of(body, step, eid):
                wait_count(pe, hidT_ready, body, STEPS, step + 1)
                wait_count(pe, y_ready, body, STEPS, step - 1)
                if eid is None:
                    w = sdn_w[:, SHARED_AT.index(step % STEPS), :]
                else:
                    w = dn_w[:, bass.ds(eid, 1), :].rearrange("p a d -> p (a d)")
                pe.matmul(bank[6 + step % 2][:, 0:D], hidT[:, step % 2], w, start=True, stop=True).then_inc(y_done, 1)

            def body_of(body, first, last):
                src = (eids[0:1, body, 0:NEXP] if isinstance(body, int)
                       else eids[0:1, bass.ds(body, 1), 0:NEXP].rearrange("p a n -> p (a n)"))
                _, ids = nc.values_load_multi_w_load_instructions(
                    src, engines=(mybir.EngineType.PE,), min_val=0, max_val=E - 1,
                    skip_runtime_bounds_check_because="clamped to E - 1 where the table is made")
                eid_of = {s: ids[u] for u, s in enumerate(EXPERTS_AT)}
                for step in range(STEPS):
                    gate_up_of(body, step, eid_of.get(step))
                    if not (last and step + 2 >= STEPS):
                        turn_x(body, step + 2)
                    if not (first and step < 1):
                        turn_hid(body, step - 1)
                    if not (first and step < 2):
                        down_of(body, step - 2, eid_of.get(step - 2))

            turn_x(0, 0)
            turn_x(0, 1)
            body_of(0, True, False)
            with pe.Fori(1, BODIES - 1) as body:
                body_of(body, False, False)
            body_of(BODIES - 1, False, True)
            turn_hid(BODIES - 1, STEPS - 1)
            down_of(BODIES - 1, STEPS - 2, None)
            down_of(BODIES - 1, STEPS - 1, None)

            def late_turn(turn, i):
                wait_count(pe, late_ready, turn, 2, i + 1, 2)
                wait_count(pe, late_xT, turn, 2, i - 1, 2)
                for c in range(KC):
                    ins = pe.transpose(turn_ps[i % 2][:, c, :], xs[:, i % 2, c * P:(c + 1) * P], ident[:, :])
                ins.then_inc(late_turned, 1)

            def late_gate_up(turn, i):
                wait_count(pe, late_xT, turn, 2, i + 1, 2)
                wait_count(pe, late_gated, turn, 2, i - 1, 2)
                for m in range(2):
                    for c in range(KC):
                        ins = pe.matmul(bank[2 + i % 2][:, m * 2 * I:(m + 1) * 2 * I], xT[:, i % 2, c, :],
                                        sgu_w[:, m, c, :], start=(c == 0), stop=(c == KC - 1))
                ins.then_inc(late_gu, 1)

            def late_turn_hid(turn, i):
                wait_count(pe, late_hid, turn, 2, i + 1, 2)
                wait_count(pe, late_hT, turn, 2, i - 1, 2)
                for m in range(2):
                    ins = pe.transpose(bank[4 + i % 2][:, m * P:(m + 1) * P], late_h[:, i % 2, m * P:(m + 1) * P],
                                       ident[:, :])
                ins.then_inc(late_hturned, 1)

            def late_down_of(turn, i):
                wait_count(pe, late_hT, turn, 2, i + 1, 2)
                wait_count(pe, late_y, turn, 2, i - 1, 2)
                for m in range(2):
                    ins = pe.matmul(bank[6 + i % 2][:, 0:D], late_hidT[:, i % 2, m, :], sdn_w[:, m, :],
                                    start=(m == 0), stop=(m == 1))
                ins.then_inc(late_down, 1)

            pe.wait_ge(xT_ready, BODIES * STEPS)
            pe.wait_ge(hid_ready, BODIES * STEPS)
            pe.wait_ge(hidT_ready, BODIES * STEPS)
            pe.wait_ge(y_ready, BODIES * STEPS)
            late_loop(pe, [(late_gate_up, 0), (late_turn, 1), (late_turn_hid, -1), (late_down_of, -2)],
                      first=lambda: late_turn(0, 0))

        @block.vector
        def _(dve):
            done = [0]

            def seq(ins):
                done[0] += 1
                ins.then_inc(dve_seq, 1)
                dve.wait_ge(dve_seq, done[0])

            roots = [0]

            def root():
                roots[0] += 1
                dve.wait_ge(rstd_ready, roots[0])

            def ask_root(a, b):
                dve.tensor_scalar(var_e[:, a:b], mv[:, a:b, 1:2].rearrange("p t a -> p (t a)"), EPS, None, ALU.add
                                  ).then_inc(var_ready, 1)

            def shifts(a, b):
                root()
                dve.scalar_tensor_tensor(shift[:, a:b], mv[:, a:b, 0:1].rearrange("p t a -> p (t a)"), -1.0,
                                         rstd[:, a:b], ALU.mult, ALU.mult).then_inc(norm_ready, 1)

            def statistics(g):
                a, b = GROUPS_OF_TILES[g]
                dve.wait_ge(x_in[g], 16)
                if g in POOL_GROUPS:
                    dve.wait_ge(bias_added, POOL_GROUPS.index(g) + 1)
                else:
                    seq(dve.tensor_tensor(x_sb[:, a:b, :], x_sb[:, a:b, :],
                                          row("ob").unsqueeze(1).to_broadcast([P, b - a, D]), ALU.add))
                for t in range(a, b):
                    ins = dve.bn_stats(stats[:, t, :], x_sb[:, t, :])
                seq(ins)
                for t in range(a, b):
                    ins = dve.bn_aggr(mv[:, t, :], stats[:, t, :])
                seq(ins)
                ask_root(a, b)

            def route(a, b):
                n = b - a
                TG = n * GROUPS
                dve.wait_ge(scores_done, 3 if a == 0 else 2)
                dve.wait_ge(consts_made, N_CONSTS)
                sel_ab = sel[:, a * E:b * E]
                sel3 = sel_ab.rearrange("p (t e) -> p t e", e=E)
                seq(dve.tensor_tensor(sel3, sc3[:, a:b, :], row("bias").unsqueeze(1).to_broadcast([P, n, E]), ALU.add))
                yield
                s8 = sel_ab.rearrange("p (n j) -> p n j", j=GSIZE)
                hi = work[:, 0, 0:TG * 4].rearrange("p (n j) -> p n j", j=4)
                lo = work[:, 0, TG * 4:TG * 8].rearrange("p (n j) -> p n j", j=4)
                dve.tensor_tensor(hi, s8[:, :, 0:4], s8[:, :, 4:8], ALU.max)
                seq(dve.tensor_tensor(lo, s8[:, :, 0:4], s8[:, :, 4:8], ALU.min))
                yield
                for level, width in enumerate((2, 1)):
                    h_new, h_min, l_max, l_new = [work[:, 1 + level, k * TG:(k + width) * TG].rearrange(
                        "p (n j) -> p n j", j=width) for k in range(0, 4 * width, width)]
                    top, low = hi[:, :, 0:width], hi[:, :, width:2 * width]
                    dve.tensor_tensor(h_new, top, low, ALU.max)
                    dve.tensor_tensor(h_min, top, low, ALU.min)
                    seq(dve.tensor_tensor(l_max, lo[:, :, 0:width], lo[:, :, width:2 * width], ALU.max))
                    seq(dve.tensor_tensor(l_new, h_min, l_max, ALU.max))
                    hi, lo = h_new, l_new
                    yield

                def groups(k):
                    return small[:, k, 0:TG].rearrange("p (t g) -> p t g", g=GROUPS)

                gs, beats = groups(0), groups(1)
                seq(dve.tensor_tensor(small[:, 0, 0:TG], hi.rearrange("p n a -> p (n a)"),
                                      lo.rearrange("p n a -> p (n a)"), ALU.add))
                dve.tensor_copy(beats, iota_g[:, :].unsqueeze(1).to_broadcast([P, n, GROUPS]))
                wins = []
                for d in range(1, GROUPS):
                    c = groups(1 + d)[:, :, 0:GROUPS - d]
                    ins = dve.tensor_tensor(c, gs[:, :, 0:GROUPS - d], gs[:, :, d:GROUPS], ALU.is_ge)
                    wins.append(c)
                seq(ins)
                yield
                for d, c in enumerate(wins, 1):
                    seq(dve.tensor_tensor(beats[:, :, 0:GROUPS - d], beats[:, :, 0:GROUPS - d], c, ALU.add))
                    seq(dve.tensor_tensor(beats[:, :, d:GROUPS], beats[:, :, d:GROUPS], c, ALU.subtract))
                yield
                seq(dve.tensor_scalar(small[:, 5, 0:TG], small[:, 1, 0:TG], float(GROUPS - TOPG), None, ALU.is_ge))
                seq(dve.tensor_tensor(s8, s8, small[:, 5, 0:TG].unsqueeze(2).to_broadcast([P, TG, GSIZE]), ALU.mult))
                yield
                for t in range(a, b):
                    ins = dve.max(top8[:, t, :], sel3[:, t - a, :])
                    if t % 8 == 7:
                        yield
                seq(ins)
                for t in range(a, b):
                    ins = dve.max_index(idx8[:, t, :], top8[:, t, :], sel3[:, t - a, :])
                    if t % 8 == 7:
                        yield
                seq(ins)
                seq(dve.tensor_copy(idxf[:, a:b, :], idx8[:, a:b, 0:TOPK]))
                for k in range(TOPK):
                    ins = dve.tensor_tensor(hot_b[:, k, a:b], iota_e[:, :].unsqueeze(1).to_broadcast([P, n, E]),
                                            idxf[:, a:b, k:k + 1].to_broadcast([P, n, E]), ALU.is_equal)
                    if k == TOPK - 1:
                        ins.then_inc(hot_ready, 1)
                    yield

            others = route(1, TT)

            def fill(parts):
                for _ in range(parts):
                    next(others, None)

            pes, exps = [0], [0]

            def to_pe(ins):
                ins.then_inc(att_ready, 1)

            def from_pe():
                pes[0] += 1
                dve.wait_ge(att_pe, pes[0])

            def by_scalar():
                pes[0] += 1

            dve.wait_ge(att_x_in, 16)
            x0 = x_sb[:, 0, :]

            def centred(dst, src):
                seq(dve.bn_stats(stats[:, 0, :], src))
                seq(dve.bn_aggr(mv[:, 0, :], stats[:, 0, :]))
                ask_root(0, 1)
                root()
                seq(dve.tensor_scalar(dst, src, mv[:, 0, 0:1], rstd[:, 0:1], ALU.subtract, ALU.mult))

            centred(at_c, x0)
            centred(at_d, at_c)
            dve.wait_ge(small_in, 32)
            dve.wait_ge(consts_made, N_MASKS)
            dve.wait_ge(attw_in, 48)
            centre = hst[:, 5, 0:4]
            biases = row_sb[:, ROW_AT["lqb"][0]:ROW_AT["lqb"][0] + 2 * HD].rearrange("p (m d) -> p m d", m=2)
            for k, what in enumerate((local_sb[:, 0:2, :], biases)):
                mean = centre[:, 2 * k:2 * k + 2]
                seq(dve.tensor_reduce(mean, what, AX.X, ALU.add))
                seq(dve.tensor_scalar(mean, mean, 1.0 / HD, None, ALU.mult))
                seq(dve.tensor_tensor(what, what, mean.unsqueeze(2).to_broadcast([P, 2, HD]), ALU.subtract))
            for m in range(3):
                dve.tensor_tensor(blockw[:, m], local_sb[:, m, :].unsqueeze(1).to_broadcast([P, HEADS // 2, HD]),
                                  head_mask[:, :].unsqueeze(2).to_broadcast([P, HEADS // 2, HD]), ALU.mult)
            for g in range(4):
                dve.tensor_copy(spread[:, g], ident[:, 32 * g:32 * g + 32].unsqueeze(1).to_broadcast([P, 4, 32]))
            dve.tensor_tensor(at_a, at_d, row("lna"), ALU.mult)
            to_pe(dve.tensor_tensor(at_b, at_d, row("lnb"), ALU.mult))
            statistics(0)
            from_pe()
            to_pe(dve.tensor_copy(inT[:, :, :, :].rearrange("p m c t -> p (m c t)"), att_ps[0][:, :]))
            shifts(*GROUPS_OF_TILES[0])
            statistics(1)
            from_pe()
            for c in range(KC):
                dve.tensor_scalar(q_cur[:, c, :], att_ps[1][:, c * P:(c + 1) * P], col_sb[:, c:c + 1], None, ALU.add)
                dve.tensor_copy(at_T[:, c, :], att_ps[2][:, c * P:(c + 1) * P])
                ins = dve.tensor_scalar(at_d[:, c * P:(c + 1) * P], att_ps[3][:, c * P:(c + 1) * P],
                                        col_sb[:, 2 + c:3 + c], None, ALU.add)
            to_pe(ins)
            shifts(*GROUPS_OF_TILES[1])
            from_pe()

            def heads(ap):
                return ap.rearrange("p (h d) -> p h d", d=HD)

            def per_head(ap):
                return ap.unsqueeze(2).to_broadcast([P, HEADS, HD])

            def per_dim(ap):
                return ap.unsqueeze(1).to_broadcast([P, HEADS, HD])

            def head_norm(dst, ps, bias, weight, fill_wait):
                seq(dve.tensor_tensor(heads(at_c), heads(ps), per_dim(row(bias)), ALU.add))
                seq(dve.tensor_tensor(at_d, at_c, at_c, ALU.mult))
                seq(dve.tensor_reduce(hst[:, 0, :], heads(at_d), AX.X, ALU.add))
                dve.tensor_scalar(hst[:, 2, :], hst[:, 0, :], 1.0 / HD, EPS, ALU.mult, ALU.add).then_inc(var_ready, 1)
                fill_wait()
                root()
                seq(dve.tensor_tensor(heads(at_c), heads(at_c), per_head(hst[:, 3, :]), ALU.mult))
                return dve.tensor_tensor(heads(dst), heads(at_c), per_dim(row(weight)), ALU.mult)

            seq(dve.tensor_tensor(heads(at_b), heads(att_ps[1][:, 0:D]), per_dim(row("lvb")), ALU.add))
            to_pe(head_norm(at_a, att_ps[0][:, 0:D], "lkb", "lnd", lambda: statistics(2)))
            shifts(*GROUPS_OF_TILES[2])
            statistics(3)
            shifts(*GROUPS_OF_TILES[3])
            from_pe()
            for c in range(KC):
                dve.tensor_tensor(keys[:, c], att_ps[2][:, c * P:(c + 1) * P].unsqueeze(1).to_broadcast([P, HEADS // 2, P]),
                                  head_mask[:, :].unsqueeze(2).to_broadcast([P, HEADS // 2, P]), ALU.mult)
            for g in range(4):
                ps = att_ps[(0, 3)[g // 2]][:, (g % 2) * D:(g % 2 + 1) * D]
                ins = dve.tensor_tensor(vals[:, g].rearrange("p (j q d) -> p j q d", j=4, q=4),
                                        ps.rearrange("p (j q d) -> p j q d", j=4, q=4),
                                        quad_mask[:, :].unsqueeze(1).unsqueeze(3).to_broadcast([P, 4, 4, HD]), ALU.mult)
            to_pe(ins)
            prob3 = prob.rearrange("p (h k) -> p h k", k=32)

            def per_row(ap):
                return ap.unsqueeze(2).to_broadcast([P, HEADS, 32])

            for it in range(ITERATIONS):
                from_pe()
                to_pe(head_norm(at_a, att_ps[0][:, 0:D], "lqb", "lnc", lambda: fill(2 if it else 0)))
                by_scalar()
                fill(2)
                from_pe()
                seq(dve.tensor_tensor(prob3, att_ps[2][:, :].rearrange("p (h k) -> p h k", k=32),
                                      batch_mask[:, :, :].rearrange("p a k -> p (a k)").unsqueeze(1).to_broadcast([P, HEADS, 32]),
                                      ALU.add))
                seq(dve.tensor_reduce(hst[:, 0, :], prob3, AX.X, ALU.max))
                exps[0] += 2
                dve.tensor_tensor(prob3, prob3, per_row(hst[:, 0, :]), ALU.subtract).then_inc(att_exp, 1)
                dve.wait_ge(att_exp, exps[0])
                to_pe(dve.tensor_reduce(hst[:, 1, :], prob3, AX.X, ALU.add))
                by_scalar()
                fill(2)
                from_pe()
                seq(dve.reciprocal(hst[:, 4, :], hst[:, 1, :]))
                o = att_out[:, it, :]
                ins = dve.tensor_tensor(heads(o), heads(att_ps[0][:, 0:D]), per_head(hst[:, 4, :]), ALU.mult)
                if it < ITERATIONS - 1:
                    to_pe(ins)
                    fill(1)
                    from_pe()
                    to_pe(dve.tensor_tensor(q_cur[:, :, :].rearrange("p c t -> p (c t)"),
                                            q_cur[:, :, :].rearrange("p c t -> p (c t)"), att_ps[1][:, 0:D], ALU.add))
                    fill(1)
                else:
                    seq(ins)
            for _ in others:
                pass
            seq(dve.tensor_tensor(at_b, att_out[:, 1, :], att_out[:, 0, :], ALU.subtract))
            to_pe(dve.tensor_reduce(dsum[:, 0:1], at_b, AX.X, ALU.add, apply_absolute_value=True))
            from_pe()
            seq(dve.tensor_scalar(dsum[:, 1:2], att_ps[2][:, 0:1], 1.0 / (TOKENS * D), None, ALU.mult))
            seq(dve.tensor_scalar(dsum[:, 2:3], dsum[:, 1:2], DIFF_FACTOR, DIFF_LIMIT, ALU.mult, ALU.add))
            seq(dve.tensor_tensor(dsum[:, 3:4], dsum[:, 1:2], dsum[:, 2:3], ALU.is_lt))
            seq(dve.tensor_copy(stop_i[:, :], dsum[:, 3:4]))
            seq(dve.tensor_copy(at_a, att_out[:, 2, :]))
            to_pe(dve.copy_predicated(at_a, stop_i[:, 0:1].to_broadcast([P, D]), att_out[:, 1, :]))
            from_pe()
            to_pe(dve.tensor_copy(at_T[:, :, :].rearrange("p c t -> p (c t)"), att_ps[1][:, 0:D]))
            from_pe()
            seq(dve.tensor_tensor(at_a, x0, row("ob"), ALU.add))
            seq(dve.tensor_tensor(x0, att_ps[0][:, 0:D], at_a, ALU.add))
            seq(dve.bn_stats(stats[:, 0, :], x0))
            seq(dve.bn_aggr(mv[:, 0, :], stats[:, 0, :]))
            ask_root(0, 1)
            shifts(0, 1)

            for _ in route(0, 1):
                pass
            dve.wait_ge(counts_done, 1)
            cnt, pos = work[:, 0, :], sel
            before = work[:, 1:3, :].rearrange("p a n -> p (a n)")[:, 0:TT * E + 1]
            before_et = before[:, 0:TT * E].rearrange("p (e t) -> p e t", t=TT)
            cnt_et = cnt.rearrange("p (e t) -> p e t", t=TT)
            dve.memset(before[:, 0:1], 0.0)
            dve.memset(e_row[:, :, :], 0.0)
            for h in range(2):
                ins = dve.tensor_copy(cnt_et[:, :, 16 * h:16 * h + 16].rearrange("p e t -> p t e"),
                                      bank[6 + h][:, :].rearrange("p (t e) -> p t e", e=E))
            seq(ins)
            seq(dve.tensor_tensor_scan(before[:, 1:], ones_b[:, 0:1].to_broadcast([P, TT * E]), cnt, 0.0,
                                       ALU.mult, ALU.add))
            begins, number, tiles, tiles_incl, tiles_i, adj = (e_row[:, k, :] for k in range(6))
            seq(dve.tensor_copy(begins, before_et[:, :, 0:1].rearrange("p e a -> p (e a)")))
            ends = before[:, 1:].rearrange("p (e t) -> p e t", t=TT)[:, :, TT - 1:TT].rearrange("p e a -> p (e a)")
            seq(dve.tensor_tensor(number, ends, begins, ALU.subtract))
            tiles_i = tiles_i.bitcast(I32)
            seq(dve.tensor_scalar(tiles_i, number, float(P - 1), None, ALU.add))
            seq(dve.tensor_scalar(tiles_i, tiles_i, 7, None, ALU.arith_shift_right))
            seq(dve.tensor_copy(tiles, tiles_i))
            seq(dve.tensor_tensor_scan(tiles_incl, e_row[:, 6, :], tiles, 0.0, ALU.add, ALU.add))
            seq(dve.tensor_tensor(adj, tiles_incl, tiles, ALU.subtract))
            seq(dve.scalar_tensor_tensor(adj, adj, float(P), begins, ALU.mult, ALU.subtract))
            for c in range(2):
                seq(dve.tensor_tensor(e_row[:, 7, :], tiles_incl, iota_p[:, c:c + 1].to_broadcast([P, E]), ALU.is_le))
                seq(dve.tensor_reduce(ecol[:, 2 + c:3 + c], e_row[:, 7, :], AX.X, ALU.add))
            dve.tensor_scalar(ecol[:, 0:2], ecol[:, 2:4], float(E - 1), None, ALU.min).then_inc(ecol_ready, 1)
            seq(dve.tensor_tensor(before_et, before_et, adj.unsqueeze(2).to_broadcast([P, E, TT]), ALU.add))
            pos3 = pos.rearrange("p (t e) -> p t e", e=E)
            for h in range(2):
                seq(dve.tensor_tensor(pos3[:, 16 * h:16 * h + 16, :],
                                      bank[4 + h][:, :].rearrange("p (t e) -> p t e", e=E),
                                      before_et[:, :, 16 * h:16 * h + 16].rearrange("p e t -> p t e"), ALU.add))
            dve.sem_inc(places_ready, 1)
            for k in range(TOPK):
                mine = cnt.rearrange("p (t e) -> p t e", e=E)
                if k < TOPK // 2:
                    seq(dve.tensor_tensor(mine, hot_b[:, k], pos3, ALU.mult))
                else:
                    mine = work[:, k - 1, :].rearrange("p (t e) -> p t e", e=E)
                    dve.wait_ge(places_hot, k - TOPK // 2 + 1)
                seq(dve.tensor_reduce(slot_f[:, :, k:k + 1], mine, AX.X, ALU.add))
            seq(dve.tensor_copy(slot_i[:, 0, :], slot_f[:, :, :].rearrange("p t k -> p (t k)")))
            seq(dve.tensor_scalar(slot_i[:, 1, :], slot_i[:, 0, :], P - 1, None, ALU.bitwise_and))
            seq(dve.tensor_scalar(slot_i[:, 2, :], slot_i[:, 0, :], 7, None, ALU.arith_shift_right))
            seq(dve.tensor_copy(slot_b[:, :, :], slot_i[:, 1:3, :]))
            codes_b = code_u[:, :].bitcast(BF16)

            def hot_pairs(i, first=False):
                for b in range(HOTBUFS):
                    if not first:
                        dve.wait_ge(pairs_used, i * HOTBUFS + b - (HOTBUFS - 1))

                    def by(columns, h, n):
                        at = b * HOTS + h
                        columns = (columns[:, at:(b + 1) * HOTS] if first
                                   else columns[:, bass.ds(i * (HOTBUFS * HOTS) + at, HOTS - h)])
                        return columns.unsqueeze(1).to_broadcast([P, n, HOTS - h])

                    dve.tensor_tensor(hotr[b], iota_b[:, 0:P, :], by(slot_b[:, 0], 0, P), ALU.is_equal
                                      ).then_inc(rows_hot, 1)
                    dve.tensor_tensor(hotj[b], iota_b[:, :, :], by(slot_b[:, 1], 0, SLOT_TILES), ALU.is_equal)
                    dve.wait_ge(rows_hot, i * HOTBUFS + b + 1)
                    dve.tensor_tensor(hotr[b][:, :, CODED:HOTS], hotr[b][:, :, CODED:HOTS], by(codes_b, CODED, P),
                                      ALU.mult).then_inc(pairs_hot, 1)

            hot_pairs(0, first=True)
            with dve.Fori(1, TT * TOPK // (HOTBUFS * HOTS)) as i:
                hot_pairs(i)
            dve.wait_ge(pairs_used, TT * TOPK // HOTS)
            code_i = work[:, 0, 0:SLOT_TILES].bitcast(I32)
            pair_0 = work[:, 1, 0:SLOT_TILES].bitcast(I32)
            seq(dve.tensor_scalar(code_i, bank[0][:, 0:SLOT_TILES].bitcast(I32), 16, None, ALU.arith_shift_right))
            seq(dve.tensor_scalar(pair_at[:, :], code_i, float(-CODE), None, ALU.add))
            seq(dve.tensor_scalar(pair_0, pair_at[:, :], 0.0, None, ALU.max))
            seq(dve.tensor_scalar(tok_at[:, 0:SLOT_TILES], pair_0, 2, None, ALU.arith_shift_right))
            dve.wait_ge(eid_turned, 1)
            dve.tensor_copy(eids[0:1, :, 0:NEXP], bank[1][0:1, 0:SLOT_TILES].rearrange("p (b n) -> p b n", n=NEXP)
                            ).then_inc(tables_ready, 1)
            sum4 = small[:, 6, 0:TT]
            hot_score = cnt.rearrange("p (t e) -> p t e", e=E)

            def weights(part):
                k, reduce = divmod(part, 2)
                if k < TOPK and not reduce:
                    seq(dve.tensor_tensor(hot_score, hot_b[:, k], sc3, ALU.mult))
                elif k < TOPK:
                    seq(dve.tensor_reduce(wts[:, :, k:k + 1], hot_score, AX.X, ALU.add))
                elif not reduce:
                    seq(dve.tensor_reduce(sum4, wts[:, :, :], AX.X, ALU.add))
                    seq(dve.tensor_scalar(sum4, sum4, 1e-20, None, ALU.add))
                else:
                    seq(dve.reciprocal(sum4, sum4))
                    seq(dve.tensor_scalar(sum4, sum4, ROUTE_SCALE, None, ALU.mult))
                    seq(dve.tensor_tensor(wts[:, :, :], wts[:, :, :],
                                          sum4.unsqueeze(2).to_broadcast([P, TT, TOPK]), ALU.mult))
                    dve.sem_inc(weights_made, 1)

            def hidden(body, step):
                wait_count(dve, silu_done, body, STEPS, step + 1)
                wait_count(dve, hid_turned, body, STEPS, step - 1)
                dve.tensor_tensor(hid[:, step % 2], silu[:, step % 2], bank[2 + step % 2][:, I:2 * I], ALU.mult
                                  ).then_inc(hid_ready, 1)

            def keep_hid(body, step):
                wait_count(dve, hid_turned, body, STEPS, step + 1)
                wait_count(dve, y_done, body, STEPS, step - 1)
                dve.tensor_copy(hidT[:, step % 2], bank[4 + step % 2][:, 0:P]).then_inc(hidT_ready, 1)

            def keep_y(body, step):
                s = step % STEPS
                wait_count(dve, y_done, body, STEPS, step + 1)
                ps = bank[6 + step % 2][:, 0:D]
                if s in SHARED_AT:
                    if isinstance(body, int):
                        xt = x_sb[:, body + step // STEPS, :]
                    else:
                        xt = x_sb[:, bass.ds(body + step // STEPS, 1), :].rearrange("p a d -> p (a d)")
                    if s == SHARED_AT[1]:
                        wait_count(dve, y_ready, body, STEPS, step)
                    dve.tensor_tensor(xt, ps, xt, ALU.add).then_inc(y_ready, 1)
                else:
                    u = EXPERTS_AT.index(s)
                    wait_count(dve, scattered[u], body, 16, 16 * (step // STEPS))
                    dve.tensor_copy(yb[u], ps).then_inc(y_ready, 1)

            def body_of(body, first):
                for step in range(STEPS):
                    hidden(body, step)
                    if not (first and step < 1):
                        keep_hid(body, step - 1)
                    if not (first and step < 2):
                        keep_y(body, step - 2)
                    if first and 1 <= step <= WEIGHT_PARTS:
                        weights(step - 1)

            body_of(0, True)
            with dve.Fori(1, BODIES) as body:
                body_of(body, False)
            keep_hid(BODIES - 1, STEPS - 1)
            keep_y(BODIES - 1, STEPS - 2)
            keep_y(BODIES - 1, STEPS - 1)

            for t in range(0, TT, 2):
                for k in range(TOPK):
                    for tile in (t, t + 1):
                        if k == 0:
                            dve.wait_ge(pairs_in[tile % LOADS], 16 * (tile // LOADS + 1))
                            if tile >= TT - LATE:
                                dve.wait_ge(late_added, tile - (TT - LATE) + 1)
                        else:
                            dve.wait_ge(added, t * (TOPK - 1) + (k - 1) * 2 + tile - t + 1)
                        ins = dve.scalar_tensor_tensor(x_sb[:, tile, :], load4[:, tile % LOADS, k, :],
                                                       wts[:, tile, k:k + 1], x_sb[:, tile, :], ALU.mult, ALU.add)
                        ins.then_inc(added if k < TOPK - 1 else tile_summed, 1)


def kernel(**inputs):
    import concourse.bacc as bacc
    from concourse.bass_utils import run_bass_kernel_spmd

    a = {n.replace("L0_attn_", "").replace("L0_ffn_", ""): np.asarray(v) for n, v in inputs.items()}

    def chunked(w):
        w = w.reshape(*w.shape[:-2], -1, P, w.shape[-1])
        return np.ascontiguousarray(np.moveaxis(w, -2, 0))

    gate_up = np.concatenate([a["gate_w"], a["up_w"]], axis=1).transpose(0, 2, 1)
    shared = np.concatenate([a["shared_gate_w"].reshape(2, I, D), a["shared_up_w"].reshape(2, I, D)],
                            axis=1).transpose(0, 2, 1)
    wide = {"lna": "lna_w", "lnb": "lnb_w", "lnc": "lnc_w", "lnd": "lnd_w", "bias": "router_bias"}
    arrays = {
        "in_x": np.ascontiguousarray(a["x"]),
        "in_qkvo": chunked(np.stack([a[n].T for n in ("qw", "kw", "vw", "ow")])),
        "in_gate_up": chunked(gate_up),
        "in_down": np.ascontiguousarray(a["down_w"].transpose(2, 0, 1)),
        "in_sh_gate_up": chunked(shared),
        "in_sh_down": chunked(a["shared_down_w"].T),
        "in_router": chunked(a["router_weight"].T),
        "in_rows": np.concatenate([a[wide.get(n, n)] for n, _ in ROW_PARTS])[None],
        "in_cols": np.ascontiguousarray(np.concatenate([a["qb"].reshape(KC, P), a["vb"].reshape(KC, P)]).T),
        "in_local": np.ascontiguousarray(
            np.stack([np.tile(a[n].T, (P // HD, 1)) for n in ("lqw", "lkw", "lvw")], axis=1)),
    }
    nc = bacc.Bacc("TRN2", target_bir_lowering=False, num_devices=1)
    args = [nc.dram_tensor(n, v.shape, mybir.dt.from_np(v.dtype), kind="ExternalInput").ap()
            for n, v in arrays.items()]
    out = nc.dram_tensor("out", (BATCH, CTX, D), F32, kind="ExternalOutput").ap()
    tokens_dram = nc.dram_tensor("tokens_dram", (TOKENS, D), F32).ap()
    pairs_dram = nc.dram_tensor("pairs_dram", (PAIRS, D), F32).ap()
    build_program(nc, *args, out, tokens_dram, pairs_dram)
    r = run_bass_kernel_spmd(nc, [arrays], core_ids=[0])
    return r.results[0]["out"]
```

```python
from contextlib import ExitStack

import numpy as np

import concourse.bass as bass
from concourse import mybir

F32 = mybir.dt.float32
BF16 = mybir.dt.bfloat16
I32 = mybir.dt.int32
U16 = mybir.dt.uint16
U32 = mybir.dt.uint32
ALU = mybir.AluOpType
ACT = mybir.ActivationFunctionType
AX = mybir.AxisListType

P = 128
BATCH, CTX, D = 8, 512, 256
HEADS, HD = 16, 16
ROWS = 16
TOKENS = BATCH * CTX
TT = TOKENS // P
REST = (CTX - ROWS) // ROWS
E, I, TOPK = 32, 128, 4
GROUPS, GSIZE, TOPG = 4, 8, 2
PAIRS = TOKENS * TOPK
KC = D // P
EPS = 1e-5
MASKED = -1e30
ITERATIONS = 3
DIFF_LIMIT, DIFF_FACTOR = 0.01, 0.1
ROUTE_SCALE = 2.5
SLOT_TILES = 160
assert (PAIRS + E * (P - 1)) // P <= SLOT_TILES
GROUPS_OF_TILES = [(1, 9), (9, 17), (17, 25), (25, 32)]
POOL_GROUPS = [2, 3]
OUT_GROUPS = [(0, 1), (1, 9), (9, 17), (17, 25), (25, 28), (28, 30), (30, 32)]
LOADS = 8
CODE = 0x800
HOTS = 8
HOTBUFS = 4
CODED = 5
N_MASKS = 20
N_CONSTS = 26

STEPS = 12
WEIGHT_PARTS = 2 * TOPK + 2
SHARED_AT = [10, 11]
EXPERTS_AT = [s for s in range(STEPS) if s not in SHARED_AT]
NEXP = len(EXPERTS_AT)
BODIES = SLOT_TILES // NEXP
FIXED = BODIES - 2
LATE = TT - FIXED
SUMS_FIRST = 8
LATE_NAMED = 5
RING = 5
LAG = 3
EIDS = 12
assert LATE % 2 == 0 and NEXP == 2 * RING

ATT_STEPS = 4 + 6 * ITERATIONS - 1 + 2
LOGIT_STEPS = [4 + 6 * it + 2 for it in range(ITERATIONS)]
TILES_AT = [0, 0, 8, 8, 8, 7] + [0] * (ATT_STEPS - 6)
ROUTED_AT = 5
assert sum(TILES_AT) == TT - 1 and TILES_AT[ROUTED_AT]
ROOTS = [1, 1, GROUPS_OF_TILES[0], GROUPS_OF_TILES[1], HEADS, GROUPS_OF_TILES[2], GROUPS_OF_TILES[3],
         *[HEADS] * ITERATIONS, 1]

ROW_PARTS = [("lna", D), ("lnb", D), ("ob", D), ("lqb", HD), ("lkb", HD), ("lvb", HD), ("lnc", HD),
             ("lnd", HD), ("bias", E)]
ROW_AT = {}
for _name, _n in ROW_PARTS:
    ROW_AT[_name] = (sum(n for _, n in ROW_PARTS[:len(ROW_AT)]), _n)
ROW_LEN = sum(n for _, n in ROW_PARTS)


def wait_count(eng, sem, body, per_body, offset, loop_from=1):
    if isinstance(body, int):
        count = body * per_body + offset
        if per_body == STEPS:
            count -= max(0, body - FIXED) * (STEPS - NEXP)
        if count > 0:
            eng.wait_ge(sem, count)
    else:
        assert loop_from * per_body + offset > 0
        eng.wait_ge(sem, body * per_body + offset)


def used_parts(eng, slots, part):
    for body in range(FIXED, BODIES):
        with eng.If(slots > body * NEXP * P):
            part(body)


def late_loop(eng, parts, first):
    def turn_of(turn):
        for i in range(2):
            for part, offset in parts:
                if not isinstance(turn, int) or 0 <= 2 * turn + i + offset < LATE:
                    part(turn, i + offset)

    first()
    turn_of(0)
    turn_of(1)
    with eng.Fori(2, LATE // 2 - 1) as turn:
        turn_of(turn)
    for turn in range(LATE // 2 - 1, LATE // 2 + 2):
        turn_of(turn)


def build_program(nc, x, qkvo, gate_up, down, sh_gate_up, sh_down, router, rows, cols, local, out,
                  tokens_dram, pairs_dram):
    ctx = ExitStack()
    with ctx:
        def sb(name, shape, dt=F32):
            return ctx.enter_context(nc.sbuf_tensor(name, shape, dt))

        def sem(name):
            return ctx.enter_context(nc.semaphore(name))

        two_banks = [ctx.enter_context(nc.psum_tensor(f"two_banks{i}", [P, 2, 512], F32)) for i in range(4)]
        bank = [two_banks[i // 2][:, i % 2, :] for i in range(8)]
        gu_w = sb("gu_w", [P, E, KC, 2 * I])
        dn_w = sb("dn_w", [P, E, D])
        sgu_w = sb("sgu_w", [P, 2, KC, 2 * I])
        sdn_w = sb("sdn_w", [P, 2, D])
        x_sb = sb("x_sb", [P, TT, D])
        xn = sb("xn", [P, 4, D])
        row_sb = sb("row_sb", [P, ROW_LEN])
        col_sb = sb("col_sb", [P, 4])
        rt_w = sb("rt_w", [P, KC, E])
        ident = sb("ident", [P, P])
        stats = sb("stats", [P, TT, 6])
        mv = sb("mv", [P, TT, 2])
        var_e = sb("var_e", [P, TT])
        rstd = sb("rstd", [P, TT])
        half = sb("half", [P, TT])
        shift = sb("shift", [P, TT])
        xnT = sb("xnT", [P, 2, KC, P])
        wts = sb("wts", [P, TT, TOPK])
        pair_at = sb("pair_at", [P, SLOT_TILES], I32)
        tok_at = sb("tok_at", [P, SLOT_TILES], I32)
        used = sb("used", [1, 4], I32)
        eids = sb("eids", [1, BODIES, EIDS], I32)

        def row(name):
            a, n = ROW_AT[name]
            return row_sb[:, a:a + n]

        routing = sb("routing", [P, 7 * TT * E])
        scratch = routing[:, 0:4 * TT * E]
        work = routing[:, 4 * TT * E:].rearrange("p (m n) -> p m n", m=3)
        def piece(k, n=1):
            return scratch[:, k * TT * E:(k + n) * TT * E]
        sc3 = piece(0).rearrange("p (t e) -> p t e", e=E)
        sel = piece(1)
        hot_b = piece(2, 2).bitcast(BF16).rearrange("p (k t e) -> p k t e", k=TOPK, e=E)
        load4 = gu_w[:, 0:2 * LOADS].rearrange("p (s e) c i -> p s (e c i)", s=LOADS
                                               ).rearrange("p s (k d) -> p s k d", k=TOPK)
        small = sb("small", [P, 7, TT * GROUPS])
        idxf = sb("idxf", [P, TT, TOPK])
        e_row = sb("e_row", [P, 8, E])
        code_u = sb("code_u", [P, TT * TOPK], U16)
        lower = sb("lower", [P, P], BF16)
        ones_b = sb("ones_b", [P, P], BF16)
        iota_b = sb("iota_b", [P, SLOT_TILES, HOTS], BF16)
        iota_e = sb("iota_e", [P, E])
        iota_g = sb("iota_g", [P, GROUPS])
        iota_p = sb("iota_p", [P, 2])
        ecol = sb("ecol", [P, 4])

        loopb = sb("loopb", [P, 22 * D])
        def lb(k, n=1):
            return loopb[:, k * D:(k + n) * D]
        xg = lb(0, RING).rearrange("p (r d) -> p r d", d=D)
        more = work[:, 1:3, :].rearrange("p a n -> p (a n)")
        yb = [lb(5 + k) for k in range(RING)] + [more[:, k * D:(k + 1) * D] for k in range(NEXP - RING)]
        xs = lb(10, 2).rearrange("p (r d) -> p r d", d=D)
        xT = lb(12, 2).rearrange("p (r c t) -> p r c t", r=2, c=KC)
        silu = lb(14).rearrange("p (r i) -> p r i", r=2)
        hid = lb(15).rearrange("p (r i) -> p r i", r=2)
        hidT = lb(16).rearrange("p (r i) -> p r i", r=2)
        assert LATE * D <= 5 * TT * E
        late_x = routing[:, 0:LATE * D].rearrange("p (t d) -> p t d", t=LATE)
        late_silu = lb(0, 2).rearrange("p (r n) -> p r n", r=2)
        late_up = lb(2, 2).rearrange("p (r n) -> p r n", r=2)
        late_h = lb(17, 2).rearrange("p (r n) -> p r n", r=2)
        late_hidT = lb(19, 2).rearrange("p (r m t) -> p r m t", r=2, m=2)
        late_out = [lb(4), lb(21)]
        hotr = [area[:, k * D * 2:(k + 1) * D * 2].bitcast(BF16).rearrange("p (r h) -> p r h", h=HOTS)
                for area in (lb(0, 4), lb(17, 4)) for k in range(2)]
        hotj = [area[:, k * SLOT_TILES * 4:(k + 1) * SLOT_TILES * 4].bitcast(BF16)
                .rearrange("p (j h) -> p j h", h=HOTS)
                for area in (lb(11, 5), work[:, 0:2, :].rearrange("p a n -> p (a n)")) for k in range(2)]
        resets = lb(19, 2).bitcast(BF16)
        code_f = lb(16)[:, 0:TT * TOPK]
        top8 = dn_w[:, 18, :].rearrange("p (t j) -> p t j", j=8)
        idx8 = dn_w[:, 19, :].bitcast(U32).rearrange("p (t j) -> p t j", j=8)
        slots = lb(7, 4)
        slot_f = slots[:, 0:TT * TOPK].rearrange("p (t k) -> p t k", k=TOPK)
        slot_i = slots[:, P:4 * P].bitcast(I32).rearrange("p (m n) -> p m n", m=3)
        slot_b = slots[:, 4 * P:5 * P].bitcast(BF16).rearrange("p (m n) -> p m n", m=2)
        table_out = sb("table_out", [P, 1])
        stage_g = sb("stage_g", [P, NEXP], I32)
        stage_s = sb("stage_s", [P, NEXP], I32)

        att_mem = dn_w[:, 0:16, :].rearrange("p e d -> p (e d)")
        att_mem_b = dn_w[:, 16:18, :].rearrange("p e d -> p (e d)")
        w4 = att_mem[:, 0:8 * D].rearrange("p (m c n) -> p m c n", m=4, c=KC)
        head_mask = sb("head_mask", [P, HEADS // 2])
        quad_mask = sb("quad_mask", [P, 4])
        batch_mask = sb("batch_mask", [P, 2, ROWS])
        spread = att_mem_b[:, 0:4 * P].rearrange("p (g a t) -> p g a t", g=4, a=4)
        local_sb = sb("local_sb", [P, 3, HD])
        blockw = lb(0, 3).rearrange("p (m h d) -> p m h d", m=6, d=HD)[:, 0:3]
        at_a, at_b, at_c = lb(3), lb(4), lb(5)
        at_d = lb(6)
        inT = lb(7, 2).rearrange("p (m c t) -> p m c t", m=2, c=KC)
        q_cur = lb(9).rearrange("p (c t) -> p c t", c=KC)
        at_T = lb(10).rearrange("p (c t) -> p c t", c=KC)
        att_out = lb(11, 3).rearrange("p (i n) -> p i n", i=3)
        prob = lb(14, 2)
        probT = lb(16, 2).rearrange("p (j t) -> p j t", j=4)
        keys = att_mem[:, 8 * D:16 * D].rearrange("p (c h t) -> p c h t", c=KC, t=P)
        vals = lb(18, 4).rearrange("p (g n) -> p g n", g=4)
        hst = sb("hst", [P, 6, HEADS])
        dsum = sb("dsum", [P, 4])
        stop_i = sb("stop_i", [P, 1], I32)
        ones_f = lb(0, 3)[:, 4 * P:5 * P]

        att_x_in = sem("att_x_in")
        x_in = [sem(f"x_in{g}") for g in range(len(GROUPS_OF_TILES))]
        small_in = sem("small_in")
        attw_in = sem("attw_in")
        expert_w_in = sem("expert_w_in")
        consts_made = sem("consts_made")
        bias_added = sem("bias_added")
        var_ready = sem("var_ready")
        rstd_ready = sem("rstd_ready")
        norm_ready = sem("norm_ready")
        xn_ready = sem("xn_ready")
        xn_turned = sem("xn_turned")
        xnT_ready = sem("xnT_ready")
        logits_done = sem("logits_done")
        tok_stored = [sem(f"tok_stored{s}") for s in range(4)]
        att_ready = sem("att_ready")
        att_pe = sem("att_pe")
        att_exp = sem("att_exp")
        diff_ready = sem("diff_ready")
        diff_summed = sem("diff_summed")
        dve_seq = sem("dve_seq")
        pool_seq = sem("pool_seq")
        scores_done = sem("scores_done")
        hot_ready = sem("hot_ready")
        counts_done = sem("counts_done")
        places_ready = sem("places_ready")
        places_hot = sem("places_hot")
        pairs_hot = sem("pairs_hot")
        pairs_used = sem("pairs_used")
        rows_hot = sem("rows_hot")
        pairs_coded = sem("pairs_coded")
        codes_kept = sem("codes_kept")
        ecol_ready = sem("ecol_ready")
        eid_turned = sem("eid_turned")
        tables_ready = sem("tables_ready")
        gathered = [sem(f"gathered{k}") for k in range(RING)]
        scattered = [sem(f"scattered{k}") for k in range(NEXP)]
        shared_in = sem("shared_in")
        tokens_staged = sem("tokens_staged")
        pairs_staged = sem("pairs_staged")
        x_turned = sem("x_turned")
        xT_ready = sem("xT_ready")
        gu_done = sem("gu_done")
        silu_done = sem("silu_done")
        hid_ready = sem("hid_ready")
        hid_turned = sem("hid_turned")
        hidT_ready = sem("hidT_ready")
        y_done = sem("y_done")
        y_ready = sem("y_ready")
        experts_done = sem("experts_done")
        parts_scattered = sem("parts_scattered")
        weights_made = sem("weights_made")
        late_in = sem("late_in")
        late_ready = sem("late_ready")
        late_turned = sem("late_turned")
        late_xT = sem("late_xT")
        late_gu = sem("late_gu")
        late_gated = sem("late_gated")
        late_hid = sem("late_hid")
        late_hturned = sem("late_hturned")
        late_hT = sem("late_hT")
        late_down = sem("late_down")
        late_y = sem("late_y")
        late_added = sem("late_added")
        pairs_in = [sem(f"pairs_in{s}") for s in range(LOADS)]
        added = sem("added")
        tile_summed = sem("tile_summed")
        stored = sem("stored")

        turn_ps = [bank[0][:, 0:D].rearrange("p (c t) -> p c t", c=KC),
                   bank[1][:, 0:D].rearrange("p (c t) -> p c t", c=KC)]
        diff_ps = bank[1][:, D:D + 1]
        logit_ps = [bank[2], bank[3]]
        att_ps = bank[4:8]

        x_rest = x[:, ROWS:CTX, :].rearrange("b (q j) d -> b q (j d)", j=REST)
        out_rest = out[:, ROWS:CTX, :].rearrange("b (q j) d -> b q (j d)", j=REST)
        tok_tiles = tokens_dram.rearrange("(p t) d -> p t d", t=TT)
        pair_tiles = pairs_dram.rearrange("(p t k) d -> p t (k d)", t=TT, k=TOPK)
        tile_order = list(range(1, TT)) + [0]

        block = ctx.enter_context(nc.Block())

        @block.sync
        def _(sp):
            sp.dma_start(x_sb[:, 0, :], x[:, 0:ROWS, :]).then_inc(att_x_in, 16)
            sp.dma_start(row_sb[:, :], rows.to_broadcast([P, ROW_LEN])).then_inc(small_in, 16)
            sp.dma_start(rt_w[:, :, :], router).then_inc(small_in, 16)
            for g, (a, b) in enumerate(GROUPS_OF_TILES):
                sp.dma_start(x_sb[:, a:b, :].rearrange("p j d -> p (j d)"),
                             x_rest[:, :, (a - 1) * D:(b - 1) * D]).then_inc(x_in[g], 16)
            for n, t in enumerate(tile_order):
                if n == TT - 1:
                    for m in range(4):
                        e = slice(8 * m, 8 * m + 8)
                        sp.dma_start(gu_w[:, e], gate_up[:, e]).then_inc(expert_w_in, 16)
                    sp.dma_start(sgu_w[:, :, :, :], sh_gate_up).then_inc(expert_w_in, 16)
                    sp.dma_start(sdn_w[:, :, :], sh_down).then_inc(expert_w_in, 16)
                sp.wait_ge(xn_ready, n + 1)
                sp.dma_start(tok_tiles[:, t, :], xn[:, n % 4, :]).then_inc(tok_stored[n % 4], 16)
            sp.wait_ge(hot_ready, 2)
            for m in range(4):
                e = slice(8 * m, 8 * m + 8)
                sp.dma_start(dn_w[:, e], down[:, e]).then_inc(expert_w_in, 16)
            for s in range(4):
                sp.wait_ge(tok_stored[s], 16 * (TT // 4))
            sp.wait_ge(tables_ready, 2)
            sp.dma_start(xs[:, 0, :], tok_tiles[:, 0, :]).then_inc(shared_in, 16)
            sp.wait_ge(weights_made, 1)
            sp.dma_start(late_x[:, :, :].rearrange("p t d -> p (t d)"),
                         tok_tiles[:, TT - LATE:TT, :].rearrange("p t d -> p (t d)")).then_inc(late_in, 16)
            with sp.Fori(1, FIXED) as body:
                sp.wait_ge(x_turned, body * STEPS)
                sp.dma_start(xs[:, 0, :], tok_tiles[:, bass.ds(body, 1), :].rearrange("p a d -> p (a d)")
                             ).then_inc(shared_in, 16)
            for k in range(NEXP):
                sp.wait_ge(scattered[k], 16 * FIXED)
            sp.wait_ge(parts_scattered, 1)

            def store(a, b):
                if b == 1:
                    sp.dma_start(out[:, 0:ROWS, :], x_sb[:, 0, :]).then_inc(stored, 16)
                else:
                    sp.dma_start(out_rest[:, :, (a - 1) * D:(b - 1) * D],
                                 x_sb[:, a:b, :].rearrange("p j d -> p (j d)")).then_inc(stored, 16)

            for t in range(TT):
                if t >= LOADS:
                    sp.wait_ge(tile_summed, t - LOADS + 1)
                sp.dma_start(load4[:, t % LOADS].rearrange("p k d -> p (k d)"), pair_tiles[:, t, :]
                             ).then_inc(pairs_in[t % LOADS], 16)
                for a, b in OUT_GROUPS:
                    if b == t - LOADS + 1:
                        store(a, b)
            for a, b in OUT_GROUPS:
                if b > TT - LOADS:
                    sp.wait_ge(tile_summed, b)
                    store(a, b)
            sp.wait_ge(stored, 16 * len(OUT_GROUPS))

        @block.gpsimd
        def _(pool):
            made = [0]

            def const(ins):
                made[0] += 1
                ins.then_inc(consts_made, 1)
                pool.wait_ge(consts_made, made[0])

            const(pool.memset(half[:, :], -0.5))
            const(pool.memset(ident[:, :], 0.0))
            const(pool.affine_select(ident[:, :], ident[:, :], [[-1, P]], ALU.not_equal, 1.0, base=0,
                                     channel_multiplier=1))
            rstds = [0]

            def inverse_root(what):
                rstds[0] += 1
                pool.wait_ge(var_ready, rstds[0])
                if what == HEADS:
                    pool.tensor_tensor(hst[:, 3, :], hst[:, 2, :], half[:, 0:HEADS], ALU.pow).then_inc(rstd_ready, 1)
                else:
                    a, b = (0, 1) if what == 1 else what
                    pool.tensor_tensor(rstd[:, a:b], var_e[:, a:b], half[:, a:b], ALU.pow).then_inc(rstd_ready, 1)

            const(pool.memset(ones_f[:, :], 1.0))
            const(pool.memset(ones_b[:, :], 1.0))
            for mask, n, width in ((head_mask, HEADS // 2, HD), (quad_mask, 4, 32)):
                const(pool.memset(mask[:, :], 1.0))
                const(pool.affine_select(mask[:, :], mask[:, :], [[-width, n]], ALU.is_ge, 0.0, base=0,
                                         channel_multiplier=1))
                const(pool.affine_select(mask[:, :], mask[:, :], [[width, n]], ALU.is_ge, 0.0, base=width - 1,
                                         channel_multiplier=-1))
            inverse_root(ROOTS[0])
            const(pool.memset(batch_mask[:, :, :], 0.0))
            for g in range(4):
                q = batch_mask[32 * g:32 * g + 32]
                const(pool.affine_select(q[:, 0, :], q[:, 0, :], [[0, ROWS]], ALU.is_ge, MASKED, base=ROWS - 1,
                                         channel_multiplier=-1))
                const(pool.affine_select(q[:, 1, :], q[:, 1, :], [[0, ROWS]], ALU.is_ge, MASKED, base=-ROWS,
                                         channel_multiplier=1))
            assert made[0] == N_MASKS
            inverse_root(ROOTS[1])
            const(pool.iota(iota_b[:, :, :], [[1, SLOT_TILES], [0, HOTS]], base=0, channel_multiplier=0,
                            allow_small_or_imprecise_dtypes=True))
            const(pool.iota(iota_e[:, :], [[1, E]], base=0, channel_multiplier=0,
                            allow_small_or_imprecise_dtypes=True))
            const(pool.iota(iota_g[:, :], [[1, GROUPS]], base=0, channel_multiplier=0,
                            allow_small_or_imprecise_dtypes=True))
            const(pool.iota(iota_p[:, :], [[P * P, 2]], base=0, channel_multiplier=P,
                            allow_small_or_imprecise_dtypes=True))
            const(pool.iota(code_u[:, :], [[1, TT * TOPK]], base=CODE, channel_multiplier=TT * TOPK,
                            allow_small_or_imprecise_dtypes=True))
            const(pool.affine_select(lower[:, :], ones_b[:, :], [[1, P]], ALU.is_gt, 0.0, base=0,
                                     channel_multiplier=-1))
            assert made[0] == N_CONSTS
            for what in ROOTS[2:]:
                inverse_root(what)
                if what in GROUPS_OF_TILES[0:2]:
                    g = POOL_GROUPS[GROUPS_OF_TILES.index(what)]
                    a, b = GROUPS_OF_TILES[g]
                    pool.wait_ge(small_in, 32)
                    pool.wait_ge(x_in[g], 16)
                    pool.tensor_tensor(x_sb[:, a:b, :], x_sb[:, a:b, :],
                                       row("ob").unsqueeze(1).to_broadcast([P, b - a, D]),
                                       ALU.add).then_inc(bias_added, 1)

            pool.wait_ge(places_ready, 1)
            for k in range(TOPK // 2, TOPK):
                pool.tensor_tensor(work[:, k - 1, :], hot_b[:, k].rearrange("p t e -> p (t e)"), sel, ALU.mult
                                   ).then_inc(places_hot, 1)

            for s in range(4):
                pool.wait_ge(tok_stored[s], 16 * (TT // 4))
            pool.wait_ge(tables_ready, 2)

            def gather(k, index):
                pool.indirect_dma_start(out=xg[:, k, :], out_offset=None, in_=tokens_dram,
                                        in_offset=bass.IndirectOffsetOnAxis(ap=index, axis=0)
                                        ).then_inc(gathered[k], 16)

            for k in range(RING):
                gather(k, tok_at[:, k:k + 1])

            def wait_before_dma(sem_, body, per_body, offset):
                wait_count(pool, sem_, body, per_body, offset)
                if not isinstance(body, int):
                    pool.sem_inc(pool_seq, 1)

            def scatter_rows(u, index):
                pool.indirect_dma_start(out=pairs_dram, out_offset=bass.IndirectOffsetOnAxis(ap=index, axis=0),
                                        in_=yb[u], in_offset=None, bounds_check=PAIRS - 1,
                                        oob_is_err=False).then_inc(scattered[u], 16)

            def scatter(body, u):
                back, column = divmod(u, NEXP)
                if column % RING == 0:
                    wait_before_dma(pairs_staged, body, 2, 2 * back + column // RING + 1)
                wait_before_dma(y_ready, body, STEPS, back * STEPS + EXPERTS_AT[column] + 1)
                scatter_rows(column, stage_s[:, column:column + 1])

            def body_of(body, first, last):
                for u, step in enumerate(EXPERTS_AT):
                    k = u % RING
                    if k == 0:
                        wait_before_dma(tokens_staged, body, 2, 1 + u // RING)
                    if not (last and u >= NEXP - RING):
                        wait_before_dma(x_turned, body, STEPS, step + 1)
                        gather(k, stage_g[:, u:u + 1])
                    if not (first and u < LAG):
                        scatter(body, u - LAG)

            body_of(0, True, False)
            with pool.Fori(1, FIXED - 1) as body:
                body_of(body, False, False)
            slots = pool.value_load(used[0:1, 0:1], min_val=0, max_val=SLOT_TILES * P)
            body_of(FIXED - 1, False, True)
            for u in range(NEXP - LAG, NEXP):
                scatter(FIXED - 1, u)

            def part(body):
                first = body * NEXP
                wait_count(pool, x_turned, body, STEPS, 0)
                for k in range(RING):
                    gather(k, tok_at[:, first + k:first + k + 1])
                for u in range(NEXP + LAG):
                    if u + RING < NEXP:
                        wait_count(pool, x_turned, body, STEPS, u + 1)
                        gather(u % RING, tok_at[:, first + u + RING:first + u + RING + 1])
                    if u >= LAG:
                        wait_count(pool, y_ready, body, STEPS, u - LAG + 1)
                        scatter_rows(u - LAG, pair_at[:, first + u - LAG:first + u - LAG + 1])
                for k in range(NEXP):
                    pool.wait_ge(scattered[k], 16 * (body + 1))

            used_parts(pool, slots, part)
            pool.sem_inc(parts_scattered, 1)

            def late_input(turn, i):
                if isinstance(turn, int) and 2 * turn + i < LATE_NAMED:
                    return
                wait_count(pool, late_turned, turn, 2, i - 1, 2)
                src = late_x[:, 2 * turn + i, :] if isinstance(turn, int) else (
                    late_x[:, bass.ds(turn * 2 + i, 1), :].rearrange("p a d -> p (a d)"))
                pool.tensor_copy(xs[:, i % 2, :], src).then_inc(late_ready, 1)

            def late_gating(turn, i):
                wait_count(pool, late_gated, turn, 2, i + 1, 2)
                wait_count(pool, late_hturned, turn, 2, i - 1, 2)
                pool.tensor_tensor(late_h[:, i % 2], late_silu[:, i % 2], late_up[:, i % 2], ALU.mult
                                   ).then_inc(late_hid, 1)

            def late_add(turn, i):
                wait_count(pool, late_y, turn, 2, i + 1, 2)
                if isinstance(turn, int):
                    xt = x_sb[:, TT - LATE + 2 * turn + i, :]
                else:
                    xt = x_sb[:, bass.ds(turn * 2 + (TT - LATE + i), 1), :].rearrange("p a d -> p (a d)")
                pool.tensor_tensor(xt, xt, late_out[i % 2], ALU.add).then_inc(late_added, 1)

            pool.wait_ge(late_in, 16)
            pool.wait_ge(experts_done, 3)
            late_loop(pool, [(late_input, 2), (late_gating, 0), (late_add, -3)], first=lambda: None)

        @block.scalar
        def _(act):
            act.dma_start(w4[:, :, :, :], qkvo).then_inc(attw_in, 16)
            act.dma_start(col_sb[:, :], cols).then_inc(attw_in, 16)
            act.dma_start(local_sb[:, :, :], local).then_inc(attw_in, 16)

            def normalise(n, t):
                if n >= 4:
                    act.wait_ge(tok_stored[n % 4], 16 * (n // 4))
                    act.wait_ge(xn_turned, n - 3)
                act.activation(xn[:, n % 4, :], x_sb[:, t, :], ACT.Identity, bias=shift[:, t:t + 1],
                               scale=rstd[:, t:t + 1]).then_inc(xn_ready, 1)

            def keep_turned(n):
                act.wait_ge(xn_turned, n + 1)
                if n >= 2:
                    act.wait_ge(logits_done, n - 1)
                act.activation(xnT[:, n % 2], turn_ps[n % 2], ACT.Copy).then_inc(xnT_ready, 1)

            def scores(a, b):
                for h in range(2):
                    lo, hi = max(a, 16 * h), min(b, 16 * h + 16)
                    if lo < hi:
                        act.activation(sc3[:, lo:hi, :], logit_ps[h][:, (lo - 16 * h) * E:(hi - 16 * h) * E]
                                       .rearrange("p (t e) -> p t e", e=E), ACT.Sigmoid).then_inc(scores_done, 1)

            def load_table(function):
                act.activation(table_out[:, :], half[:, 0:1], function)

            act.wait_ge(consts_made, 1)
            n = exps = 0
            for step, tiles in enumerate(TILES_AT):
                for _ in range(tiles):
                    t = tile_order[n]
                    for g, (a, b) in enumerate(GROUPS_OF_TILES):
                        if t == a:
                            act.wait_ge(norm_ready, g + 1)
                    normalise(n, t)
                    if n:
                        keep_turned(n - 1)
                    n += 1
                if step == ROUTED_AT:
                    keep_turned(n - 1)
                    act.wait_ge(logits_done, TT - 1)
                    scores(1, TT)
                    load_table(ACT.Exp)
                if step in LOGIT_STEPS:
                    act.wait_ge(att_exp, 2 * exps + 1)
                    act.activation(prob, prob, ACT.Exp, scale=float(HD) ** -0.5).then_inc(att_exp, 1)
                    exps += 1
                if step + 1 in LOGIT_STEPS:
                    act.wait_ge(att_pe, step + 1)
                    act.activation(at_T[:, :, :].rearrange("p c t -> p (c t)"), att_ps[1][:, 0:D], ACT.Copy
                                   ).then_inc(att_ready, 1)
                if step - 1 in LOGIT_STEPS:
                    act.wait_ge(att_pe, step + 1)
                    act.activation(probT[:, :, :].rearrange("p j t -> p (j t)"), att_ps[3][:, :], ACT.Copy
                                   ).then_inc(att_ready, 1)
            load_table(ACT.Sigmoid)
            act.wait_ge(norm_ready, len(GROUPS_OF_TILES) + 1)
            normalise(n, 0)
            keep_turned(n)
            act.wait_ge(logits_done, TT)
            scores(0, 1)
            load_table(ACT.Silu)
            act.activation(code_f[:, :], code_u[:, :].bitcast(BF16), ACT.Copy).then_inc(codes_kept, 1)
            act.wait_ge(codes_kept, 1)

            def code_pairs(i):
                for b in range(HOTBUFS):
                    act.wait_ge(rows_hot, i * HOTBUFS + b + 1)
                    for h in range(CODED):
                        if isinstance(i, int):
                            scale = code_f[:, b * HOTS + h:b * HOTS + h + 1]
                        else:
                            scale = code_f[:, bass.ds(i * (HOTBUFS * HOTS) + (b * HOTS + h), 1)]
                        ins = act.activation(hotr[b][:, :, h], hotr[b][:, :, h], ACT.Copy, scale=scale)
                    ins.then_inc(pairs_coded, 1)

            code_pairs(0)
            with act.Fori(1, TT * TOPK // (HOTBUFS * HOTS)) as i:
                code_pairs(i)

            def keep_x(body, step):
                wait_count(act, x_turned, body, STEPS, step + 1)
                wait_count(act, gu_done, body, STEPS, step - 1)
                act.activation(xT[:, step % 2], turn_ps[step % 2], ACT.Copy).then_inc(xT_ready, 1)

            def gate(body, step):
                wait_count(act, gu_done, body, STEPS, step + 1)
                wait_count(act, hid_ready, body, STEPS, step - 1)
                act.activation(silu[:, step % 2], bank[2 + step % 2][:, 0:I], ACT.Silu).then_inc(silu_done, 1)

            def stage_tokens(body, h):
                for k in range(RING):
                    wait_count(act, gathered[k], body, 16 * 2, 16 * h if not isinstance(body, int) or body else 0)
                at, first = h * RING, body * NEXP + h * RING
                act.activation(stage_g[:, at:at + RING], tok_at[:, bass.ds(first + RING, RING)], ACT.Copy
                               ).then_inc(tokens_staged, 1)

            def stage_pairs(body, h):
                for k in range(RING):
                    wait_count(act, scattered[h * RING + k], body, 16, 0)
                at, first = h * RING, body * NEXP + h * RING
                act.activation(stage_s[:, at:at + RING], pair_at[:, bass.ds(first, RING)], ACT.Copy
                               ).then_inc(pairs_staged, 1)

            def part(body):
                keep_x(body, 0)
                keep_x(body, 1)
                for step in range(NEXP):
                    gate(body, step)
                    if step + 2 < NEXP:
                        keep_x(body, step + 2)
                through(body)

            def through(body):
                for written in (xT_ready, silu_done):
                    wait_count(act, written, body + 1, STEPS, 0)

            def body_of(body, last):
                for step in range(STEPS):
                    gate(body, step)
                    if not (last and step + 2 >= STEPS):
                        keep_x(body, step + 2)
                    if step in (0, RING):
                        stage_pairs(body, step // RING)
                    if step == RING - 3 and not (isinstance(body, int) and body == 0):
                        stage_tokens(body, 1)
                    if step == NEXP - 3 and not last:
                        stage_tokens(body + 1, 0)

            act.wait_ge(tables_ready, 2)
            stage_tokens(0, 0)
            stage_tokens(0, 1)
            keep_x(0, 0)
            keep_x(0, 1)
            body_of(0, False)
            with act.Fori(1, FIXED - 1) as body:
                body_of(body, False)
            slots = act.value_load(used[0:1, 0:1], min_val=0, max_val=SLOT_TILES * P)
            body_of(FIXED - 1, True)
            through(FIXED - 1)
            used_parts(act, slots, part)
            act.sem_inc(experts_done, 1)

            def late_keep_x(turn, i):
                wait_count(act, late_turned, turn, 2, i + 1, 2)
                wait_count(act, late_gu, turn, 2, i - 1, 2)
                act.activation(xT[:, i % 2], turn_ps[i % 2], ACT.Copy).then_inc(late_xT, 1)

            def late_gate(turn, i):
                wait_count(act, late_gu, turn, 2, i + 1, 2)
                wait_count(act, late_hid, turn, 2, i - 1, 2)
                gu = bank[2 + i % 2][:, :].rearrange("p (m k i) -> p m k i", m=2, k=2)
                act.activation(late_silu[:, i % 2].rearrange("p (m i) -> p m i", m=2), gu[:, :, 0, :], ACT.Silu)
                act.activation(late_up[:, i % 2].rearrange("p (m i) -> p m i", m=2), gu[:, :, 1, :], ACT.Copy
                               ).then_inc(late_gated, 1)

            def late_keep_hid(turn, i):
                wait_count(act, late_hturned, turn, 2, i + 1, 2)
                wait_count(act, late_down, turn, 2, i - 1, 2)
                act.activation(late_hidT[:, i % 2].rearrange("p m t -> p (m t)"), bank[4 + i % 2][:, 0:2 * P], ACT.Copy
                               ).then_inc(late_hT, 1)

            def late_keep_y(turn, i):
                wait_count(act, late_down, turn, 2, i + 1, 2)
                wait_count(act, late_added, turn, 2, i - 1, 2)
                act.activation(late_out[i % 2], bank[6 + i % 2][:, 0:D], ACT.Copy).then_inc(late_y, 1)

            act.wait_ge(experts_done, 3)
            late_loop(act, [(late_gate, 0), (late_keep_x, 1), (late_keep_hid, -1), (late_keep_y, -2)],
                      first=lambda: late_keep_x(0, 0))

        @block.tensor
        def _(pe):
            pe.wait_ge(consts_made, 3)
            pe.wait_ge(small_in, 32)

            def turn(n):
                pe.wait_ge(xn_ready, n + 1)
                if n >= 2:
                    pe.wait_ge(xnT_ready, n - 1)
                for c in range(KC):
                    ins = pe.transpose(turn_ps[n % 2][:, c, :], xn[:, n % 4, c * P:(c + 1) * P], ident[:, :])
                ins.then_inc(xn_turned, 1)

            def logits(n, t):
                pe.wait_ge(xnT_ready, n + 1)
                o = logit_ps[t // 16][:, (t % 16) * E:(t % 16 + 1) * E]
                for c in range(KC):
                    ins = pe.matmul(o, xnT[:, n % 2, c, :], rt_w[:, c, :], start=(c == 0), stop=(c == KC - 1),
                                    skip_group_check=True)
                ins.then_inc(logits_done, 1)

            step, turned = [0], [0]

            def after_dve():
                for _ in range(TILES_AT[step[0]]):
                    n = turned[0]
                    turn(n)
                    if n:
                        logits(n - 1, tile_order[n - 1])
                    turned[0] += 1
                if step[0] == ROUTED_AT:
                    logits(TT - 2, tile_order[TT - 2])
                step[0] += 1
                pe.wait_ge(att_ready, step[0])

            after_dve()
            pe.wait_ge(attw_in, 48)
            for m, src in enumerate((at_a, at_b)):
                for c in range(KC):
                    ins = pe.transpose(att_ps[0][:, (m * KC + c) * P:(m * KC + c + 1) * P],
                                       src[:, c * P:(c + 1) * P], ident[:, :])
            ins.then_inc(att_pe, 1)
            after_dve()
            for m, src in ((0, 0), (1, 1), (2, 1)):
                for c in range(KC):
                    for k in range(KC):
                        ins = pe.matmul(att_ps[1 + m][:, c * P:(c + 1) * P], w4[:, m, k, c * P:(c + 1) * P],
                                        inT[:, src, k, :], start=(k == 0), stop=(k == KC - 1))
            ins.then_inc(att_pe, 1)
            after_dve()
            for m, src in ((0, at_T), (1, at_d.rearrange("p (c t) -> p c t", c=KC))):
                for c in range(KC):
                    ins = pe.matmul(att_ps[m][:, c * P:(c + 1) * P], src[:, c, :],
                                    blockw[:, 1 + m].rearrange("p h d -> p (h d)"), start=True, stop=True)
            ins.then_inc(att_pe, 1)
            after_dve()
            for c in range(KC):
                ins = pe.transpose(att_ps[2][:, c * P:(c + 1) * P], at_a[:, c * P:(c + 1) * P], ident[:, :])
            for g in range(4):
                ins = pe.matmul(att_ps[(0, 3)[g // 2]][:, (g % 2) * D:(g % 2 + 1) * D],
                                spread[:, g].rearrange("p a t -> p (a t)"), at_b, start=True, stop=True)
            ins.then_inc(att_pe, 1)
            for it in range(ITERATIONS):
                after_dve()
                for c in range(KC):
                    ins = pe.matmul(att_ps[0][:, c * P:(c + 1) * P], q_cur[:, c, :],
                                    blockw[:, 0].rearrange("p h d -> p (h d)"), start=True, stop=True)
                ins.then_inc(att_pe, 1)
                if it == ITERATIONS - 1:
                    pe.wait_ge(diff_ready, 1)
                    pe.matmul(diff_ps, ones_f[:, :], dsum[:, 0:1], start=True, stop=True).then_inc(diff_summed, 1)
                after_dve()
                for c in range(KC):
                    ins = pe.transpose(att_ps[1][:, c * P:(c + 1) * P], at_a[:, c * P:(c + 1) * P], ident[:, :])
                ins.then_inc(att_pe, 1)
                after_dve()
                for g in range(4):
                    for c in range(KC):
                        ins = pe.matmul(att_ps[2][32 * g:32 * g + 32, c * D:(c + 1) * D],
                                        at_T[:, c, 32 * g:32 * g + 32],
                                        keys[:, c, :, 32 * g:32 * g + 32], start=True, stop=True)
                ins.then_inc(att_pe, 1)
                after_dve()
                for j in range(4):
                    ins = pe.transpose(att_ps[3][:, j * P:(j + 1) * P], prob[:, j * P:(j + 1) * P], ident[:, :])
                ins.then_inc(att_pe, 1)
                after_dve()
                for g in range(4):
                    for j in range(4):
                        ins = pe.matmul(att_ps[0][32 * g:32 * g + 32, 64 * j:64 * j + 64],
                                        probT[:, j, 32 * g:32 * g + 32], vals[:, g, 64 * j:64 * j + 64],
                                        start=True, stop=True)
                ins.then_inc(att_pe, 1)
                if it < ITERATIONS - 1:
                    after_dve()
                    for c in range(KC):
                        ins = pe.transpose(att_ps[1][:, c * P:(c + 1) * P],
                                           att_out[:, it, c * P:(c + 1) * P], ident[:, :])
                    ins.then_inc(att_pe, 1)
            after_dve()
            for c in range(KC):
                ins = pe.transpose(att_ps[1][:, c * P:(c + 1) * P], att_out[:, ITERATIONS - 1, c * P:(c + 1) * P],
                                   ident[:, :])
            ins.then_inc(att_pe, 1)
            after_dve()
            for k in range(KC):
                ins = pe.matmul(att_ps[0][:, 0:D], at_T[:, k, :], w4[:, 3, k, :], start=(k == 0), stop=(k == KC - 1))
            ins.then_inc(att_pe, 1)
            assert step[0] == ATT_STEPS
            def pairs_before(a, b):
                for k in range(TOPK):
                    ins = pe.matmul(bank[4 + a // 16][:, (a % 16) * E:((b - 1) % 16 + 1) * E], lower[:, :],
                                    hot_b[:, k, a:b, :].rearrange("p t e -> p (t e)"),
                                    start=(k == 0), stop=(k == TOPK - 1), skip_group_check=True)
                return ins

            def pairs_of(a, b):
                at = (a + 1) % TT
                for h in range(2):
                    o = bank[6 + h].rearrange("p (e t) -> p e t", t=TT)[:, :, at:at + b - a]
                    for k in range(TOPK):
                        ins = pe.matmul(o, ones_b[:, :], hot_b[:, k, a:b, 16 * h:16 * h + 16].rearrange("p t e -> p e t"),
                                        start=(k == 0), stop=(k == TOPK - 1), skip_group_check=True)
                return ins

            pe.wait_ge(hot_ready, 1)
            pairs_of(1, TT - 1)
            pairs_of(TT - 1, TT).then_inc(counts_done, 1)
            turn(TT - 1)
            logits(TT - 1, 0)
            pairs_before(1, 16)
            pairs_before(16, TT)
            pe.wait_ge(hot_ready, 2)
            pairs_of(0, 1).then_inc(counts_done, 1)
            pairs_before(0, 1).then_inc(counts_done, 1)
            turns = TT * TOPK // (HOTBUFS * HOTS)

            def codes(i, first=False, last=False):
                for b in range(HOTBUFS):
                    pe.wait_ge(pairs_hot, i * HOTBUFS + b + 1)
                    pe.wait_ge(pairs_coded, i * HOTBUFS + b + 1)
                    for h in range(HOTS):
                        ins = pe.matmul(bank[0][:, 0:SLOT_TILES], hotr[b][:, :, h], hotj[b][:, :, h],
                                        start=(first and b == h == 0),
                                        stop=(last and b == HOTBUFS - 1 and h == HOTS - 1))
                    ins.then_inc(pairs_used, 1)

            codes(0, first=True)
            with pe.Fori(1, turns - 1) as i:
                codes(i)
            codes(turns - 1, last=True)
            pe.wait_ge(ecol_ready, 1)
            for c in range(2):
                ins = pe.matmul(bank[1][0:1, c * P:(c + 1) * P], ecol[:, c:c + 1], ident[:, :], start=True, stop=True)
            ins.then_inc(eid_turned, 1)

            pe.wait_ge(tables_ready, 2)
            pe.wait_ge(expert_w_in, 160)

            def turn_x(body, step):
                s = step % STEPS
                if s in SHARED_AT:
                    src = xs[:, 0, :]
                    wait_count(pe, shared_in, body, 16, 16 * (step // STEPS + 1))
                else:
                    u = EXPERTS_AT.index(s) + step // STEPS * NEXP
                    src = xg[:, u % RING, :]
                    wait_count(pe, gathered[u % RING], body, 16 * NEXP // RING, 16 * (u // RING + 1))
                wait_count(pe, xT_ready, body, STEPS, step - 1)
                for c in range(KC):
                    ins = pe.transpose(turn_ps[step % 2][:, c, :], src[:, c * P:(c + 1) * P], ident[:, :])
                ins.then_inc(x_turned, 1)

            def gate_up_of(body, step, eid):
                wait_count(pe, xT_ready, body, STEPS, step + 1)
                wait_count(pe, hid_ready, body, STEPS, step - 1)
                for c in range(KC):
                    if eid is None:
                        w = sgu_w[:, SHARED_AT.index(step), c, :]
                    else:
                        w = gu_w[:, bass.ds(eid, 1), c, :].rearrange("p a i -> p (a i)")
                    ins = pe.matmul(bank[2 + step % 2][:, 0:2 * I], xT[:, step % 2, c, :], w, start=(c == 0),
                                    stop=(c == KC - 1))
                ins.then_inc(gu_done, 1)

            def turn_hid(body, step):
                wait_count(pe, hid_ready, body, STEPS, step + 1)
                wait_count(pe, hidT_ready, body, STEPS, step - 1)
                pe.transpose(bank[4 + step % 2][:, 0:P], hid[:, step % 2], ident[:, :]).then_inc(hid_turned, 1)

            def down_of(body, step, eid):
                wait_count(pe, hidT_ready, body, STEPS, step + 1)
                wait_count(pe, y_ready, body, STEPS, step - 1)
                if eid is None:
                    w = sdn_w[:, SHARED_AT.index(step % STEPS), :]
                else:
                    w = dn_w[:, bass.ds(eid, 1), :].rearrange("p a d -> p (a d)")
                pe.matmul(bank[6 + step % 2][:, 0:D], hidT[:, step % 2], w, start=True, stop=True).then_inc(y_done, 1)

            def body_of(body, first, last, steps=STEPS):
                src = (eids[0:1, body, 0:NEXP] if isinstance(body, int)
                       else eids[0:1, bass.ds(body, 1), 0:NEXP].rearrange("p a n -> p (a n)"))
                _, ids = nc.values_load_multi_w_load_instructions(
                    src, engines=(mybir.EngineType.PE,), min_val=0, max_val=E - 1,
                    skip_runtime_bounds_check_because="clamped to E - 1 where the table is made")
                eid_of = {s: ids[u] for u, s in enumerate(EXPERTS_AT)}
                for step in range(steps):
                    gate_up_of(body, step, eid_of.get(step))
                    if not (last and step + 2 >= steps):
                        turn_x(body, step + 2)
                    if not (first and step < 1):
                        turn_hid(body, step - 1)
                    if not (first and step < 2):
                        down_of(body, step - 2, eid_of.get(step - 2))
                if last:
                    turn_hid(body, steps - 1)
                    down_of(body, steps - 2, eid_of.get(steps - 2))
                    down_of(body, steps - 1, eid_of.get(steps - 1))
                    for written in (x_turned, gu_done, hid_turned, y_done):
                        wait_count(pe, written, body + 1, STEPS, 0)

            def part(body):
                turn_x(body, 0)
                turn_x(body, 1)
                body_of(body, True, True, NEXP)

            turn_x(0, 0)
            turn_x(0, 1)
            body_of(0, True, False)
            with pe.Fori(1, FIXED - 1) as body:
                body_of(body, False, False)
            slots = pe.value_load(used[0:1, 0:1], min_val=0, max_val=SLOT_TILES * P)
            body_of(FIXED - 1, False, True)
            used_parts(pe, slots, part)
            pe.sem_inc(experts_done, 1)

            def late_turn(turn, i):
                if isinstance(turn, int):
                    src = late_x[:, 2 * turn + i, :]
                else:
                    src = xs[:, i % 2, :]
                    wait_count(pe, late_ready, turn, 2, i + 1 - LATE_NAMED, 2)
                wait_count(pe, late_xT, turn, 2, i - 1, 2)
                for c in range(KC):
                    ins = pe.transpose(turn_ps[i % 2][:, c, :], src[:, c * P:(c + 1) * P], ident[:, :])
                ins.then_inc(late_turned, 1)

            def late_gate_up(turn, i):
                wait_count(pe, late_xT, turn, 2, i + 1, 2)
                wait_count(pe, late_gated, turn, 2, i - 1, 2)
                for m in range(2):
                    for c in range(KC):
                        ins = pe.matmul(bank[2 + i % 2][:, m * 2 * I:(m + 1) * 2 * I], xT[:, i % 2, c, :],
                                        sgu_w[:, m, c, :], start=(c == 0), stop=(c == KC - 1))
                ins.then_inc(late_gu, 1)

            def late_turn_hid(turn, i):
                wait_count(pe, late_hid, turn, 2, i + 1, 2)
                wait_count(pe, late_hT, turn, 2, i - 1, 2)
                for m in range(2):
                    ins = pe.transpose(bank[4 + i % 2][:, m * P:(m + 1) * P], late_h[:, i % 2, m * P:(m + 1) * P],
                                       ident[:, :])
                ins.then_inc(late_hturned, 1)

            def late_down_of(turn, i):
                wait_count(pe, late_hT, turn, 2, i + 1, 2)
                wait_count(pe, late_y, turn, 2, i - 1, 2)
                for m in range(2):
                    ins = pe.matmul(bank[6 + i % 2][:, 0:D], late_hidT[:, i % 2, m, :], sdn_w[:, m, :],
                                    start=(m == 0), stop=(m == 1))
                ins.then_inc(late_down, 1)

            pe.wait_ge(late_in, 16)
            pe.wait_ge(experts_done, 3)
            late_loop(pe, [(late_gate_up, 0), (late_turn, 1), (late_turn_hid, -1), (late_down_of, -2)],
                      first=lambda: late_turn(0, 0))

        @block.vector
        def _(dve):
            done = [0]

            def seq(ins):
                done[0] += 1
                ins.then_inc(dve_seq, 1)
                dve.wait_ge(dve_seq, done[0])

            roots = [0]

            def root():
                roots[0] += 1
                dve.wait_ge(rstd_ready, roots[0])

            def ask_root(a, b):
                dve.tensor_scalar(var_e[:, a:b], mv[:, a:b, 1:2].rearrange("p t a -> p (t a)"), EPS, None, ALU.add
                                  ).then_inc(var_ready, 1)

            def shifts(a, b):
                root()
                dve.scalar_tensor_tensor(shift[:, a:b], mv[:, a:b, 0:1].rearrange("p t a -> p (t a)"), -1.0,
                                         rstd[:, a:b], ALU.mult, ALU.mult).then_inc(norm_ready, 1)

            def statistics(g):
                a, b = GROUPS_OF_TILES[g]
                dve.wait_ge(x_in[g], 16)
                if g in POOL_GROUPS:
                    dve.wait_ge(bias_added, POOL_GROUPS.index(g) + 1)
                else:
                    seq(dve.tensor_tensor(x_sb[:, a:b, :], x_sb[:, a:b, :],
                                          row("ob").unsqueeze(1).to_broadcast([P, b - a, D]), ALU.add))
                for t in range(a, b):
                    ins = dve.bn_stats(stats[:, t, :], x_sb[:, t, :])
                seq(ins)
                for t in range(a, b):
                    ins = dve.bn_aggr(mv[:, t, :], stats[:, t, :])
                seq(ins)
                ask_root(a, b)

            def route(a, b):
                n = b - a
                TG = n * GROUPS
                dve.wait_ge(scores_done, 3 if a == 0 else 2)
                dve.wait_ge(consts_made, N_CONSTS)
                sel_ab = sel[:, a * E:b * E]
                sel3 = sel_ab.rearrange("p (t e) -> p t e", e=E)
                seq(dve.tensor_tensor(sel3, sc3[:, a:b, :], row("bias").unsqueeze(1).to_broadcast([P, n, E]), ALU.add))
                yield
                s8 = sel_ab.rearrange("p (n j) -> p n j", j=GSIZE)
                hi = work[:, 0, 0:TG * 4].rearrange("p (n j) -> p n j", j=4)
                lo = work[:, 0, TG * 4:TG * 8].rearrange("p (n j) -> p n j", j=4)
                dve.tensor_tensor(hi, s8[:, :, 0:4], s8[:, :, 4:8], ALU.max)
                seq(dve.tensor_tensor(lo, s8[:, :, 0:4], s8[:, :, 4:8], ALU.min))
                yield
                for level, width in enumerate((2, 1)):
                    h_new, h_min, l_max, l_new = [work[:, 1 + level, k * TG:(k + width) * TG].rearrange(
                        "p (n j) -> p n j", j=width) for k in range(0, 4 * width, width)]
                    top, low = hi[:, :, 0:width], hi[:, :, width:2 * width]
                    dve.tensor_tensor(h_new, top, low, ALU.max)
                    dve.tensor_tensor(h_min, top, low, ALU.min)
                    seq(dve.tensor_tensor(l_max, lo[:, :, 0:width], lo[:, :, width:2 * width], ALU.max))
                    seq(dve.tensor_tensor(l_new, h_min, l_max, ALU.max))
                    hi, lo = h_new, l_new
                    yield

                def groups(k):
                    return small[:, k, 0:TG].rearrange("p (t g) -> p t g", g=GROUPS)

                gs, beats = groups(0), groups(1)
                seq(dve.tensor_tensor(small[:, 0, 0:TG], hi.rearrange("p n a -> p (n a)"),
                                      lo.rearrange("p n a -> p (n a)"), ALU.add))
                dve.tensor_copy(beats, iota_g[:, :].unsqueeze(1).to_broadcast([P, n, GROUPS]))
                wins = []
                for d in range(1, GROUPS):
                    c = groups(1 + d)[:, :, 0:GROUPS - d]
                    ins = dve.tensor_tensor(c, gs[:, :, 0:GROUPS - d], gs[:, :, d:GROUPS], ALU.is_ge)
                    wins.append(c)
                seq(ins)
                yield
                for d, c in enumerate(wins, 1):
                    seq(dve.tensor_tensor(beats[:, :, 0:GROUPS - d], beats[:, :, 0:GROUPS - d], c, ALU.add))
                    seq(dve.tensor_tensor(beats[:, :, d:GROUPS], beats[:, :, d:GROUPS], c, ALU.subtract))
                yield
                seq(dve.tensor_scalar(small[:, 5, 0:TG], small[:, 1, 0:TG], float(GROUPS - TOPG), None, ALU.is_ge))
                seq(dve.tensor_tensor(s8, s8, small[:, 5, 0:TG].unsqueeze(2).to_broadcast([P, TG, GSIZE]), ALU.mult))
                yield
                for t in range(a, b):
                    ins = dve.max(top8[:, t, :], sel3[:, t - a, :])
                    if t % 8 == 7 and t < b - 1:
                        yield
                seq(ins)
                yield
                for t in range(a, b):
                    ins = dve.max_index(idx8[:, t, :], top8[:, t, :], sel3[:, t - a, :])
                    if t % 8 == 7 and t < b - 1:
                        yield
                seq(ins)
                yield
                seq(dve.tensor_copy(idxf[:, a:b, :], idx8[:, a:b, 0:TOPK]))
                for k in range(TOPK):
                    ins = dve.tensor_tensor(hot_b[:, k, a:b], iota_e[:, :].unsqueeze(1).to_broadcast([P, n, E]),
                                            idxf[:, a:b, k:k + 1].to_broadcast([P, n, E]), ALU.is_equal)
                    if k == TOPK - 1:
                        ins.then_inc(hot_ready, 1)
                    yield

            others = route(1, TT)

            def fill(parts):
                for _ in range(parts):
                    next(others, None)

            pes, exps = [0], [0]

            def to_pe(ins):
                ins.then_inc(att_ready, 1)

            def from_pe():
                pes[0] += 1
                dve.wait_ge(att_pe, pes[0])

            def by_scalar():
                pes[0] += 1

            dve.wait_ge(att_x_in, 16)
            x0 = x_sb[:, 0, :]

            def centred(dst, src):
                seq(dve.bn_stats(stats[:, 0, :], src))
                seq(dve.bn_aggr(mv[:, 0, :], stats[:, 0, :]))
                ask_root(0, 1)
                root()
                seq(dve.tensor_scalar(dst, src, mv[:, 0, 0:1], rstd[:, 0:1], ALU.subtract, ALU.mult))

            centred(at_c, x0)
            centred(at_d, at_c)
            dve.wait_ge(small_in, 32)
            dve.wait_ge(consts_made, N_MASKS)
            dve.wait_ge(attw_in, 48)
            centre = hst[:, 5, 0:4]
            biases = row_sb[:, ROW_AT["lqb"][0]:ROW_AT["lqb"][0] + 2 * HD].rearrange("p (m d) -> p m d", m=2)
            for k, what in enumerate((local_sb[:, 0:2, :], biases)):
                mean = centre[:, 2 * k:2 * k + 2]
                seq(dve.tensor_reduce(mean, what, AX.X, ALU.add))
                seq(dve.tensor_scalar(mean, mean, 1.0 / HD, None, ALU.mult))
                seq(dve.tensor_tensor(what, what, mean.unsqueeze(2).to_broadcast([P, 2, HD]), ALU.subtract))
            for m in range(3):
                dve.tensor_tensor(blockw[:, m], local_sb[:, m, :].unsqueeze(1).to_broadcast([P, HEADS // 2, HD]),
                                  head_mask[:, :].unsqueeze(2).to_broadcast([P, HEADS // 2, HD]), ALU.mult)
            for g in range(4):
                dve.tensor_copy(spread[:, g], ident[:, 32 * g:32 * g + 32].unsqueeze(1).to_broadcast([P, 4, 32]))
            dve.tensor_tensor(at_a, at_d, row("lna"), ALU.mult)
            to_pe(dve.tensor_tensor(at_b, at_d, row("lnb"), ALU.mult))
            statistics(0)
            from_pe()
            to_pe(dve.tensor_copy(inT[:, :, :, :].rearrange("p m c t -> p (m c t)"), att_ps[0][:, :]))
            shifts(*GROUPS_OF_TILES[0])
            statistics(1)
            from_pe()
            for c in range(KC):
                dve.tensor_scalar(q_cur[:, c, :], att_ps[1][:, c * P:(c + 1) * P], col_sb[:, c:c + 1], None, ALU.add)
                dve.tensor_copy(at_T[:, c, :], att_ps[2][:, c * P:(c + 1) * P])
                ins = dve.tensor_scalar(at_d[:, c * P:(c + 1) * P], att_ps[3][:, c * P:(c + 1) * P],
                                        col_sb[:, 2 + c:3 + c], None, ALU.add)
            to_pe(ins)
            shifts(*GROUPS_OF_TILES[1])
            from_pe()

            def heads(ap):
                return ap.rearrange("p (h d) -> p h d", d=HD)

            def per_head(ap):
                return ap.unsqueeze(2).to_broadcast([P, HEADS, HD])

            def per_dim(ap):
                return ap.unsqueeze(1).to_broadcast([P, HEADS, HD])

            def ask_head_roots():
                seq(dve.tensor_tensor(at_d, at_c, at_c, ALU.mult))
                seq(dve.tensor_reduce(hst[:, 0, :], heads(at_d), AX.X, ALU.add))
                dve.tensor_scalar(hst[:, 2, :], hst[:, 0, :], 1.0 / HD, EPS, ALU.mult, ALU.add).then_inc(var_ready, 1)

            def head_norm(dst, ps, bias, weight, fill_wait):
                seq(dve.tensor_tensor(heads(at_c), heads(ps), per_dim(row(bias)), ALU.add))
                ask_head_roots()
                fill_wait()
                root()
                seq(dve.tensor_tensor(heads(at_c), heads(at_c), per_head(hst[:, 3, :]), ALU.mult))
                return dve.tensor_tensor(heads(dst), heads(at_c), per_dim(row(weight)), ALU.mult)

            seq(dve.tensor_tensor(heads(at_b), heads(att_ps[1][:, 0:D]), per_dim(row("lvb")), ALU.add))
            to_pe(head_norm(at_a, att_ps[0][:, 0:D], "lkb", "lnd", lambda: statistics(2)))
            shifts(*GROUPS_OF_TILES[2])
            statistics(3)
            shifts(*GROUPS_OF_TILES[3])
            from_pe()
            for c in range(KC):
                dve.tensor_tensor(keys[:, c], att_ps[2][:, c * P:(c + 1) * P].unsqueeze(1).to_broadcast([P, HEADS // 2, P]),
                                  head_mask[:, :].unsqueeze(2).to_broadcast([P, HEADS // 2, P]), ALU.mult)
            for g in range(4):
                ps = att_ps[(0, 3)[g // 2]][:, (g % 2) * D:(g % 2 + 1) * D]
                ins = dve.tensor_tensor(vals[:, g].rearrange("p (j q d) -> p j q d", j=4, q=4),
                                        ps.rearrange("p (j q d) -> p j q d", j=4, q=4),
                                        quad_mask[:, :].unsqueeze(1).unsqueeze(3).to_broadcast([P, 4, 4, HD]), ALU.mult)
            to_pe(ins)
            prob3 = prob.rearrange("p (h k) -> p h k", k=32)

            def per_row(ap):
                return ap.unsqueeze(2).to_broadcast([P, HEADS, 32])

            def difference():
                seq(dve.tensor_tensor(at_b, att_out[:, 1, :], att_out[:, 0, :], ALU.subtract))
                dve.tensor_reduce(dsum[:, 0:1], at_b, AX.X, ALU.add, apply_absolute_value=True
                                  ).then_inc(diff_ready, 1)

            def decide():
                dve.wait_ge(diff_summed, 1)
                seq(dve.tensor_scalar(dsum[:, 1:2], diff_ps, 1.0 / (TOKENS * D), None, ALU.mult))
                seq(dve.tensor_scalar(dsum[:, 2:3], dsum[:, 1:2], DIFF_FACTOR, DIFF_LIMIT, ALU.mult, ALU.add))
                seq(dve.tensor_tensor(dsum[:, 3:4], dsum[:, 1:2], dsum[:, 2:3], ALU.is_lt))
                seq(dve.tensor_copy(stop_i[:, :], dsum[:, 3:4]))

            for it in range(ITERATIONS):
                from_pe()
                seq(dve.tensor_tensor(heads(at_c), heads(att_ps[0][:, 0:D]), per_dim(row("lqb")), ALU.add))
                to_pe(dve.tensor_tensor(heads(at_a), heads(at_c), per_dim(row("lnc")), ALU.mult))
                by_scalar()
                ask_head_roots()
                if it == ITERATIONS - 1:
                    decide()
                fill(2)
                root()
                from_pe()
                seq(dve.tensor_tensor(prob3, att_ps[2][:, :].rearrange("p (h k) -> p h k", k=32),
                                      per_row(hst[:, 3, :]), ALU.mult))
                seq(dve.tensor_tensor(prob3, prob3,
                                      batch_mask[:, :, :].rearrange("p a k -> p (a k)").unsqueeze(1).to_broadcast([P, HEADS, 32]),
                                      ALU.add))
                seq(dve.tensor_reduce(hst[:, 0, :], prob3, AX.X, ALU.max))
                exps[0] += 2
                dve.tensor_tensor(prob3, prob3, per_row(hst[:, 0, :]), ALU.subtract).then_inc(att_exp, 1)
                dve.wait_ge(att_exp, exps[0])
                to_pe(dve.tensor_reduce(hst[:, 1, :], prob3, AX.X, ALU.add))
                by_scalar()
                fill(3)
                from_pe()
                seq(dve.reciprocal(hst[:, 4, :], hst[:, 1, :]))
                o = att_out[:, it, :]
                ins = dve.tensor_tensor(heads(o), heads(att_ps[0][:, 0:D]), per_head(hst[:, 4, :]), ALU.mult)
                if it < ITERATIONS - 1:
                    to_pe(ins)
                    fill(1)
                    from_pe()
                    to_pe(dve.tensor_tensor(q_cur[:, :, :].rearrange("p c t -> p (c t)"),
                                            q_cur[:, :, :].rearrange("p c t -> p (c t)"), att_ps[1][:, 0:D], ALU.add))
                    if it == 1:
                        difference()
                    else:
                        fill(1)
                else:
                    seq(ins)
            to_pe(dve.copy_predicated(att_out[:, 2, :], stop_i[:, 0:1].to_broadcast([P, D]), att_out[:, 1, :]))
            fill(1)
            from_pe()
            to_pe(dve.tensor_copy(at_T[:, :, :].rearrange("p c t -> p (c t)"), att_ps[1][:, 0:D]))
            for _ in others:
                pass
            seq(dve.tensor_tensor(at_a, x0, row("ob"), ALU.add))
            from_pe()
            seq(dve.tensor_tensor(x0, att_ps[0][:, 0:D], at_a, ALU.add))
            seq(dve.bn_stats(stats[:, 0, :], x0))
            seq(dve.bn_aggr(mv[:, 0, :], stats[:, 0, :]))
            ask_root(0, 1)
            shifts(0, 1)

            rest, number, tiles, ends = (e_row[:, k, :] for k in range(4))
            counts = two_banks[3][:, :, :].rearrange("p h (e t) -> p (h e) t", t=TT)
            dve.memset(e_row[:, :, :], 0.0)
            resets_et = resets.rearrange("p (e t) -> p e t", t=TT)
            seq(dve.memset(resets, 1.0))
            dve.memset(resets_et[:, :, 0:1], 0.0)
            dve.wait_ge(counts_done, 1)
            seq(dve.tensor_reduce(rest, counts[:, :, 2:TT], AX.X, ALU.add))
            seq(dve.tensor_tensor(rest, rest, counts[:, :, 0:1].rearrange("p e a -> p (e a)"), ALU.add))

            for _ in route(0, 1):
                pass
            cnt, pos = work[:, 0, :], sel
            before = work[:, 1:2, :].rearrange("p a n -> p (a n)")
            before_et = before.rearrange("p (e t) -> p e t", t=TT)
            dve.wait_ge(counts_done, 2)
            number = number.bitcast(I32)
            seq(dve.scalar_tensor_tensor(number, counts[:, :, 1:2].rearrange("p e a -> p (e a)"), float(P - 1), rest,
                                         ALU.add, ALU.add))
            seq(dve.tensor_scalar(number, number, 2 * PAIRS - P, None, ALU.bitwise_and))
            seq(dve.tensor_copy(tiles, number))
            seq(dve.tensor_tensor_scan(ends, e_row[:, 6, :], tiles, 0.0, ALU.add, ALU.add))
            seq(dve.tensor_tensor(counts[:, :, 0:1].rearrange("p e a -> p (e a)"), ends, tiles, ALU.subtract))
            seq(dve.tensor_tensor_scan(before, resets, two_banks[3][:, :, :].rearrange("p h n -> p (h n)"), 0.0,
                                       ALU.mult, ALU.add))
            pos3 = pos.rearrange("p (t e) -> p t e", e=E)
            dve.wait_ge(counts_done, 3)
            by_tile = two_banks[2][:, :, :].rearrange("p h (t e) -> p e (h t)", e=E)
            seq(dve.tensor_tensor(pos3.rearrange("p t e -> p e t"), by_tile, before_et, ALU.add))
            dve.sem_inc(places_ready, 1)
            for k in range(TOPK):
                mine = cnt.rearrange("p (t e) -> p t e", e=E)
                if k < TOPK // 2:
                    seq(dve.tensor_tensor(mine, hot_b[:, k], pos3, ALU.mult))
                else:
                    mine = work[:, k - 1, :].rearrange("p (t e) -> p t e", e=E)
                    dve.wait_ge(places_hot, k - TOPK // 2 + 1)
                seq(dve.tensor_reduce(slot_f[:, :, k:k + 1], mine, AX.X, ALU.add))
            seq(dve.tensor_copy(slot_i[:, 0, :], slot_f[:, :, :].rearrange("p t k -> p (t k)")))
            seq(dve.tensor_scalar(slot_i[:, 1, :], slot_i[:, 0, :], P - 1, None, ALU.bitwise_and))
            seq(dve.tensor_scalar(slot_i[:, 2, :], slot_i[:, 0, :], 7, None, ALU.arith_shift_right))
            seq(dve.tensor_copy(slot_b[:, :, :], slot_i[:, 1:3, :]))
            codes_b = code_u[:, :].bitcast(BF16)

            def hot_pairs(i, first=False):
                for b in range(HOTBUFS):
                    if not first:
                        dve.wait_ge(pairs_used, i * HOTBUFS + b - (HOTBUFS - 1))

                    def by(columns, h, n):
                        at = b * HOTS + h
                        columns = (columns[:, at:(b + 1) * HOTS] if first
                                   else columns[:, bass.ds(i * (HOTBUFS * HOTS) + at, HOTS - h)])
                        return columns.unsqueeze(1).to_broadcast([P, n, HOTS - h])

                    dve.tensor_tensor(hotr[b], iota_b[:, 0:P, :], by(slot_b[:, 0], 0, P), ALU.is_equal
                                      ).then_inc(rows_hot, 1)
                    dve.tensor_tensor(hotj[b], iota_b[:, :, :], by(slot_b[:, 1], 0, SLOT_TILES), ALU.is_equal)
                    dve.wait_ge(rows_hot, i * HOTBUFS + b + 1)
                    dve.tensor_tensor(hotr[b][:, :, CODED:HOTS], hotr[b][:, :, CODED:HOTS], by(codes_b, CODED, P),
                                      ALU.mult).then_inc(pairs_hot, 1)

            hot_pairs(0, first=True)
            with dve.Fori(1, TT * TOPK // (HOTBUFS * HOTS)) as i:
                hot_pairs(i)
            dve.tensor_copy(used[0:1, 0:1], ends[0:1, E - 1:E])
            for c in range(2):
                ins = dve.tensor_tensor(e_row[:, 6 + c, :], ends, iota_p[:, c:c + 1].to_broadcast([P, E]),
                                        ALU.is_le)
            seq(ins)
            seq(dve.tensor_reduce(ecol[:, 2:4], e_row[:, 6:8, :], AX.X, ALU.add))
            seq(dve.tensor_scalar(ecol[:, 0:2], ecol[:, 2:4], float(E - 1), None, ALU.min))
            dve.sem_inc(ecol_ready, 1)
            dve.wait_ge(pairs_used, TT * TOPK // HOTS)
            code_i = work[:, 0, 0:SLOT_TILES].bitcast(I32)
            pair_0 = work[:, 1, 0:SLOT_TILES].bitcast(I32)
            seq(dve.tensor_scalar(code_i, bank[0][:, 0:SLOT_TILES].bitcast(I32), 16, None, ALU.arith_shift_right))
            seq(dve.tensor_scalar(pair_at[:, :], code_i, float(-CODE), None, ALU.add))
            seq(dve.tensor_scalar(pair_0, pair_at[:, :], 0.0, None, ALU.max))
            dve.wait_ge(eid_turned, 1)
            dve.tensor_copy(eids[0:1, :, 0:NEXP], bank[1][0:1, 0:SLOT_TILES].rearrange("p (b n) -> p b n", n=NEXP)
                            ).then_inc(tables_ready, 1)
            dve.tensor_scalar(tok_at[:, :], pair_0, 2, None, ALU.arith_shift_right).then_inc(tables_ready, 1)
            sum4 = small[:, 6, 0:TT]
            hot_score = cnt.rearrange("p (t e) -> p t e", e=E)

            def weights(part):
                k, reduce = divmod(part, 2)
                if k < TOPK and not reduce:
                    seq(dve.tensor_tensor(hot_score, hot_b[:, k], sc3, ALU.mult))
                elif k < TOPK:
                    seq(dve.tensor_reduce(wts[:, :, k:k + 1], hot_score, AX.X, ALU.add))
                elif not reduce:
                    seq(dve.tensor_reduce(sum4, wts[:, :, :], AX.X, ALU.add))
                    seq(dve.tensor_scalar(sum4, sum4, 1e-20, None, ALU.add))
                else:
                    seq(dve.reciprocal(sum4, sum4))
                    seq(dve.tensor_scalar(sum4, sum4, ROUTE_SCALE, None, ALU.mult))
                    seq(dve.tensor_tensor(wts[:, :, :], wts[:, :, :],
                                          sum4.unsqueeze(2).to_broadcast([P, TT, TOPK]), ALU.mult))
                    dve.sem_inc(weights_made, 1)

            def hidden(body, step):
                wait_count(dve, silu_done, body, STEPS, step + 1)
                wait_count(dve, hid_turned, body, STEPS, step - 1)
                dve.tensor_tensor(hid[:, step % 2], silu[:, step % 2], bank[2 + step % 2][:, I:2 * I], ALU.mult
                                  ).then_inc(hid_ready, 1)

            def keep_hid(body, step):
                wait_count(dve, hid_turned, body, STEPS, step + 1)
                wait_count(dve, y_done, body, STEPS, step - 1)
                dve.tensor_copy(hidT[:, step % 2], bank[4 + step % 2][:, 0:P]).then_inc(hidT_ready, 1)

            def keep_y(body, step):
                s = step % STEPS
                wait_count(dve, y_done, body, STEPS, step + 1)
                ps = bank[6 + step % 2][:, 0:D]
                if s in SHARED_AT:
                    if isinstance(body, int):
                        xt = x_sb[:, body + step // STEPS, :]
                    else:
                        xt = x_sb[:, bass.ds(body + step // STEPS, 1), :].rearrange("p a d -> p (a d)")
                    if s == SHARED_AT[1]:
                        wait_count(dve, y_ready, body, STEPS, step)
                    dve.tensor_tensor(xt, ps, xt, ALU.add).then_inc(y_ready, 1)
                else:
                    u = EXPERTS_AT.index(s)
                    wait_count(dve, scattered[u], body, 16, 16 * (step // STEPS))
                    dve.tensor_copy(yb[u], ps).then_inc(y_ready, 1)

            def drain(body, steps):
                keep_hid(body, steps - 1)
                keep_y(body, steps - 2)
                keep_y(body, steps - 1)
                for written in (hid_ready, hidT_ready, y_ready):
                    wait_count(dve, written, body + 1, STEPS, 0)

            def part(body):
                for step in range(NEXP):
                    hidden(body, step)
                    if step >= 1:
                        keep_hid(body, step - 1)
                    if step >= 2:
                        keep_y(body, step - 2)
                drain(body, NEXP)

            def body_of(body, first):
                for step in range(STEPS):
                    hidden(body, step)
                    if not (first and step < 1):
                        keep_hid(body, step - 1)
                    if not (first and step < 2):
                        keep_y(body, step - 2)
                    if first and 1 <= step <= WEIGHT_PARTS:
                        weights(step - 1)

            body_of(0, True)
            with dve.Fori(1, FIXED - 1) as body:
                body_of(body, False)
            slots = dve.value_load(used[0:1, 0:1], min_val=0, max_val=SLOT_TILES * P)
            body_of(FIXED - 1, False)
            drain(FIXED - 1, STEPS)
            used_parts(dve, slots, part)
            dve.sem_inc(experts_done, 1)

            for t in range(0, TT - SUMS_FIRST, 2):
                for k in range(TOPK):
                    for tile in (t, t + 1):
                        if k == 0:
                            dve.wait_ge(pairs_in[tile % LOADS], 16 * (tile // LOADS + 1))
                            if tile >= TT - LATE:
                                dve.wait_ge(late_added, tile - (TT - LATE) + 1)
                        else:
                            dve.wait_ge(added, t * (TOPK - 1) + (k - 1) * 2 + tile - t + 1)
                        ins = dve.scalar_tensor_tensor(x_sb[:, tile, :], load4[:, tile % LOADS, k, :],
                                                       wts[:, tile, k:k + 1], x_sb[:, tile, :], ALU.mult, ALU.add)
                        ins.then_inc(added if k < TOPK - 1 else tile_summed, 1)
            sums = (TT - SUMS_FIRST) * (TOPK - 1)

            def add_sums(t):
                for tile in (t, t + 1):
                    dve.wait_ge(added, sums_at[tile])
                    dve.wait_ge(late_added, tile - (TT - LATE) + 1)
                    dve.tensor_tensor(x_sb[:, tile, :], x_sb[:, tile, :], load4[:, tile % LOADS, 0, :], ALU.add
                                      ).then_inc(tile_summed, 1)

            sums_at = {}
            for t in range(TT - SUMS_FIRST, TT, 2):
                for k in range(TOPK):
                    for tile in (t, t + 1):
                        total, y = load4[:, tile % LOADS, 0, :], load4[:, tile % LOADS, k, :]
                        weight = wts[:, tile, k:k + 1]
                        if k == 0:
                            dve.wait_ge(pairs_in[tile % LOADS], 16 * (tile // LOADS + 1))
                            ins = dve.tensor_scalar(total, y, weight, None, ALU.mult)
                        else:
                            dve.wait_ge(added, sums - 1)
                            ins = dve.scalar_tensor_tensor(total, y, weight, total, ALU.mult, ALU.add)
                        ins.then_inc(added, 1)
                        sums += 1
                        sums_at[tile] = sums
                if t > TT - SUMS_FIRST:
                    add_sums(t - 2)
            add_sums(TT - 2)


def kernel(**inputs):
    import concourse.bacc as bacc
    from concourse.bass_utils import run_bass_kernel_spmd

    a = {n.replace("L0_attn_", "").replace("L0_ffn_", ""): np.asarray(v) for n, v in inputs.items()}

    def chunked(w):
        w = w.reshape(*w.shape[:-2], -1, P, w.shape[-1])
        return np.ascontiguousarray(np.moveaxis(w, -2, 0))

    gate_up = np.concatenate([a["gate_w"], a["up_w"]], axis=1).transpose(0, 2, 1)
    shared = np.concatenate([a["shared_gate_w"].reshape(2, I, D), a["shared_up_w"].reshape(2, I, D)],
                            axis=1).transpose(0, 2, 1)
    wide = {"lna": "lna_w", "lnb": "lnb_w", "lnc": "lnc_w", "lnd": "lnd_w", "bias": "router_bias"}
    arrays = {
        "in_x": np.ascontiguousarray(a["x"]),
        "in_qkvo": chunked(np.stack([a[n].T for n in ("qw", "kw", "vw", "ow")])),
        "in_gate_up": chunked(gate_up),
        "in_down": np.ascontiguousarray(a["down_w"].transpose(2, 0, 1)),
        "in_sh_gate_up": chunked(shared),
        "in_sh_down": chunked(a["shared_down_w"].T),
        "in_router": chunked(a["router_weight"].T),
        "in_rows": np.concatenate([a[wide.get(n, n)] for n, _ in ROW_PARTS])[None],
        "in_cols": np.ascontiguousarray(np.concatenate([a["qb"].reshape(KC, P), a["vb"].reshape(KC, P)]).T),
        "in_local": np.ascontiguousarray(
            np.stack([np.tile(a[n].T, (P // HD, 1)) for n in ("lqw", "lkw", "lvw")], axis=1)),
    }
    nc = bacc.Bacc("TRN2", target_bir_lowering=False, num_devices=1)
    args = [nc.dram_tensor(n, v.shape, mybir.dt.from_np(v.dtype), kind="ExternalInput").ap()
            for n, v in arrays.items()]
    out = nc.dram_tensor("out", (BATCH, CTX, D), F32, kind="ExternalOutput").ap()
    tokens_dram = nc.dram_tensor("tokens_dram", (TOKENS, D), F32).ap()
    pairs_dram = nc.dram_tensor("pairs_dram", (PAIRS, D), F32).ap()
    build_program(nc, *args, out, tokens_dram, pairs_dram)
    r = run_bass_kernel_spmd(nc, [arrays], core_ids=[0])
    return r.results[0]["out"]
```
